# Optimizing a Trainium2 kernel written in Bass

```python
import numpy as np
import jax
import jax.numpy as jnp

def _softmax(x, axis=-1):
    return jax.nn.softmax(x, axis=axis)

def _gelu(x):
    return jax.nn.gelu(x, approximate=True)

def _silu(x):
    return jax.nn.silu(x)

def _sigmoid(x):
    return jax.nn.sigmoid(x)

def _layernorm(x, axis=-1, eps=1e-05):
    m = jnp.mean(x, axis=axis, keepdims=True)
    v = jnp.var(x, axis=axis, keepdims=True)
    return (x - m) / jnp.sqrt(v + eps)

def _scatter_add(tgt, idx, src, axis=0):
    return tgt.at[idx].add(src)

def _segment_sum(src, seg, n):
    return jax.ops.segment_sum(src, seg, n)
kernel_name = 'mk_decoder_postln_d2_seqx_r4_f56b98'

def setup_inputs(seed: int=0):
    np.random.seed(seed)
    _w = jnp.asarray

    def _rec_inputs():
        import jax
        import jax.numpy as jnp
        _rk = jax.random.key(seed)
        x = 7.22e-05 + 1 * jax.random.normal(jax.random.fold_in(_rk, 1), (16, 128, 512), jnp.float32)
        _lenS = 128 - jax.random.randint(jax.random.fold_in(_rk, 7), (16,), 0, max(1, 128 // 4) + 1, jnp.int32)
        _lenS2 = 128 - jax.random.randint(jax.random.fold_in(_rk, 8), (16,), 0, max(1, 128 // 4) + 1, jnp.int32)
        _ctx_1024P = jax.random.normal(jax.random.fold_in(_rk, 11), (16, 16, 256), jnp.float32)
        _ctx_1024c = jax.random.dirichlet(jax.random.fold_in(_rk, 511), 0.3 * jnp.ones((16,), jnp.float32), (16, 128))
        _ctx_1024t = jnp.einsum('bsk,bkd->bsd', _ctx_1024c, _ctx_1024P)
        _ctx_1024t = _ctx_1024t * jax.lax.rsqrt(jnp.mean(jnp.square(_ctx_1024t)) + 1e-12) * 0.953939
        ctx_1024 = -1.39393e-06 + 0.999914 * (_ctx_1024t + 0.3 * jax.random.normal(jax.random.fold_in(_rk, 611), (16, 128, 256), jnp.float32))
        fside_BxSx2_0 = jax.random.uniform(jax.random.fold_in(_rk, 12), (16, 128, 2), jnp.float32, 0.0, 0.999707)
        return (x, ctx_1024, fside_BxSx2_0)
    x, ctx_1024, fside_BxSx2_0 = _rec_inputs()

    def _L0_attn_setup():
        import jax, jax.numpy as jnp
        import numpy as np
        B, T, C = (2, 512, 512)
        NH, NKV, HD = (16, 8, 64)
        SOFTCAP = 50.0
        ROPE_BASE = 10000.0

        def _rotate_half(x):
            x1, x2 = (x[..., :x.shape[-1] // 2], x[..., x.shape[-1] // 2:])
            return jnp.concatenate((-x2, x1), axis=-1)

        def _rope_cos_sin(t, head_dim, dtype):
            inv_freq = 1.0 / ROPE_BASE ** (jnp.arange(0, head_dim, 2, dtype=jnp.int32).astype(jnp.float32) / head_dim)
            pos = jnp.arange(t, dtype=jnp.float32)
            freqs = pos[:, None] * inv_freq[None, :]
            emb = jnp.concatenate((freqs, freqs), axis=-1)
            return (jnp.cos(emb).astype(dtype)[None, None], jnp.sin(emb).astype(dtype)[None, None])
        key = jax.random.key(seed)
        ks = jax.random.split(key, 5)
        s = 0.02
        return {'X': jax.random.normal(ks[0], (B, T, C), dtype=jnp.float32), 'Wq': jax.random.normal(ks[1], (C, NH * HD), dtype=jnp.float32) * s, 'Wk': jax.random.normal(ks[2], (C, NKV * HD), dtype=jnp.float32) * s, 'Wv': jax.random.normal(ks[3], (C, NKV * HD), dtype=jnp.float32) * s, 'Wo': jax.random.normal(ks[4], (NH * HD, C), dtype=jnp.float32) * s}
    _L0_attn_all = _L0_attn_setup()
    _L0_attn_in = {k: v for k, v in _L0_attn_all.items() if k in ('Wq', 'Wk', 'Wv', 'Wo')}
    del _L0_attn_all

    def _L0_xattn_setup():
        import jax, jax.numpy as jnp
        import numpy as np
        DIM = 512
        CTX_DIM = 256
        N_HEADS = 32
        HEAD_DIM = DIM // N_HEADS
        POS_DIM = 2
        B, N, CTXN = (2, 512, 512)
        ROPE_BASE = 10000.0

        def apply_axial_rope(x, pos):
            b, n, h, d = x.shape
            p = pos.shape[-1]
            dpa = d // p
            half = dpa // 2
            freqs = ROPE_BASE ** (-jnp.arange(half, dtype=x.dtype) / half)
            ang = pos[..., :, None] * freqs
            cos = jnp.cos(ang)[:, :, None, :, :]
            sin = jnp.sin(ang)[:, :, None, :, :]
            xr = x.reshape(b, n, h, p, half, 2)
            x1, x2 = (xr[..., 0], xr[..., 1])
            out = jnp.stack([x1 * cos - x2 * sin, x1 * sin + x2 * cos], axis=-1)
            return out.reshape(b, n, h, d)
        key = jax.random.key(seed)
        ks = jax.random.split(key, 8)
        x = jax.random.normal(ks[0], (B, N, DIM), jnp.float32)
        ctx = jax.random.normal(ks[1], (B, CTXN, CTX_DIM), jnp.float32)
        pos_map = jax.random.uniform(ks[2], (B, N, POS_DIM), jnp.float32)
        ctx_pos_map = jax.random.uniform(ks[3], (B, CTXN, POS_DIM), jnp.float32)
        Wq = jax.random.normal(ks[4], (DIM, DIM), jnp.float32) / np.sqrt(DIM)
        Wkv = jax.random.normal(ks[5], (CTX_DIM, 2 * DIM), jnp.float32) / np.sqrt(CTX_DIM)
        Wout = jax.random.normal(ks[6], (DIM, DIM), jnp.float32) / np.sqrt(DIM)
        bout = jnp.zeros((DIM,), jnp.float32)
        return {'x': x, 'ctx': ctx, 'pos_map': pos_map, 'ctx_pos_map': ctx_pos_map, 'Wq': Wq, 'Wkv': Wkv, 'Wout': Wout, 'bout': bout}
    _L0_xattn_all = _L0_xattn_setup()
    _L0_xattn_in = {k: v for k, v in _L0_xattn_all.items() if k in ('Wq', 'Wkv', 'Wout', 'bout')}
    del _L0_xattn_all

    def _L0_ffn_setup():
        import jax, jax.numpy as jnp
        import numpy as np
        TOP_K = 2
        key = jax.random.key(seed)
        k1, k2, k3, k4, k5 = jax.random.split(key, 5)
        B, S, H, O, E = (2, 256, 512, 512, 8)
        hidden_states = jax.random.normal(k1, (B, S, H), dtype=jnp.float32)
        router_w = jax.random.normal(k2, (O * E, H), dtype=jnp.float32) * 0.02
        router_b = jnp.zeros((O * E,), dtype=jnp.float32)
        expert_w = jax.random.normal(k3, (E, O, H), dtype=jnp.float32) * 0.02
        expert_b = jnp.zeros((E, O), dtype=jnp.float32)
        return {'hidden_states': hidden_states, 'router_w': router_w, 'router_b': router_b, 'expert_w': expert_w, 'expert_b': expert_b}
    _L0_ffn_all = _L0_ffn_setup()
    _L0_ffn_in = {k: v for k, v in _L0_ffn_all.items() if k in ('router_w', 'router_b', 'expert_w', 'expert_b')}
    del _L0_ffn_all

    def _L1_attn_setup():
        import jax, jax.numpy as jnp
        import numpy as np
        D, E, N, D_DELTA, D_CONV = (512, 1024, 16, 128, 4)
        B_SZ, L = (1, 512)
        EPS = 1e-05

        def _silu(x):
            return x * jax.nn.sigmoid(x)
        key = jax.random.key(seed)
        ks = jax.random.split(key, 16)
        s = lambda k, shape, scale: jax.random.normal(k, shape, dtype=jnp.float32) * scale
        return {'resid': s(ks[0], (B_SZ, L, D), 1.0), 'norm_w': jnp.ones((D,), jnp.float32), 'W_skip': s(ks[1], (D, E), D ** (-0.5)), 'W_in': s(ks[2], (D, E), D ** (-0.5)), 'conv_w': s(ks[3], (D_CONV, 1, E), D_CONV ** (-0.5)), 'conv_b': s(ks[4], (E,), 0.02), 'W_delta_1': s(ks[5], (E, D_DELTA), E ** (-0.5)), 'W_delta_2': s(ks[6], (D_DELTA, E), D_DELTA ** (-0.5)), 'b_delta_2': s(ks[7], (E,), 0.02), 'W_B': s(ks[8], (E, N), E ** (-0.5)), 'W_C': s(ks[9], (E, N), E ** (-0.5)), 'A_log': s(ks[10], (E, N), 0.5), 'W_D': jnp.ones((E,), jnp.float32), 'W_out': s(ks[11], (E, D), E ** (-0.5))}
    _L1_attn_all = _L1_attn_setup()
    _L1_attn_in = {k: v for k, v in _L1_attn_all.items() if k in ('norm_w', 'W_skip', 'W_in', 'conv_w', 'conv_b', 'W_delta_1', 'W_delta_2', 'b_delta_2', 'W_B', 'W_C', 'A_log', 'W_D', 'W_out')}
    del _L1_attn_all

    def _L1_xattn_setup():
        import jax, jax.numpy as jnp
        import numpy as np
        EPS = 1e-05

        def rmsnorm(x, g, eps=EPS):
            var = jnp.mean(jnp.square(x), axis=-1, keepdims=True)
            return x * jax.lax.rsqrt(var + eps) * g
        key = jax.random.key(seed)
        ks = jax.random.split(key, 8)
        B, Sq, Skv = (2, 1024, 128)
        dim, cdim, H, D = (512, 256, 16, 128)
        inner = H * D
        s = lambda f: 1.0 / np.sqrt(f)
        return {'hidden_states': jax.random.normal(ks[0], (B, Sq, dim), jnp.float32), 'encoder_hidden_states': jax.random.normal(ks[1], (B, Skv, cdim), jnp.float32), 'Wq': jax.random.normal(ks[2], (dim, inner), jnp.float32) * s(dim), 'Wk': jax.random.normal(ks[3], (cdim, inner), jnp.float32) * s(cdim), 'Wv': jax.random.normal(ks[4], (cdim, inner), jnp.float32) * s(cdim), 'Wo': jax.random.normal(ks[5], (inner, dim), jnp.float32) * s(inner), 'gq': jnp.ones((D,), jnp.float32), 'gk': jnp.ones((D,), jnp.float32)}
    _L1_xattn_all = _L1_xattn_setup()
    _L1_xattn_in = {k: v for k, v in _L1_xattn_all.items() if k in ('Wq', 'Wk', 'Wv', 'Wo', 'gq', 'gk')}
    del _L1_xattn_all

    def _L1_ffn_setup():
        import jax, jax.numpy as jnp
        import numpy as np
        B, S, D_IN, D_OUT = (4, 512, 512, 512)
        EPS = 1e-10
        key = jax.random.key(seed)
        kx, kw, kb = jax.random.split(key, 3)
        x = jax.random.normal(kx, (B, S, D_IN), dtype=jnp.float32)
        weight = jax.random.normal(kw, (D_OUT, D_IN), dtype=jnp.float32) * 0.02
        bias = jax.random.normal(kb, (D_OUT,), dtype=jnp.float32) * 0.02
        return {'x': x, 'weight': weight, 'bias': bias}
    _L1_ffn_all = _L1_ffn_setup()
    _L1_ffn_in = {k: v for k, v in _L1_ffn_all.items() if k in ('weight', 'bias')}
    del _L1_ffn_all
    return {'x': x, 'ctx_1024': ctx_1024, 'fside_BxSx2_0': fside_BxSx2_0, 'L0_attn_Wq': _L0_attn_in['Wq'], 'L0_attn_Wk': _L0_attn_in['Wk'], 'L0_attn_Wv': _L0_attn_in['Wv'], 'L0_attn_Wo': _L0_attn_in['Wo'], 'L0_xattn_Wq': _L0_xattn_in['Wq'], 'L0_xattn_Wkv': _L0_xattn_in['Wkv'], 'L0_xattn_Wout': _L0_xattn_in['Wout'], 'L0_xattn_bout': _L0_xattn_in['bout'], 'L0_ffn_router_w': _L0_ffn_in['router_w'], 'L0_ffn_router_b': _L0_ffn_in['router_b'], 'L0_ffn_expert_w': _L0_ffn_in['expert_w'], 'L0_ffn_expert_b': _L0_ffn_in['expert_b'], 'L1_attn_norm_w': _L1_attn_in['norm_w'], 'L1_attn_W_skip': _L1_attn_in['W_skip'], 'L1_attn_W_in': _L1_attn_in['W_in'], 'L1_attn_conv_w': _L1_attn_in['conv_w'], 'L1_attn_conv_b': _L1_attn_in['conv_b'], 'L1_attn_W_delta_1': _L1_attn_in['W_delta_1'], 'L1_attn_W_delta_2': _L1_attn_in['W_delta_2'], 'L1_attn_b_delta_2': _L1_attn_in['b_delta_2'], 'L1_attn_W_B': _L1_attn_in['W_B'], 'L1_attn_W_C': _L1_attn_in['W_C'], 'L1_attn_A_log': _L1_attn_in['A_log'], 'L1_attn_W_D': _L1_attn_in['W_D'], 'L1_attn_W_out': _L1_attn_in['W_out'], 'L1_xattn_Wq': _L1_xattn_in['Wq'], 'L1_xattn_Wk': _L1_xattn_in['Wk'], 'L1_xattn_Wv': _L1_xattn_in['Wv'], 'L1_xattn_Wo': _L1_xattn_in['Wo'], 'L1_xattn_gq': _L1_xattn_in['gq'], 'L1_xattn_gk': _L1_xattn_in['gk'], 'L1_ffn_weight': _L1_ffn_in['weight'], 'L1_ffn_bias': _L1_ffn_in['bias']}

def reference(x, ctx_1024, fside_BxSx2_0, L0_attn_Wq, L0_attn_Wk, L0_attn_Wv, L0_attn_Wo, L0_xattn_Wq, L0_xattn_Wkv, L0_xattn_Wout, L0_xattn_bout, L0_ffn_router_w, L0_ffn_router_b, L0_ffn_expert_w, L0_ffn_expert_b, L1_attn_norm_w, L1_attn_W_skip, L1_attn_W_in, L1_attn_conv_w, L1_attn_conv_b, L1_attn_W_delta_1, L1_attn_W_delta_2, L1_attn_b_delta_2, L1_attn_W_B, L1_attn_W_C, L1_attn_A_log, L1_attn_W_D, L1_attn_W_out, L1_xattn_Wq, L1_xattn_Wk, L1_xattn_Wv, L1_xattn_Wo, L1_xattn_gq, L1_xattn_gk, L1_ffn_weight, L1_ffn_bias):
    import jax
    import jax.numpy as jnp

    def _L0_attn_ref(X, Wq, Wk, Wv, Wo):
        import jax, jax.numpy as jnp
        import numpy as np
        B, T, C = (2, 512, 512)
        NH, NKV, HD = (16, 8, 64)
        SOFTCAP = 50.0
        ROPE_BASE = 10000.0

        def _rotate_half(x):
            x1, x2 = (x[..., :x.shape[-1] // 2], x[..., x.shape[-1] // 2:])
            return jnp.concatenate((-x2, x1), axis=-1)

        def _rope_cos_sin(t, head_dim, dtype):
            inv_freq = 1.0 / ROPE_BASE ** (jnp.arange(0, head_dim, 2, dtype=jnp.int32).astype(jnp.float32) / head_dim)
            pos = jnp.arange(t, dtype=jnp.float32)
            freqs = pos[:, None] * inv_freq[None, :]
            emb = jnp.concatenate((freqs, freqs), axis=-1)
            return (jnp.cos(emb).astype(dtype)[None, None], jnp.sin(emb).astype(dtype)[None, None])
        b, t, c = X.shape
        n_rep = NH // NKV
        q = (X @ Wq).reshape(b, t, NH, HD).transpose(0, 2, 1, 3)
        k = (X @ Wk).reshape(b, t, NKV, HD).transpose(0, 2, 1, 3)
        v = (X @ Wv).reshape(b, t, NKV, HD).transpose(0, 2, 1, 3)
        cos, sin = _rope_cos_sin(t, HD, X.dtype)
        q = q * cos + _rotate_half(q) * sin
        k = k * cos + _rotate_half(k) * sin
        k = jnp.repeat(k, n_rep, axis=1)
        v = jnp.repeat(v, n_rep, axis=1)
        scale = 256.0 ** (-0.5)
        att = jnp.einsum('bhqd,bhkd->bhqk', q, k) * scale
        att = SOFTCAP * jnp.tanh(att / SOFTCAP)
        causal = jnp.tril(jnp.ones((t, t), dtype=bool))
        att = jnp.where(causal[None, None], att, -jnp.inf)
        att = jax.nn.softmax(att, axis=-1)
        y = jnp.einsum('bhqk,bhkd->bhqd', att, v)
        y = y.transpose(0, 2, 1, 3).reshape(b, t, NH * HD)
        return y @ Wo

    def _L0_xattn_ref(x, ctx, pos_map, ctx_pos_map, Wq, Wkv, Wout, bout):
        import jax, jax.numpy as jnp
        import numpy as np
        DIM = 512
        CTX_DIM = 256
        N_HEADS = 32
        HEAD_DIM = DIM // N_HEADS
        POS_DIM = 2
        B, N, CTXN = (2, 512, 512)
        ROPE_BASE = 10000.0

        def apply_axial_rope(x, pos):
            b, n, h, d = x.shape
            p = pos.shape[-1]
            dpa = d // p
            half = dpa // 2
            freqs = ROPE_BASE ** (-jnp.arange(half, dtype=x.dtype) / half)
            ang = pos[..., :, None] * freqs
            cos = jnp.cos(ang)[:, :, None, :, :]
            sin = jnp.sin(ang)[:, :, None, :, :]
            xr = x.reshape(b, n, h, p, half, 2)
            x1, x2 = (xr[..., 0], xr[..., 1])
            out = jnp.stack([x1 * cos - x2 * sin, x1 * sin + x2 * cos], axis=-1)
            return out.reshape(b, n, h, d)
        b, n, _ = x.shape
        ctx_n = ctx.shape[1]
        q = (x @ Wq).reshape(b, n, N_HEADS, HEAD_DIM)
        k, v = jnp.split(ctx @ Wkv, 2, axis=-1)
        k = k.reshape(b, ctx_n, N_HEADS, HEAD_DIM)
        v = v.reshape(b, ctx_n, N_HEADS, HEAD_DIM)
        q = apply_axial_rope(q, pos_map)
        k = apply_axial_rope(k, ctx_pos_map)
        scale = 1.0 / np.sqrt(HEAD_DIM).astype(np.float32)
        logits = jnp.einsum('bqhd,bkhd->bhqk', q, k) * scale
        w = jax.nn.softmax(logits, axis=-1)
        attn = jnp.einsum('bhqk,bkhd->bqhd', w, v)
        attn = attn.reshape(b, n, N_HEADS * HEAD_DIM)
        return attn @ Wout + bout

    def _L0_ffn_ref(hidden_states, router_w, router_b, expert_w, expert_b):
        import jax, jax.numpy as jnp
        import numpy as np
        TOP_K = 2
        B, S, H = hidden_states.shape
        E, O, _ = expert_w.shape
        T = B * S
        h = hidden_states.reshape(T, H)
        logits = (h @ router_w.T + router_b).reshape(T, O, E)
        probs = jax.nn.softmax(logits.astype(jnp.float32), axis=-1)
        w, sel = jax.lax.top_k(probs, TOP_K)
        w = w / jnp.sum(w, axis=-1, keepdims=True)
        w = w.astype(h.dtype)
        t_idx = jnp.arange(T)[:, None, None]
        c = jnp.zeros((T, E), dtype=h.dtype).at[t_idx, sel].add(w)
        expert_out = jnp.einsum('th,eoh->teo', h, expert_w) + expert_b[None, :, :]
        final = jnp.einsum('te,teo->to', c, expert_out)
        return final.reshape(B, S, O)

    def _L1_attn_ref(resid, norm_w, W_skip, W_in, conv_w, conv_b, W_delta_1, W_delta_2, b_delta_2, W_B, W_C, A_log, W_D, W_out):
        import jax, jax.numpy as jnp
        import numpy as np
        D, E, N, D_DELTA, D_CONV = (512, 1024, 16, 128, 4)
        B_SZ, L = (1, 512)
        EPS = 1e-05

        def _silu(x):
            return x * jax.nn.sigmoid(x)
        resid_norm = resid * jax.lax.rsqrt(jnp.mean(resid * resid, axis=-1, keepdims=True) + EPS) * norm_w
        skip = resid_norm @ W_skip
        x_in = resid_norm @ W_in
        conv = jax.lax.conv_general_dilated(x_in, conv_w, window_strides=(1,), padding=[(D_CONV - 1, 0)], dimension_numbers=('NWC', 'WIO', 'NWC'), feature_group_count=E)
        x = _silu(conv + conv_b)
        delta = jax.nn.softplus(x @ W_delta_1 @ W_delta_2 + b_delta_2)
        Bm = x @ W_B
        Cm = x @ W_C
        A = -jnp.exp(A_log)

        def step(h, inp):
            d_l, B_l, C_l, x_l = inp
            A_bar = jnp.exp(d_l[:, :, None] * A)
            h = h * A_bar + (d_l * x_l)[:, :, None] * B_l[:, None, :]
            y_l = jnp.einsum('ben,bn->be', h, C_l)
            return (h, y_l)
        h0 = jnp.zeros((resid.shape[0], E, N), x.dtype)
        xs = (jnp.swapaxes(delta, 0, 1), jnp.swapaxes(Bm, 0, 1), jnp.swapaxes(Cm, 0, 1), jnp.swapaxes(x, 0, 1))
        _, ys = jax.lax.scan(step, h0, xs)
        y = jnp.swapaxes(ys, 0, 1)
        y_apply_D = y + x * W_D
        y_skip = y_apply_D * _silu(skip)
        return resid + y_skip @ W_out

    def _L1_xattn_ref(hidden_states, encoder_hidden_states, Wq, Wk, Wv, Wo, gq, gk):
        import jax, jax.numpy as jnp
        import numpy as np
        EPS = 1e-05

        def rmsnorm(x, g, eps=EPS):
            var = jnp.mean(jnp.square(x), axis=-1, keepdims=True)
            return x * jax.lax.rsqrt(var + eps) * g
        B, Sq, _ = hidden_states.shape
        Skv = encoder_hidden_states.shape[1]
        D = gq.shape[0]
        H = Wq.shape[1] // D
        scale = 1.0 / np.sqrt(D)
        q = (hidden_states @ Wq).reshape(B, Sq, H, D)
        k = (encoder_hidden_states @ Wk).reshape(B, Skv, H, D)
        v = (encoder_hidden_states @ Wv).reshape(B, Skv, H, D)
        q = rmsnorm(q, gq)
        k = rmsnorm(k, gk)
        scores = jnp.einsum('bqhd,bkhd->bhqk', q, k) * scale
        attn = jax.nn.softmax(scores, axis=-1)
        out = jnp.einsum('bhqk,bkhd->bqhd', attn, v)
        out = out.reshape(B, Sq, H * D)
        return out @ Wo

    def _L1_ffn_ref(x, weight, bias):
        import jax, jax.numpy as jnp
        import numpy as np
        B, S, D_IN, D_OUT = (4, 512, 512, 512)
        EPS = 1e-10
        scale = jnp.mean(jnp.abs(weight))
        w_t = jnp.clip(jnp.round(weight / (scale + EPS)), -1.0, 1.0)
        w_ste = weight + jax.lax.stop_gradient(w_t * scale - weight)
        return jnp.einsum('bsi,oi->bso', x, w_ste) + bias
    x = _layernorm(x + _L0_attn_ref(x, L0_attn_Wq, L0_attn_Wk, L0_attn_Wv, L0_attn_Wo), axis=-1)
    x = _layernorm(x + _L0_xattn_ref(x, ctx_1024, fside_BxSx2_0, fside_BxSx2_0, L0_xattn_Wq, L0_xattn_Wkv, L0_xattn_Wout, L0_xattn_bout), axis=-1)
    x = _layernorm(x + _L0_ffn_ref(x, L0_ffn_router_w, L0_ffn_router_b, L0_ffn_expert_w, L0_ffn_expert_b), axis=-1)
    x = _layernorm(x + _L1_attn_ref(x, L1_attn_norm_w, L1_attn_W_skip, L1_attn_W_in, L1_attn_conv_w, L1_attn_conv_b, L1_attn_W_delta_1, L1_attn_W_delta_2, L1_attn_b_delta_2, L1_attn_W_B, L1_attn_W_C, L1_attn_A_log, L1_attn_W_D, L1_attn_W_out), axis=-1)
    x = _layernorm(x + _L1_xattn_ref(x, ctx_1024, L1_xattn_Wq, L1_xattn_Wk, L1_xattn_Wv, L1_xattn_Wo, L1_xattn_gq, L1_xattn_gk), axis=-1)
    x = _layernorm(x + _L1_ffn_ref(x, L1_ffn_weight, L1_ffn_bias), axis=-1)
    return x

_drawn_inputs = setup_inputs


def setup_inputs(seed=0):
    import zlib

    import numpy as np

    out = dict(_drawn_inputs(seed))
    spreads = {'L0_xattn_bout': (0.0, 0.1),
     'L0_ffn_router_b': (0.0, 0.1),
     'L0_ffn_expert_b': (0.0, 0.1),
     'L1_attn_norm_w': (1.0, 0.2),
     'L1_attn_W_D': (1.0, 0.2),
     'L1_xattn_gq': (1.0, 0.2),
     'L1_xattn_gk': (1.0, 0.2)}
    factors = {'L0_attn_Wq': 8.0,
     'L0_attn_Wk': 8.0,
     'L1_attn_conv_b': 5.063,
     'L1_attn_b_delta_2': 23.113,
     'L1_ffn_bias': 2.965}
    for name, (base, spread) in spreads.items():
        noise = np.random.default_rng([zlib.crc32(name.encode()), seed]).standard_normal(out[name].shape)
        drawn = base * np.exp(spread * noise) if base else spread * noise
        out[name] = jnp.asarray(drawn.astype(out[name].dtype))
    for name, factor in factors.items():
        out[name] = (out[name] * factor).astype(out[name].dtype)
    return out
```

```python
from contextlib import ExitStack

import concourse.bass as bass
from concourse import mybir

F32 = mybir.dt.float32
ALU = mybir.AluOpType
ACT = mybir.ActivationFunctionType
AX = mybir.AxisListType

P = 128
SEQS, TOK, D = 16, 128, 512
KC = D // P
EPS = 1e-5
DMA = 16
TWO_PI = 6.283185307179586
ARENA = 53200


class Region:

    def __init__(self, arena, start, end=ARENA):
        self.arena, self.at, self.end = arena, start, end

    def take(self, *dims):
        n = 1
        for d in dims:
            n *= d
        assert self.at + n <= self.end, (self.at, n, self.end)
        view = self.arena[:, self.at:self.at + n]
        self.at += n
        if len(dims) == 2:
            return view.rearrange("p (a b) -> p a b", a=dims[0])
        if len(dims) == 3:
            return view.rearrange("p (a b c) -> p a b c", a=dims[0], b=dims[1])
        return view


def reused(eng, sem, value):
    if not isinstance(value, int) or value > 0:
        eng.wait_ge(sem, value)


class Steps:

    def __init__(self, eng, sem, before):
        self.eng, self.sem, self.before, self.n = eng, sem, before, 0

    def __call__(self, ins):
        ins.then_inc(self.sem, 1)
        self.n += 1

    def wait(self):
        reused(self.eng, self.sem, self.before + self.n)


def over_sequences(eng, body):
    body(0)
    with eng.Fori(1, SEQS - 1) as b:
        body(b)


def row(dram, b):
    return dram[bass.ds(b, 1), :, :].rearrange("a p d -> (a p) d")


def spread(ap, axis, n):
    v = ap.unsqueeze(axis)
    shape = list(v.shape)
    shape[axis] = n
    return v.broadcast_to(shape)


def project(pe, bank, stationary, moving, chunks):
    for c in range(chunks):
        last = pe.matmul(bank, stationary(c), moving(c), start=(c == 0), stop=(c == chunks - 1))
    return last


def turn(pe, bank, tiles, ident):
    for i, tile in enumerate(tiles):
        last = pe.transpose(bank[:, i * P:(i + 1) * P], tile, ident)
    return last


def halves(tile, n=KC):
    return [tile[:, i * P:(i + 1) * P] for i in range(n)]


class NormSems:

    def __init__(self, sem, stage):
        self.var = sem(f"{stage}_variance_ready")
        self.rstd = sem(f"{stage}_rstd_ready")
        self.out = sem(f"{stage}_normed")


def norm_moments(dve, sems, steps, z, stats, moments):
    steps.wait()
    steps(dve.bn_stats(stats, z))
    steps.wait()
    dve.memset(moments[:, 2:3], 0.0)
    steps(dve.bn_aggr(moments[:, 0:2], stats))
    steps.wait()
    dve.tensor_scalar(moments[:, 1:2], moments[:, 1:2], EPS, None, ALU.add).then_inc(sems.var, 1)


def norm_apply(dve, b, sems, z, moments, rstd, out, stored):
    dve.wait_ge(sems.rstd, b + 1)
    if stored is not None:
        reused(dve, stored, b * DMA)
    dve.tensor_scalar(out, z, moments[:, 0:1], rstd, ALU.subtract, ALU.mult).then_inc(sems.out, 1)


def norm_vector(dve, b, sems, steps, z, stats, moments, rstd, out, stored):
    norm_moments(dve, sems, steps, z, stats, moments)
    norm_apply(dve, b, sems, z, moments, rstd, out, stored)


def norm_gpsimd(pool, b, sems, moments, rstd, minus_half):
    pool.wait_ge(sems.var, b + 1)
    pool.tensor_tensor(rstd, moments[:, 1:2], minus_half, ALU.pow).then_inc(sems.rstd, 1)


def stage_self_attention(nc, sem, ps, arena, const, weights, prefetch, src, dst):
    HEADS, KV, HD = 16, 8, 64
    CAP, SCALE = 50.0, 256.0 ** -0.5
    ident, minus_half = const["ident"], const["minus_half"]
    cos, sgnsin, causal = const["rope_cos"], const["rope_sgnsin"], const["causal"]
    Wqkv, Wo, weights_loaded = weights

    r = Region(arena, const["work"])
    xa, xr = r.take(D), r.take(D)
    xT = r.take(KC, P)
    tcos, tsin = r.take(3, D), r.take(3, D)
    qk = r.take(3 * D)
    qkT = r.take(12, P)
    V = r.take(KV, HD + 1)
    prob = r.take(4, D)
    y, yT = r.take(HEADS * HD), r.take(8, P)
    rden = r.take(4, 4)
    z, out = r.take(D), r.take(D)
    stats, moments, rstd = r.take(6), r.take(3), r.take(1)
    qT, kT = qkT[:, 0:8, :], qkT[:, 8:12, :]

    x_loaded = sem("a_x_loaded")
    resid_loaded = sem("a_resid_loaded")
    stored = sem("a_stored")
    consts_set = sem("a_consts_set")
    x_turned = sem("a_x_turned")
    xT_copied = sem("a_xT_copied")
    projected = sem("a_projected")
    v_copied = sem("a_v_copied")
    rope_parts = sem("a_rope_parts")
    roped = sem("a_roped")
    qk_turned = sem("a_qk_turned")
    qkT_copied = sem("a_qkT_copied")
    scored = sem("a_scored")
    capped_done = sem("a_capped")
    exp_done = sem("a_exp_done")
    masked = sem("a_masked")
    mixed = sem("a_mixed")
    y_normed = sem("a_y_normed")
    y_turned = sem("a_y_turned")
    yT_copied = sem("a_yT_copied")
    out_projected = sem("a_out_projected")
    resid_added = sem("a_resid_added")
    dve_steps = sem("a_dve_steps")
    norm = NormSems(sem, "a")
    DVE_STEPS = 6
    LAST = SEQS - 1

    X_BANK = 4
    P_BANK = [5, 6, 5, 6]
    Y_BANK = [7, 4, 7, 4]
    YT_BANK = [5, 6]
    O_BANK = 7

    with nc.Block() as block:
        @block.sync
        def _(sp):
            sp.dma_start(xa, row(src, 0)).then_inc(x_loaded, DMA)
            prefetch(sp)
            sp.wait_ge(x_turned, 1)
            sp.dma_start(xa, row(src, 1)).then_inc(x_loaded, DMA)

            def body(b, more):
                reused(sp, resid_added, b)
                sp.dma_start(xr, row(src, b)).then_inc(resid_loaded, DMA)
                if more:
                    sp.wait_ge(x_turned, b + 2)
                    sp.dma_start(xa, row(src, b + 2)).then_inc(x_loaded, DMA)
                sp.wait_ge(norm.out, b + 1)
                sp.dma_start(row(dst, b), out).then_inc(stored, DMA)

            body(0, True)
            with sp.Fori(1, SEQS - 2) as b:
                body(b, True)
            body(SEQS - 2, False)
            body(LAST, False)
            sp.wait_ge(stored, SEQS * DMA)

        @block.tensor
        def _(pe):
            def turn_x(b, first=False):
                pe.wait_ge(x_loaded, (b + 1) * DMA)
                if not first:
                    pe.wait_ge(y_normed, (b - 1) * 4)
                turn(pe, ps[:, X_BANK, :], halves(xa), ident).then_inc(x_turned, 1)

            def proj(b, c, first=False):
                if c == 0:
                    pe.wait_ge(xT_copied, b + 1)
                    if not first:
                        pe.wait_ge(yT_copied, (b - 1) * 2)
                if c == 2:
                    pe.wait_ge(rope_parts, b * 3 + 1)
                if c == 3:
                    pe.wait_ge(rope_parts, b * 3 + 2)
                project(pe, ps[:, P_BANK[c], :], lambda k: xT[:, k, :],
                        lambda k: Wqkv[:, k, c * D:(c + 1) * D], KC).then_inc(projected, 1)

            def turn_qk(b):
                pe.wait_ge(roped, b * 3 + 3)
                reused(pe, capped_done, b * 4)
                for t in range(2):
                    turn(pe, ps[:, t, :], halves(qk[:, t * D:(t + 1) * D]), ident).then_inc(qk_turned, 1)
                turn(pe, ps[:, 2, :], halves(qk[:, 2 * D:3 * D]), ident).then_inc(qk_turned, 1)

            def scores(b):
                pe.wait_ge(qkT_copied, b * 3 + 3)
                for g in range(4):
                    ihalf, p = g // 2, g % 2
                    rows = slice(64 * p, 64 * p + 64)
                    for i in range(2):
                        t = 2 * ihalf + i
                        last = pe.matmul(ps[:, g, i * 256:(i + 1) * 256], kT[rows, t, :],
                                         qT[rows, 2 * t:2 * t + 2, :], start=True, stop=True)
                    last.then_inc(scored, 1)

            def mix(b, last=False):
                pe.wait_ge(v_copied, b + 1)
                for g in range(4):
                    ihalf, p = g // 2, g % 2
                    pe.wait_ge(masked, b * 4 + g + 1)
                    if g == 0:
                        reused(pe, resid_added, b)
                    elif g == 1:
                        pe.wait_ge(xT_copied, b + (1 if last else 2))
                    else:
                        pe.wait_ge(y_normed, b * 4 + g - 1)
                    for s in range(4):
                        kv = 2 * (2 * ihalf + s // 2) + p
                        done = pe.matmul(ps[:, Y_BANK[g], s * 65:(s + 1) * 65], prob[:, g, s * P:(s + 1) * P],
                                         V[:, kv, :], start=True, stop=True)
                    done.then_inc(mixed, 1)

            def out_proj(b, last=False):
                pe.wait_ge(y_normed, b * 4 + 4)
                if not last:
                    pe.wait_ge(rope_parts, b * 3 + 6)
                    pe.wait_ge(v_copied, b + 2)
                for t in range(2):
                    turn(pe, ps[:, YT_BANK[t], :], halves(y[:, t * D:(t + 1) * D]), ident).then_inc(y_turned, 1)
                pe.wait_ge(yT_copied, b * 2 + 2)
                project(pe, ps[:, O_BANK, :], lambda k: yT[:, k, :], lambda k: Wo[:, k, :], 8)\
                    .then_inc(out_projected, 1)

            pe.wait_ge(weights_loaded, 4 * DMA)
            pe.wait_ge(const["loaded"], const["loads"] * DMA)
            turn_x(0, first=True)
            for c in range(4):
                proj(0, c, first=True)

            def body(b):
                turn_qk(b)
                turn_x(b + 1)
                proj(b + 1, 0)
                proj(b + 1, 1)
                scores(b)
                proj(b + 1, 2)
                proj(b + 1, 3)
                mix(b)
                out_proj(b)

            over_sequences(pe, body)
            turn_qk(LAST)
            scores(LAST)
            mix(LAST, last=True)
            out_proj(LAST, last=True)

        @block.scalar
        def _(act):
            def copy_xT(b):
                act.wait_ge(x_turned, b + 1)
                reused(act, projected, b * 4)
                act.activation(xT, ps[:, X_BANK, :].rearrange("p (a b) -> p a b", a=KC), ACT.Copy)\
                    .then_inc(xT_copied, 1)

            def copy_v(b):
                act.wait_ge(projected, b * 4 + 4)
                reused(act, mixed, b * 4)
                act.activation(V[:, :, 0:HD], ps[:, P_BANK[3], :].rearrange("p (h d) -> p h d", h=KV), ACT.Copy)\
                    .then_inc(v_copied, 1)

            def copy_qk(b):
                for t in range(3):
                    act.wait_ge(qk_turned, b * 3 + t + 1)
                    if t == 0:
                        reused(act, scored, b * 4)
                    act.activation(qkT[:, 4 * t:4 * t + 4, :], ps[:, t, :].rearrange("p (a b) -> p a b", a=4),
                                   ACT.Copy).then_inc(qkT_copied, 1)

            def softmax(b):
                for g in range(4):
                    act.wait_ge(scored, b * 4 + g + 1)
                    reused(act, mixed, b * 4)
                    act.activation(prob[:, g, :], ps[:, g, :], ACT.Tanh, scale=SCALE / CAP)\
                        .then_inc(capped_done, 1)
                for g in range(4):
                    act.wait_ge(capped_done, b * 4 + g + 1)
                    act.activation(prob[:, g, :], prob[:, g, :], ACT.Exp, scale=CAP).then_inc(exp_done, 1)

            def copy_yT(b):
                for t in range(2):
                    act.wait_ge(y_turned, b * 2 + t + 1)
                    reused(act, out_projected, b)
                    act.activation(yT[:, 4 * t:4 * t + 4, :],
                                   ps[:, YT_BANK[t], :].rearrange("p (a b) -> p a b", a=4), ACT.Copy)\
                        .then_inc(yT_copied, 1)

            act.wait_ge(consts_set, 1)
            copy_xT(0)
            copy_v(0)

            def body(b):
                copy_qk(b)
                copy_xT(b + 1)
                softmax(b)
                copy_v(b + 1)
                copy_yT(b)

            over_sequences(act, body)
            copy_qk(LAST)
            softmax(LAST)
            copy_yT(LAST)

        @block.vector
        def _(dve):
            def rope_products(b, c):
                src_bank = ps[:, P_BANK[c], :].rearrange("p (h a d) -> p h a d", h=8, a=2)
                dve.wait_ge(projected, b * 4 + c + 1)
                reused(dve, roped, b * 3)
                dve.tensor_tensor(tcos[:, c, :].rearrange("p (h a) -> p h a", h=8),
                                  ps[:, P_BANK[c], :].rearrange("p (h a) -> p h a", h=8),
                                  spread(cos, 1, 8), ALU.mult)
                dve.tensor_tensor(tsin[:, c, :].rearrange("p (h a d) -> p h a d", h=8, a=2),
                                  src_bank[:, :, ::-1, :],
                                  spread(sgnsin.rearrange("p (a d) -> p a d", a=2), 1, 8), ALU.mult)\
                    .then_inc(rope_parts, 1)

            def norm_mix(b):
                st = Steps(dve, dve_steps, b * DVE_STEPS)
                for g in range(4):
                    ihalf, p = g // 2, g % 2
                    bank = ps[:, Y_BANK[g], 0:260].rearrange("q (s d) -> q s d", s=4)
                    dve.wait_ge(mixed, b * 4 + g + 1)
                    st(dve.reciprocal(rden[:, g, :], bank[:, :, HD]))
                    st.wait()
                    if g == 0:
                        reused(dve, y_turned, b * 2)
                    heads = y[:, ihalf * D:(ihalf + 1) * D].rearrange(
                        "q (i p j d) -> q i p j d", i=2, p=2, j=2)[:, :, p]
                    for i in range(2):
                        last = dve.tensor_tensor(heads[:, i], bank[:, 2 * i:2 * i + 2, 0:HD],
                                                 spread(rden[:, g, 2 * i:2 * i + 2], 2, HD), ALU.mult)
                    last.then_inc(y_normed, 1)
                dve.wait_ge(out_projected, b + 1)
                dve.wait_ge(resid_loaded, (b + 1) * DMA)
                dve.tensor_tensor(z, ps[:, O_BANK, :], xr, ALU.add).then_inc(resid_added, 1)
                dve.wait_ge(resid_added, b + 1)
                st.wait()
                norm_vector(dve, b, norm, st, z, stats, moments, rstd, out, stored)
                assert st.n == DVE_STEPS, st.n

            dve.memset(V[:, :, HD:HD + 1], 1.0).then_inc(consts_set, 1)
            dve.wait_ge(const["loaded"], const["loads"] * DMA)
            for c in range(3):
                rope_products(0, c)

            def body(b):
                rope_products(b + 1, 0)
                rope_products(b + 1, 1)
                rope_products(b + 1, 2)
                norm_mix(b)

            over_sequences(dve, body)
            norm_mix(LAST)

        @block.gpsimd
        def _(pool):
            def rope_sum(b, c):
                pool.wait_ge(rope_parts, b * 3 + c + 1)
                if c == 0:
                    reused(pool, qk_turned, b * 3)
                pool.tensor_tensor(qk[:, c * D:(c + 1) * D], tcos[:, c, :], tsin[:, c, :], ALU.add)\
                    .then_inc(roped, 1)

            def mask(b, g):
                pool.wait_ge(exp_done, b * 4 + g + 1)
                v = prob[:, g, :].rearrange("k (s q) -> k s q", s=4)
                pool.tensor_tensor(v, v, spread(causal, 1, 4), ALU.mult).then_inc(masked, 1)

            pool.wait_ge(const["loaded"], const["loads"] * DMA)
            for c in range(3):
                rope_sum(0, c)

            def body(b):
                rope_sum(b + 1, 0)
                rope_sum(b + 1, 1)
                for g in range(4):
                    mask(b, g)
                rope_sum(b + 1, 2)
                norm_gpsimd(pool, b, norm, moments, rstd, minus_half)

            over_sequences(pool, body)
            for g in range(4):
                mask(LAST, g)
            norm_gpsimd(pool, LAST, norm, moments, rstd, minus_half)


def stage_cross_attention(nc, sem, ps, arena, const, weights, prefetch, src, ctx, pos, dst, extra):
    HEADS, HD, PAD, CC = 32, 16, 32, 2
    SCALE = HD ** -0.5
    TILES = 8
    ident, minus_half = const["ident"], const["minus_half"]
    Wq, Wkv, Wout, bout, weights_loaded = weights

    r = Region(arena, const["work_b"])
    xa, ca, xr = r.take(D), r.take(CC * P), r.take(D)
    xT, cT = r.take(KC, P), r.take(CC, P)
    tcos, tsin = r.take(2, D), r.take(2, D)
    qkp = r.take(2, HEADS * PAD)
    qkT = r.take(2 * TILES, P)
    V = r.take(HEADS, HD + 1)
    prob = r.take(TILES // 2, D)
    probT = r.take(4, D)
    more = Region(arena, *extra)
    prob2 = more.take(TILES // 2, D)
    y, yT = r.take(D), r.take(KC, P)
    top, rden = r.take(TILES, 4), r.take(2, 16)
    z, out = r.take(D), r.take(D)
    stats, moments, rstd = r.take(6), r.take(3), r.take(1)
    cosr, sinr = r.take(SEQS, 16), r.take(SEQS, 16)
    pos_sb, freq = r.take(2 * SEQS), const["freq"]
    ang, turns = tcos[:, 0, 0:128], tcos[:, 0, 128:256]

    def prob_tile(n):
        return prob[:, n, :] if n < 4 else prob2[:, n - 4, :]

    x_loaded = sem("b_x_loaded")
    resid_loaded = sem("b_resid_loaded")
    pos_loaded = sem("b_pos_loaded")
    stored = sem("b_stored")
    consts_set = sem("b_consts_set")
    angles_ready = sem("b_angles_ready")
    sines_ready = sem("b_sines_ready")
    tables_ready = sem("b_tables_ready")
    x_turned = sem("b_x_turned")
    xT_copied = sem("b_xT_copied")
    projected = sem("b_projected")
    v_copied = sem("b_v_copied")
    rope_parts = sem("b_rope_parts")
    roped = sem("b_roped")
    qk_turned = sem("b_qk_turned")
    qkT_copied = sem("b_qkT_copied")
    scored = sem("b_scored")
    top_found = sem("b_top_found")
    shifted = sem("b_shifted")
    exp_done = sem("b_exp_done")
    prob_turned = sem("b_prob_turned")
    probT_copied = sem("b_probT_copied")
    mixed = sem("b_mixed")
    y_normed = sem("b_y_normed")
    y_turned = sem("b_y_turned")
    yT_copied = sem("b_yT_copied")
    out_projected = sem("b_out_projected")
    resid_biased = sem("b_resid_biased")
    resid_added = sem("b_resid_added")
    dve_steps = sem("b_dve_steps")
    norm = NormSems(sem, "b")
    SET_STEPS, DVE_STEPS = 12, 4
    LAST = SEQS - 1
    X_BANK, C_BANK, Q_BANK, K_BANK, V_BANK, YT_BANK, O_BANK = 4, 5, 6, 7, 5, 4, 6
    Y_BANK = [6, 7]

    with nc.Block() as block:
        @block.sync
        def _(sp):
            def load_x(b):
                sp.dma_start(xa, row(src, b)).then_inc(x_loaded, DMA)
                sp.dma_start(ca, row(ctx, b)).then_inc(x_loaded, DMA)

            sp.dma_start(pos_sb.rearrange("t (b p) -> t b p", p=2), pos.rearrange("b t p -> t b p"))\
                .then_inc(pos_loaded, DMA)
            load_x(0)
            prefetch(sp)
            sp.wait_ge(x_turned, 2)
            load_x(1)

            def body(b, more):
                reused(sp, resid_added, b)
                sp.dma_start(xr, row(src, b)).then_inc(resid_loaded, DMA)
                if more:
                    sp.wait_ge(x_turned, 2 * b + 4)
                    load_x(b + 2)
                sp.wait_ge(norm.out, b + 1)
                sp.dma_start(row(dst, b), out).then_inc(stored, DMA)

            body(0, True)
            with sp.Fori(1, SEQS - 2) as b:
                body(b, True)
            body(SEQS - 2, False)
            body(LAST, False)
            sp.wait_ge(stored, SEQS * DMA)

        @block.tensor
        def _(pe):
            def turn_x(b, first=False):
                pe.wait_ge(x_loaded, 2 * (b + 1) * DMA)
                if not first:
                    reused(pe, yT_copied, b - 1)
                turn(pe, ps[:, X_BANK, :], halves(xa), ident).then_inc(x_turned, 1)
                if not first:
                    pe.wait_ge(v_copied, b)
                turn(pe, ps[:, C_BANK, :], halves(ca, CC), ident).then_inc(x_turned, 1)

            def proj_q(b, first=False):
                pe.wait_ge(xT_copied, 2 * b + 1)
                if not first:
                    reused(pe, resid_added, b - 1)
                project(pe, ps[:, Q_BANK, :], lambda k: xT[:, k, :], lambda k: Wq[:, k, :], KC)\
                    .then_inc(projected, 1)

            def proj_k(b, first=False):
                pe.wait_ge(xT_copied, 2 * b + 2)
                if not first:
                    reused(pe, y_normed, (b - 1) * 2)
                project(pe, ps[:, K_BANK, :], lambda k: cT[:, k, :], lambda k: Wkv[:, k, 0:D], CC)\
                    .then_inc(projected, 1)

            def proj_v(b):
                reused(pe, probT_copied, b * 8)
                project(pe, ps[:, V_BANK, :], lambda k: cT[:, k, :], lambda k: Wkv[:, k, D:2 * D], CC)\
                    .then_inc(projected, 1)

            def turn_qk(b):
                reused(pe, shifted, b * 8)
                for n in range(4):
                    if n % 2 == 0:
                        pe.wait_ge(roped, b * 2 + n // 2 + 1)
                    turn(pe, ps[:, n, :], halves(qkp[:, n // 2, (n % 2) * D:(n % 2 + 1) * D]), ident)\
                        .then_inc(qk_turned, 1)

            def scores(b, half):
                if half == 0:
                    pe.wait_ge(qkT_copied, b * 4 + 4)
                for rg in range(4):
                    rows = slice(32 * rg, 32 * rg + 32)
                    if half == 1:
                        pe.wait_ge(shifted, b * 8 + rg + 1)
                    for g in range(4):
                        t = 4 * half + g
                        last = pe.matmul(ps[:, rg, g * P:(g + 1) * P], qkT[rows, t, :], qkT[rows, TILES + t, :],
                                         start=True, stop=True)
                    last.then_inc(scored, 1)

            def turn_prob(b, n, last):
                bank = 4 + n % 2
                pe.wait_ge(exp_done, b * 8 + n + 1)
                if n >= 2:
                    pe.wait_ge(probT_copied, b * 8 + n - 1)
                elif not last:
                    pe.wait_ge(xT_copied, 2 * b + 3 + n)
                turn(pe, ps[:, bank, :], halves(prob_tile(n)), ident).then_inc(prob_turned, 1)

            def mix(b, n, last):
                half, rg = n // 4, n % 4
                pe.wait_ge(probT_copied, b * 8 + n + 1)
                if rg == 0 and not last:
                    pe.wait_ge(rope_parts, (b + 1) * 2 + half + 1)
                for g in range(4):
                    h = 4 * g + rg
                    done = pe.matmul(ps[:, Y_BANK[half], h * 17:(h + 1) * 17], probT[:, n % 4, g * P:(g + 1) * P],
                                     V[:, 16 * half + h, :], start=True, stop=True)
                done.then_inc(mixed, 1)

            def attend(b, last=False):
                pe.wait_ge(v_copied, b + 1)
                turn_prob(b, 0, last)
                for n in range(8):
                    if n < 7:
                        turn_prob(b, n + 1, last)
                    mix(b, n, last)

            def out_proj(b):
                pe.wait_ge(y_normed, b * 2 + 2)
                pe.wait_ge(probT_copied, b * 8 + 8)
                turn(pe, ps[:, YT_BANK, :], halves(y), ident).then_inc(y_turned, 1)
                pe.wait_ge(yT_copied, b + 1)
                project(pe, ps[:, O_BANK, :], lambda k: yT[:, k, :], lambda k: Wout[:, k, :], KC)\
                    .then_inc(out_projected, 1)

            pe.wait_ge(weights_loaded, 4 * DMA)
            turn_x(0, first=True)
            proj_q(0, first=True)
            proj_k(0, first=True)
            proj_v(0)

            def body(b):
                turn_qk(b)
                turn_x(b + 1)
                scores(b, 0)
                proj_q(b + 1)
                scores(b, 1)
                proj_k(b + 1)
                attend(b)
                proj_v(b + 1)
                out_proj(b)

            over_sequences(pe, body)
            turn_qk(LAST)
            scores(LAST, 0)
            scores(LAST, 1)
            attend(LAST, last=True)
            out_proj(LAST)

        @block.scalar
        def _(act):
            def copy_xT(b):
                act.wait_ge(x_turned, 2 * b + 1)
                reused(act, projected, b * 3)
                act.activation(xT, ps[:, X_BANK, :].rearrange("p (a b) -> p a b", a=KC), ACT.Copy)\
                    .then_inc(xT_copied, 1)
                act.wait_ge(x_turned, 2 * b + 2)
                act.activation(cT, ps[:, C_BANK, 0:CC * P].rearrange("p (a b) -> p a b", a=CC), ACT.Copy)\
                    .then_inc(xT_copied, 1)

            def copy_v(b):
                act.wait_ge(projected, b * 3 + 3)
                reused(act, mixed, b * 8)
                act.activation(V[:, :, 0:HD], ps[:, V_BANK, :].rearrange("p (h d) -> p h d", h=HEADS), ACT.Copy)\
                    .then_inc(v_copied, 1)

            def copy_qk(b):
                for n in range(4):
                    act.wait_ge(qk_turned, b * 4 + n + 1)
                    if n == 0:
                        reused(act, scored, b * 8)
                    act.activation(qkT[:, 4 * n:4 * n + 4, :], ps[:, n, :].rearrange("p (a b) -> p a b", a=4),
                                   ACT.Copy).then_inc(qkT_copied, 1)

            def exps(b, half):
                for n in range(4 * half, 4 * half + 4):
                    act.wait_ge(shifted, b * 8 + n + 1)
                    act.activation(prob_tile(n), prob_tile(n), ACT.Exp, scale=SCALE).then_inc(exp_done, 1)

            def copy_probT(b):
                for n in range(8):
                    act.wait_ge(prob_turned, b * 8 + n + 1)
                    reused(act, mixed, b * 8 + n - 3)
                    act.activation(probT[:, n % 4, :], ps[:, 4 + n % 2, :], ACT.Copy).then_inc(probT_copied, 1)

            def copy_yT(b):
                act.wait_ge(y_turned, b + 1)
                reused(act, out_projected, b)
                act.activation(yT, ps[:, YT_BANK, :].rearrange("p (a b) -> p a b", a=4), ACT.Copy)\
                    .then_inc(yT_copied, 1)

            for n, table in ((0, sinr), (1, cosr)):
                act.wait_ge(angles_ready, n + 1)
                reused(act, tables_ready, n)
                act.activation(turns, ang, ACT.Sin).then_inc(sines_ready, 1)
            copy_xT(0)
            act.wait_ge(consts_set, 2)
            copy_v(0)

            def body(b):
                copy_qk(b)
                copy_xT(b + 1)
                exps(b, 0)
                exps(b, 1)
                copy_probT(b)
                copy_v(b + 1)
                copy_yT(b)

            over_sequences(act, body)
            copy_qk(LAST)
            exps(LAST, 0)
            exps(LAST, 1)
            copy_probT(LAST)
            copy_yT(LAST)

        @block.vector
        def _(dve):
            def make_tables():
                st = Steps(dve, dve_steps, 0)
                dve.wait_ge(pos_loaded, DMA)
                HALF_TURN, MAGIC = TWO_PI / 2, 12582912.0
                HI = 6.28125
                for n, (table, shift) in enumerate(((sinr, 0.0), (cosr, HALF_TURN / 2))):
                    if n == 1:
                        dve.wait_ge(tables_ready, 1)
                    dve.tensor_tensor(ang.rearrange("t (b j) -> t b j", j=4), spread(pos_sb, 2, 4),
                                      spread(freq, 1, 2 * SEQS), ALU.mult).then_inc(dve_steps, 1)
                    st.n += 1
                    st.wait()
                    st(dve.tensor_scalar(ang, ang, shift, None, ALU.add))
                    st.wait()
                    st(dve.tensor_scalar(turns, ang, 1.0 / TWO_PI, MAGIC, ALU.mult, ALU.add))
                    st.wait()
                    st(dve.tensor_scalar(turns, turns, -MAGIC, None, ALU.add))
                    st.wait()
                    st(dve.scalar_tensor_tensor(ang, turns, -HI, ang, ALU.mult, ALU.add))
                    st.wait()
                    st(dve.scalar_tensor_tensor(ang, turns, HI - TWO_PI, ang, ALU.mult, ALU.add))
                    st.wait()
                    dve.tensor_scalar(ang, ang, 3.1415925, -3.1415925, ALU.min, ALU.max).then_inc(angles_ready, 1)
                    dve.wait_ge(sines_ready, n + 1)
                    pair = table.rearrange("t b (j s) -> t (b j) s", s=2)
                    if n == 0:
                        dve.tensor_scalar(pair[:, :, 0], turns, -1.0, None, ALU.mult)
                    else:
                        dve.tensor_copy(pair[:, :, 0], turns)
                    dve.tensor_copy(pair[:, :, 1], turns).then_inc(tables_ready, 1)
                dve.wait_ge(tables_ready, 2)
                assert st.n == SET_STEPS, st.n

            def rope_products(b, c):
                bank = ps[:, (Q_BANK, K_BANK)[c], :]
                dve.wait_ge(projected, b * 3 + c + 1)
                reused(dve, roped, b * 2)
                if isinstance(b, int):
                    cosb, sinb = cosr[:, b, :], sinr[:, b, :]
                else:
                    cosb = cosr[:, bass.ds(b, 1), :].rearrange("t b j -> t (b j)")
                    sinb = sinr[:, bass.ds(b, 1), :].rearrange("t b j -> t (b j)")
                dve.tensor_tensor(tcos[:, c, :].rearrange("p (h a) -> p h a", h=HEADS),
                                  bank.rearrange("p (h a) -> p h a", h=HEADS), spread(cosb, 1, HEADS), ALU.mult)
                dve.tensor_tensor(tsin[:, c, :].rearrange("p (h a s) -> p h a s", h=HEADS, s=2),
                                  bank.rearrange("p (h a s) -> p h a s", h=HEADS, s=2)[:, :, :, ::-1],
                                  spread(sinb.rearrange("p (a s) -> p a s", s=2), 1, HEADS), ALU.mult)\
                    .then_inc(rope_parts, 1)

            def shift(b, half):
                for n in range(4 * half, 4 * half + 4):
                    bank = ps[:, n % 4, :].rearrange("q (g k) -> q g k", g=4)
                    dve.wait_ge(scored, b * 8 + n + 1)
                    dve.tensor_reduce(top[:, n, :], bank, AX.X, ALU.max).then_inc(top_found, 1)
                    dve.wait_ge(top_found, b * 8 + n + 1)
                    reused(dve, prob_turned, (b - 1) * 8 + n + 1)
                    dve.tensor_tensor(prob_tile(n).rearrange("q (g k) -> q g k", g=4), bank,
                                      spread(top[:, n, :], 2, P), ALU.subtract).then_inc(shifted, 1)

            def norm_mix(b):
                st = Steps(dve, dve_steps, SET_STEPS + b * DVE_STEPS)
                for half in range(2):
                    bank = ps[:, Y_BANK[half], 0:272].rearrange("q (h d) -> q h d", h=16)
                    dve.wait_ge(mixed, b * 8 + 4 * half + 4)
                    st(dve.reciprocal(rden[:, half, :], bank[:, :, HD]))
                    st.wait()
                    if half == 0:
                        reused(dve, y_turned, b)
                    dve.tensor_tensor(y[:, half * 256:(half + 1) * 256].rearrange("q (h d) -> q h d", h=16),
                                      bank[:, :, 0:HD], spread(rden[:, half, :], 2, HD), ALU.mult)\
                        .then_inc(y_normed, 1)
                dve.wait_ge(out_projected, b + 1)
                dve.wait_ge(resid_biased, b + 1)
                dve.tensor_tensor(z, ps[:, O_BANK, :], xr, ALU.add).then_inc(resid_added, 1)
                dve.wait_ge(resid_added, b + 1)
                norm_vector(dve, b, norm, st, z, stats, moments, rstd, out, stored)
                assert st.n == DVE_STEPS, st.n

            dve.memset(V[:, :, HD:HD + 1], 1.0).then_inc(consts_set, 1)
            make_tables()
            rope_products(0, 0)
            rope_products(0, 1)

            def body(b):
                shift(b, 0)
                rope_products(b + 1, 0)
                shift(b, 1)
                rope_products(b + 1, 1)
                norm_mix(b)

            over_sequences(dve, body)
            shift(LAST, 0)
            shift(LAST, 1)
            norm_mix(LAST)

        @block.gpsimd
        def _(pool):
            def rope_sum(b, c):
                pool.wait_ge(rope_parts, b * 2 + c + 1)
                reused(pool, qk_turned, b * 4)
                pool.tensor_tensor(qkp[:, c, :].rearrange("p (h a) -> p h a", h=HEADS)[:, :, 0:HD],
                                   tcos[:, c, :].rearrange("p (h a) -> p h a", h=HEADS),
                                   tsin[:, c, :].rearrange("p (h a) -> p h a", h=HEADS), ALU.add)\
                    .then_inc(roped, 1)

            def bias(b):
                pool.wait_ge(resid_loaded, (b + 1) * DMA)
                pool.tensor_tensor(xr, xr, bout, ALU.add).then_inc(resid_biased, 1)

            pool.memset(qkp, 0.0).then_inc(consts_set, 1)
            pool.wait_ge(consts_set, 2)
            pool.wait_ge(weights_loaded, 4 * DMA)
            rope_sum(0, 0)
            rope_sum(0, 1)

            def body(b):
                bias(b)
                rope_sum(b + 1, 0)
                rope_sum(b + 1, 1)
                norm_gpsimd(pool, b, norm, moments, rstd, minus_half)

            over_sequences(pool, body)
            bias(LAST)
            norm_gpsimd(pool, LAST, norm, moments, rstd, minus_half)


def over_pairs(eng, body):
    body(0, 0)
    with eng.Fori(0, (SEQS - 2) // 2) as i:
        body(i * 2 + 1, 1)
        body(i * 2 + 2, 0)


def stage_experts(nc, sem, ps, arena, const, weights, prefetch, src, dst, extra):
    E = 8
    QW = D // 4
    ident, minus_half = const["ident"], const["minus_half"]
    Wr, We_chunk, rbias, router_loaded, experts_loaded = weights

    r = Region(arena, const["work_c"])
    logits = [r.take(E, D) for _ in range(2)]
    rb = Region(arena, *extra).take(E, D)
    eb, cT = r.take(D), r.take(P)
    scaled_sb = r.take(D)
    wide, narrow = r.take(E, QW), r.take(E, QW)
    m1, m2, ex = r.take(D), r.take(D), r.take(D)
    w1, w2, left = r.take(QW), r.take(QW), r.take(QW)
    xa, acc, out = r.take(D), r.take(D), r.take(D)
    xT = [r.take(KC, P) for _ in range(2)]
    c = [r.take(E) for _ in range(2)]
    part = r.take(4, E)
    stats, moments, rstd = r.take(6), r.take(3), r.take(1)

    x_loaded = sem("c_x_loaded")
    acc_loaded = sem("c_acc_loaded")
    bias_loaded = sem("c_bias_loaded")
    stored = sem("c_stored")
    x_turned = sem("c_x_turned")
    xT_copied = sem("c_xT_copied")
    routed = sem("c_routed")
    logits_copied = sem("c_logits_copied")
    logits_biased = sem("c_logits_biased")
    gap_ready = sem("c_gap_ready")
    gap_exp = sem("c_gap_exp")
    ties_found = sem("c_ties_found")
    ties_counted = sem("c_ties_counted")
    c_ready = sem("c_c_ready")
    expert_ready = sem("c_expert_ready")
    expert_scaled = sem("c_expert_scaled")
    expert_summed = sem("c_expert_summed")
    c_turned = sem("c_c_turned")
    cT_copied = sem("c_cT_copied")
    bias_ready = sem("c_bias_ready")
    summed = sem("c_summed")
    dve_steps = sem("c_dve_steps")
    pool_steps = sem("c_pool_steps")
    norm = NormSems(sem, "c")
    LAST = SEQS - 1
    R_BANK, E_BANK, X_BANK, C_BANK = 0, 4, 6, 7
    NORM_STEPS = 2

    with nc.Block() as block:
        @block.sync
        def _(sp):
            sp.dma_start(xa, row(src, 0)).then_inc(x_loaded, DMA)
            sp.dma_start(rb.rearrange("p e o -> p (e o)"), rbias[0].partition_broadcast(P)).then_inc(bias_loaded, DMA)
            sp.dma_start(eb[0:E, :], rbias[1]).then_inc(bias_loaded, DMA)
            prefetch[0](sp)
            sp.wait_ge(x_turned, 1)
            sp.dma_start(xa, row(src, 1)).then_inc(x_loaded, DMA)
            sp.dma_start(acc, row(src, 0)).then_inc(acc_loaded, DMA)

            def body(b, left):
                if left > 1:
                    sp.wait_ge(x_turned, b + 2)
                    sp.dma_start(xa, row(src, b + 2)).then_inc(x_loaded, DMA)
                sp.wait_ge(norm.out, b + 1)
                if left > 0:
                    sp.dma_start(acc, row(src, b + 1)).then_inc(acc_loaded, DMA)
                sp.dma_start(row(dst, b), out).then_inc(stored, DMA)

            with sp.Fori(0, SEQS - 2) as b:
                body(b, 2)
            body(SEQS - 2, 1)
            sp.wait_ge(routed, SEQS * E)
            prefetch[1](sp)
            body(LAST, 0)
            sp.wait_ge(stored, SEQS * DMA)

        @block.tensor
        def _(pe):
            def turn_x(b):
                pe.wait_ge(x_loaded, (b + 1) * DMA)
                reused(pe, xT_copied, b)
                turn(pe, ps[:, X_BANK, :], halves(xa), ident).then_inc(x_turned, 1)

            def route(b, par):
                pe.wait_ge(xT_copied, b + 1)
                for e in range(E):
                    reused(pe, logits_copied, b * E + e - 3)
                    project(pe, ps[:, R_BANK + e % 4, :], lambda k: xT[par][:, k, :],
                            lambda k: Wr[:, k, e * D:(e + 1) * D], KC).then_inc(routed, 1)

            def experts(b, par):
                for e in range(E):
                    reused(pe, expert_scaled, b * E + e - 1)
                    project(pe, ps[:, E_BANK + e % 2, :], lambda k: xT[par][:, k, :],
                            lambda k: We_chunk(k)[:, e * D:(e + 1) * D], KC).then_inc(expert_ready, 1)

            def expert_bias(b, par):
                reused(pe, summed, b)
                pe.wait_ge(c_ready, b + 1)
                pe.transpose(ps[0:E, C_BANK, 0:P], c[par], ident).then_inc(c_turned, 1)
                pe.wait_ge(cT_copied, b + 1)
                pe.matmul(ps[:, C_BANK, :], cT[0:E, :], eb[0:E, :], start=True, stop=True).then_inc(bias_ready, 1)

            pe.wait_ge(router_loaded, DMA)
            turn_x(0)
            route(0, 0)
            turn_x(1)
            pe.wait_ge(experts_loaded, KC * DMA)
            pe.wait_ge(bias_loaded, 2 * DMA)

            def body(b, par, turns=True):
                route(b + 1, 1 - par)
                experts(b, par)
                if turns:
                    turn_x(b + 2)
                expert_bias(b, par)

            body(0, 0)
            with pe.Fori(0, (SEQS - 4) // 2) as i:
                body(i * 2 + 1, 1)
                body(i * 2 + 2, 0)
            body(SEQS - 3, 1)
            body(SEQS - 2, 0, turns=False)
            experts(LAST, 1)
            expert_bias(LAST, 1)

        @block.scalar
        def _(act):
            def copy_xT(b, par):
                act.wait_ge(x_turned, b + 1)
                reused(act, expert_ready, (b - 1) * E)
                act.activation(xT[par], ps[:, X_BANK, :].rearrange("p (a b) -> p a b", a=KC), ACT.Copy)\
                    .then_inc(xT_copied, 1)

            def copy_logits(b, par):
                for e in range(E):
                    act.wait_ge(routed, b * E + e + 1)
                    if e == 0:
                        reused(act, c_ready, b - 1)
                    act.activation(logits[par][:, e, :], ps[:, R_BANK + e % 4, :], ACT.Copy)\
                        .then_inc(logits_copied, 1)

            def scale(b, par, e):
                act.wait_ge(expert_ready, b * E + e + 1)
                if e == 0:
                    act.wait_ge(c_ready, b + 1)
                reused(act, expert_summed, b * E + e)
                act.activation(scaled_sb, ps[:, E_BANK + e % 2, :], ACT.Copy, scale=c[par][:, e:e + 1])\
                    .then_inc(expert_scaled, 1)

            def exp_gap(b):
                act.wait_ge(gap_ready, b + 1)
                act.activation(ex, ex, ACT.Exp).then_inc(gap_exp, 1)

            def copy_cT(b):
                act.wait_ge(c_turned, b + 1)
                reused(act, bias_ready, b)
                act.activation(cT[0:E, :], ps[0:E, C_BANK, 0:P], ACT.Copy).then_inc(cT_copied, 1)

            copy_xT(0, 0)
            copy_logits(0, 0)
            exp_gap(0)
            copy_xT(1, 1)

            def body(b, par, turns=True):
                copy_logits(b + 1, 1 - par)
                for e in range(4):
                    scale(b, par, e)
                exp_gap(b + 1)
                for e in range(4, E):
                    scale(b, par, e)
                if turns:
                    copy_xT(b + 2, par)
                copy_cT(b)

            body(0, 0)
            with act.Fori(0, (SEQS - 4) // 2) as i:
                body(i * 2 + 1, 1)
                body(i * 2 + 2, 0)
            body(SEQS - 3, 1)
            body(SEQS - 2, 0, turns=False)
            for e in range(E):
                scale(LAST, 1, e)
            copy_cT(LAST)

        @block.vector
        def _(dve):
            def find_top(b, par, st):
                dve.wait_ge(logits_biased, b * E + E)
                for q in range(4):
                    cols = slice(q * QW, (q + 1) * QW)
                    lg = logits[par][:, :, cols].rearrange("p (a s) o -> p a s o", s=2)
                    st.wait()
                    st(dve.tensor_tensor(wide[:, 0:4, :], lg[:, :, 0, :], lg[:, :, 1, :], ALU.max))
                    st(dve.tensor_tensor(wide[:, 4:8, :], lg[:, :, 0, :], lg[:, :, 1, :], ALU.min))
                    st.wait()
                    hi = wide[:, 0:4, :].rearrange("p (a s) o -> p a s o", s=2)
                    lo = wide[:, 4:8, :].rearrange("p (a s) o -> p a s o", s=2)
                    st(dve.tensor_tensor(narrow[:, 2:4, :], hi[:, :, 0, :], hi[:, :, 1, :], ALU.min))
                    st(dve.tensor_tensor(narrow[:, 4:6, :], lo[:, :, 0, :], lo[:, :, 1, :], ALU.max))
                    st(dve.tensor_tensor(narrow[:, 0:2, :], hi[:, :, 0, :], hi[:, :, 1, :], ALU.max))
                    st.wait()
                    dve.tensor_tensor(narrow[:, 6:8, :], narrow[:, 2:4, :], narrow[:, 4:6, :], ALU.max)\
                        .then_inc(st.sem, 1)
                    st.n += 1
                    dve.tensor_tensor(m1[:, cols], narrow[:, 0, :], narrow[:, 1, :], ALU.max)
                    st.wait()
                    dve.tensor_tensor(narrow[:, 2, :], narrow[:, 0, :], narrow[:, 1, :], ALU.min)
                    st(dve.tensor_tensor(narrow[:, 4, :], narrow[:, 6, :], narrow[:, 7, :], ALU.max))
                    st.wait()
                    st(dve.tensor_tensor(m2[:, cols], narrow[:, 2, :], narrow[:, 4, :], ALU.max))
                st.wait()
                dve.tensor_tensor(ex, m2, m1, ALU.subtract).then_inc(gap_ready, 1)

            def quarter(b, par, q, st):
                cols = slice(q * QW, (q + 1) * QW)
                lg = logits[par][:, :, cols]
                st.wait()
                st(dve.tensor_tensor(left, m1[:, cols], m2[:, cols], ALU.is_gt))
                st(dve.tensor_tensor(wide, lg, spread(m2[:, cols], 1, E), ALU.is_gt))
                st.wait()
                st(dve.tensor_scalar(left, left, -1.0, 2.0, ALU.mult, ALU.add))
                st.wait()
                dve.tensor_tensor(lg, lg, spread(m2[:, cols], 1, E), ALU.is_equal).then_inc(ties_found, 1)
                if q == 0:
                    dve.wait_ge(gap_exp, b + 1)
                st(dve.tensor_scalar(w1, ex[:, cols], 1.0, None, ALU.add))
                st.wait()
                st(dve.reciprocal(w1, w1))
                st.wait()
                st(dve.tensor_tensor(w2, ex[:, cols], w1, ALU.mult))
                st(dve.tensor_tensor(wide, wide, spread(w1, 1, E), ALU.mult))
                dve.wait_ge(ties_counted, b * 4 + q + 1)
                st(dve.scalar_tensor_tensor(lg, narrow, 0.0, lg, ALU.is_ge, ALU.mult))
                st.wait()
                st(dve.tensor_tensor(lg, lg, spread(w2, 1, E), ALU.mult))
                st.wait()
                st(dve.tensor_tensor(wide, wide, lg, ALU.add))
                st.wait()
                st(dve.tensor_reduce(part[:, q, :], wide, AX.X, ALU.add))

            def finish_c(b, par, st):
                reused(dve, expert_scaled, (b - 1) * E)
                reused(dve, c_turned, b - 1)
                st.wait()
                dve.tensor_reduce(c[par], part.rearrange("p q e -> p e q"), AX.X, ALU.add).then_inc(c_ready, 1)

            def normalise(b, steps):
                dve.wait_ge(bias_ready, b + 1)
                dve.wait_ge(expert_summed, b * E + E)
                dve.tensor_tensor(acc, acc, ps[:, C_BANK, :], ALU.add).then_inc(summed, 1)
                dve.wait_ge(summed, b + 1)
                norm_vector(dve, b, norm, steps, acc, stats, moments, rstd, out, stored)

            st = Steps(dve, dve_steps, 0)
            find_top(0, 0, st)
            for q in range(4):
                quarter(0, 0, q, st)
            finish_c(0, 0, st)
            per_top = st.n

            def body(b, par):
                st = Steps(dve, dve_steps, per_top + b * (per_top + NORM_STEPS))
                find_top(b + 1, 1 - par, st)
                quarter(b + 1, 1 - par, 0, st)
                quarter(b + 1, 1 - par, 1, st)
                normalise(b, st)
                quarter(b + 1, 1 - par, 2, st)
                quarter(b + 1, 1 - par, 3, st)
                finish_c(b + 1, 1 - par, st)
                assert st.n == per_top + NORM_STEPS, st.n

            over_pairs(dve, body)
            normalise(LAST, Steps(dve, dve_steps, per_top + LAST * (per_top + NORM_STEPS)))

        @block.gpsimd
        def _(pool):
            def add_bias(b, par, e):
                pool.wait_ge(logits_copied, b * E + e + 1)
                pool.tensor_tensor(logits[par][:, e, :], logits[par][:, e, :], rb[:, e, :], ALU.add)\
                    .then_inc(logits_biased, 1)

            def add_expert(b, e):
                pool.wait_ge(expert_scaled, b * E + e + 1)
                if e == 0:
                    pool.wait_ge(acc_loaded, (b + 1) * DMA)
                else:
                    pool.wait_ge(expert_summed, b * E + e)
                pool.tensor_tensor(acc, acc, scaled_sb, ALU.add).then_inc(expert_summed, 1)

            def count_ties(b, par, q):
                st = Steps(pool, pool_steps, (b * 4 + q) * (E - 1))
                pool.wait_ge(ties_found, b * 4 + q + 1)
                eq = logits[par][:, :, q * QW:(q + 1) * QW]
                st(pool.tensor_tensor(narrow[:, 0, :], left, eq[:, 0, :], ALU.subtract))
                for e in range(1, E):
                    st.wait()
                    ins = pool.tensor_tensor(narrow[:, e, :], narrow[:, e - 1, :], eq[:, e, :], ALU.subtract)
                    if e < E - 1:
                        st(ins)
                    else:
                        ins.then_inc(ties_counted, 1)

            pool.wait_ge(bias_loaded, 2 * DMA)
            for e in range(E):
                add_bias(0, 0, e)
            for q in range(4):
                count_ties(0, 0, q)

            def body(b, par):
                for e in range(E):
                    add_bias(b + 1, 1 - par, e)
                for e in range(4):
                    add_expert(b, e)
                count_ties(b + 1, 1 - par, 0)
                add_expert(b, 4)
                add_expert(b, 5)
                count_ties(b + 1, 1 - par, 1)
                add_expert(b, 6)
                add_expert(b, 7)
                norm_gpsimd(pool, b, norm, moments, rstd, minus_half)
                count_ties(b + 1, 1 - par, 2)
                count_ties(b + 1, 1 - par, 3)

            over_pairs(pool, body)
            for e in range(E):
                add_expert(LAST, e)
            norm_gpsimd(pool, LAST, norm, moments, rstd, minus_half)


def stage_selective_scan(nc, sem, ps, arena, const, weights, prefetch, src, dst, bc_dram):
    GROUPS, G, SPAN = 8, 2, 256
    JT, N, CH = 8, 16, 8
    UNITS = JT * N // CH
    TAPS = 4
    ident, minus_half = const["ident"], const["minus_half"]
    W_skip, W_in, Wd1, Wd2, Wbc, W_out, params, weights_loaded, region = weights

    r = Region(arena, *region[0])
    xs = [r.take(JT, SPAN) for _ in range(2)]
    dl = [r.take(JT, SPAN) for _ in range(2)]
    sk = [r.take(JT, SPAN) for _ in range(2)]
    Bb, Cb = [r.take(CH, SPAN) for _ in range(2)], [r.take(CH, SPAN) for _ in range(2)]
    r1 = Region(arena, *region[1])
    xa = [r1.take(D) for _ in range(G)]
    th = [r1.take(SPAN) for _ in range(2)]
    d1 = r1.take(SPAN)
    r2 = Region(arena, *region[2])
    decay = [r2.take(CH, SPAN) for _ in range(2)]
    state = [r2.take(CH, SPAN) for _ in range(2)]
    dx, yacc = r2.take(JT, SPAN), r2.take(JT, SPAN)
    xnT = r2.take(KC, SPAN)
    soft = r2.take(KC, SPAN)
    xp = [r2.take(G, TOK + TAPS - 1) for _ in range(2)]
    xr, out = r2.take(D), r2.take(D)
    conv_at = r2.at
    conv_w, conv_b, b_delta = r2.take(JT, TAPS), r2.take(JT), r2.take(JT)
    A, W_D, norm_w = r2.take(JT, N), r2.take(JT), r2.take(KC)
    stats, moments, rstd = r2.take(6), r2.take(3), r2.take(1)
    xstats, xmoments, xrms = r2.take(G, 6), r2.take(G, 3), r2.take(G, 1)
    bc = soft[0:2 * N, 0, :]
    soft_part = [soft[:, 0:2, :], soft[:, 2:4, :]]

    x_loaded = [sem(f"d_x{s}_loaded") for s in range(G)]
    params_loaded = sem("d_params_loaded")
    params_set = sem("d_params_set")
    resid_loaded = sem("d_resid_loaded")
    stored = sem("d_stored")
    bc_stored = sem("d_bc_stored")
    bc_written = sem("d_bc_written")
    b_spread = [sem(f"d_b{c}_spread") for c in range(2)]
    c_spread = [sem(f"d_c{c}_spread") for c in range(2)]
    xstat_steps = sem("d_xstat_steps")
    square_ready = sem("d_square_ready")
    xrms_ready = sem("d_xrms_ready")
    x_scaled = sem("d_x_scaled")
    x_turned = sem("d_x_turned")
    xnT_copied = sem("d_xnT_copied")
    in_projected = sem("d_in_projected")
    in_copied = sem("d_in_copied")
    conv_steps = sem("d_conv_steps")
    convolved = sem("d_convolved")
    x_tanh = sem("d_x_tanh")
    x_gated = sem("d_x_gated")
    skip_projected = sem("d_skip_projected")
    skip_tanh = sem("d_skip_tanh")
    skip_gated = sem("d_skip_gated")
    low_projected = sem("d_low_projected")
    low_copied = sem("d_low_copied")
    delta_projected = sem("d_delta_projected")
    delta_copied = sem("d_delta_copied")
    soft_steps = sem("d_soft_steps")
    soft_ready = sem("d_soft_ready")
    delta_ready = sem("d_delta_ready")
    dx_ready = sem("d_dx_ready")
    decays_ready = sem("d_decays_ready")
    inputs_ready = sem("d_inputs_ready")
    scanned = sem("d_scanned")
    weighed = sem("d_weighed")
    y_summed = sem("d_y_summed")
    y_added = sem("d_y_added")
    gated = sem("d_gated")
    out_projected = sem("d_out_projected")
    resid_doubled = sem("d_resid_doubled")
    resid_added = sem("d_resid_added")
    norm_steps = sem("d_norm_steps")
    norm = NormSems(sem, "d")

    Y_BANK, IN_BANK, SKIP_BANK, LOW_BANK, X_BANK, O_BANK = [0, 1], [2, 3], [4, 5], 6, [6, 7], [4, 5]

    def over_groups(eng, body):
        body(0, 0, True, True, False)
        body(1, 1, True, True, True)
        with eng.Fori(0, (GROUPS - 4) // 2) as i:
            body(i * 2 + 2, 0, True, True, True)
            body(i * 2 + 3, 1, True, True, True)
        body(6, 0, True, False, True)
        body(7, 1, False, False, True)

    with nc.Block() as block:
        @block.sync
        def _(sp):
            def load_x(g, s):
                reused(sp, x_turned, g * G - G + s + 1)
                sp.dma_start(xa[s], row(src, g * G + s)).then_inc(x_loaded[s], DMA)

            def load_resid(b):
                reused(sp, norm.out, b)
                sp.dma_start(xr, row(src, b)).then_inc(resid_loaded, DMA)

            def store(b):
                sp.wait_ge(norm.out, b + 1)
                sp.dma_start(row(dst, b), out).then_inc(stored, DMA)

            def spread_bc(g, c):
                if c == 0:
                    sp.wait_ge(low_copied, g * 2 + 2)
                    sp.dma_start(bc_dram[bass.ds(g, 1), :, :].rearrange("a n t -> (a n) t"), bc)\
                        .then_inc(bc_stored, DMA)
                    sp.wait_ge(bc_stored, (g + 1) * DMA)
                    sp.sem_inc(bc_written, 1)
                for tile, first, done, users in ((Bb[c], 0, b_spread[c], inputs_ready), (Cb[c], N, c_spread[c], weighed)):
                    reused(sp, users, g * UNITS - UNITS + (c + 1) * JT)
                    rows = bc_dram[bass.ds(g, 1), first + c * CH:first + (c + 1) * CH, :]
                    sp.dma_start(tile.rearrange("p n t -> p (n t)"),
                                 rows.rearrange("a n t -> (a n t)").partition_broadcast(P)).then_inc(done, DMA)

            sp.dma_start(xa[0], row(src, 0)).then_inc(x_loaded[0], DMA)
            sp.dma_start(xa[1], row(src, 1)).then_inc(x_loaded[1], DMA)
            for tile, name in ((conv_w, "conv_w"), (conv_b, "conv_b"), (b_delta, "b_delta"), (A, "A_log"),
                               (W_D, "W_D"), (norm_w, "norm_w")):
                sp.dma_start(tile, params[name]).then_inc(params_loaded, DMA)
            load_x(1, 0)
            load_x(1, 1)
            spread_bc(0, 0)
            spread_bc(0, 1)

            def body(g, par, next, next2, prev):
                if prev:
                    load_resid(g * G - G)
                if next2:
                    load_x(g + 2, 0)
                    load_x(g + 2, 1)
                if prev:
                    load_resid(g * G - G + 1)
                    store(g * G - G)
                if next:
                    spread_bc(g + 1, 0)
                if prev:
                    store(g * G - G + 1)
                if next:
                    spread_bc(g + 1, 1)

            body(0, 0, True, True, False)
            body(1, 1, True, True, True)
            with sp.Fori(0, (GROUPS - 4) // 2) as i:
                body(i * 2 + 2, 0, True, True, True)
                body(i * 2 + 3, 1, True, True, True)
            body(6, 0, True, False, True)
            sp.wait_ge(skip_projected, GROUPS * JT)
            prefetch[0](sp)
            body(7, 1, False, False, True)
            sp.wait_ge(weighed, GROUPS * UNITS)
            sp.wait_ge(y_added, GROUPS * UNITS - JT)
            prefetch[1](sp)
            load_resid(SEQS - 2)
            load_resid(SEQS - 1)
            store(SEQS - 2)
            store(SEQS - 1)
            sp.wait_ge(stored, SEQS * DMA)

        @block.tensor
        def _(pe):
            def turn_x(g):
                for s in range(G):
                    pe.wait_ge(x_scaled, g * G + s + 1)
                    reused(pe, xnT_copied, g * G)
                    reused(pe, low_copied, g * 2)
                    turn(pe, ps[:, X_BANK[s], :], halves(xa[s]), ident).then_inc(x_turned, 1)

            def project_in(g, j):
                pe.wait_ge(xnT_copied, g * G + G)
                if j < 2:
                    reused(pe, delta_copied, g * JT)
                else:
                    pe.wait_ge(in_copied, g * JT + j - 1)
                project(pe, ps[:, IN_BANK[j % 2], 0:SPAN], lambda k: W_in[:, k, j * P:(j + 1) * P],
                        lambda k: xnT[:, k, :], KC).then_inc(in_projected, 1)

            def project_skip(g, j):
                reused(pe, skip_gated, g * JT + j - 1)
                if j < 2:
                    reused(pe, resid_added, (g - 2) * G + j + 1)
                project(pe, ps[:, SKIP_BANK[j % 2], 0:SPAN], lambda k: W_skip[:, k, j * P:(j + 1) * P],
                        lambda k: xnT[:, k, :], KC).then_inc(skip_projected, 1)

            def project_low(g, par):
                pe.wait_ge(x_gated, g * JT + JT)
                pe.wait_ge(xnT_copied, g * G + G)
                project(pe, ps[:, LOW_BANK, 0:SPAN], lambda k: Wd1[:, k, :], lambda k: xs[par][:, k, :], JT)\
                    .then_inc(low_projected, 1)

            def project_bc(g, par):
                project(pe, ps[0:2 * N, LOW_BANK, SPAN:2 * SPAN], lambda k: Wbc[:, k, :],
                        lambda k: xs[par][:, k, :], JT).then_inc(low_projected, 1)

            def project_delta(g, k):
                pe.wait_ge(low_copied, g * 2 + 1)
                pe.wait_ge(in_copied, g * JT + JT)
                if k >= 2:
                    pe.wait_ge(delta_copied, g * JT + 2 * k - 2)
                for i in range(2):
                    j = 2 * k + i
                    pe.matmul(ps[:, IN_BANK[k % 2], i * SPAN:(i + 1) * SPAN], Wd2[:, j * P:(j + 1) * P], d1,
                              start=True, stop=True).then_inc(delta_projected, 1)

            def sum_states(g, u):
                pe.wait_ge(weighed, g * UNITS + u + 1)
                reused(pe, y_added, g * UNITS + u - 1)
                project(pe, ps[:, Y_BANK[u % 2], 0:SPAN], lambda n: ident, lambda n: state[u % 2][:, n, :], CH)\
                    .then_inc(y_summed, 1)

            def project_out(g, s, par, groups_ahead, half):
                if half == 0:
                    pe.wait_ge(gated, g * JT + JT)
                    pe.wait_ge(skip_gated, (g + groups_ahead + 1) * JT)
                for k in range(half * JT // 2, (half + 1) * JT // 2):
                    last = pe.matmul(ps[:, O_BANK[s], :], sk[par][:, k, s * TOK:(s + 1) * TOK], W_out[:, k, :],
                                     start=(k == 0), stop=(k == JT - 1))
                if half:
                    last.then_inc(out_projected, 1)

            pe.wait_ge(weights_loaded, 7 * DMA)
            turn_x(0)
            for j in range(JT):
                project_in(0, j)
            for j in range(JT):
                project_skip(0, j)
            project_low(0, 0)
            project_bc(0, 0)
            for k in range(4):
                project_delta(0, k)
            turn_x(1)

            def body(g, par, next, next2, prev):
                for u in range(UNITS):
                    if next and u < 4:
                        project_in(g + 1, 2 * u)
                        project_in(g + 1, 2 * u + 1)
                    if prev and u in (4, 5):
                        project_out(g - 1, 0, 1 - par, 1, u - 4)
                    if next and u == 6:
                        project_low(g + 1, 1 - par)
                    if next and u == 7:
                        project_bc(g + 1, 1 - par)
                    if prev and u in (8, 9):
                        project_out(g - 1, 1, 1 - par, 1, u - 8)
                    if next and 8 <= u < 12:
                        project_delta(g + 1, u - 8)
                    if next and 10 <= u < 14:
                        project_skip(g + 1, 2 * u - 20)
                        project_skip(g + 1, 2 * u - 19)
                    if next2 and u == 14:
                        turn_x(g + 2)
                    sum_states(g, u)

            over_groups(pe, body)
            pe.wait_ge(resid_added, (GROUPS - 1) * G)
            for s in range(G):
                project_out(GROUPS - 1, s, 1, 0, 0)
                project_out(GROUPS - 1, s, 1, 0, 1)

        @block.scalar
        def _(act):
            def copy_xnT(g):
                for s in range(G):
                    act.wait_ge(x_turned, g * G + s + 1)
                    reused(act, skip_projected, g * JT)
                    for k in range(KC):
                        last = act.activation(xnT[:, k, s * TOK:(s + 1) * TOK], ps[:, X_BANK[s], k * P:(k + 1) * P],
                                              ACT.Copy, scale=norm_w[:, k:k + 1])
                    last.then_inc(xnT_copied, 1)

            def copy_in(g, j):
                act.wait_ge(in_projected, g * JT + j + 1)
                reused(act, convolved, g * JT + j - 1)
                act.activation(xp[j % 2][:, :, TAPS - 1:], ps[:, IN_BANK[j % 2], 0:SPAN]
                               .rearrange("p (s t) -> p s t", s=G), ACT.Copy).then_inc(in_copied, 1)

            def tanh_x(g, par, j):
                act.wait_ge(convolved, g * JT + j + 1)
                reused(act, x_gated, g * JT + j - 1)
                act.activation(th[j % 2], xs[par][:, j, :], ACT.Tanh).then_inc(x_tanh, 1)

            def tanh_skip(g, par, j):
                act.wait_ge(skip_projected, g * JT + j + 1)
                reused(act, out_projected, (g - 1) * G)
                act.activation(sk[par][:, j, :], ps[:, SKIP_BANK[j % 2], 0:SPAN], ACT.Tanh, scale=0.5)\
                    .then_inc(skip_tanh, 1)

            def copy_low(g):
                act.wait_ge(low_projected, g * 2 + 2)
                reused(act, delta_projected, g * JT)
                act.activation(d1, ps[:, LOW_BANK, 0:SPAN], ACT.Copy).then_inc(low_copied, 1)
                reused(act, delta_ready, g * 4)
                reused(act, bc_stored, g * DMA)
                act.activation(bc, ps[0:2 * N, LOW_BANK, SPAN:2 * SPAN], ACT.Copy).then_inc(low_copied, 1)

            def copy_delta(g, par, k):
                for j in (2 * k, 2 * k + 1):
                    act.wait_ge(delta_projected, g * JT + 2 * k + 2)
                    reused(act, dx_ready, (g - 1) * JT)
                    reused(act, decays_ready, (g - 1) * UNITS)
                    act.activation(dl[par][:, j, :], ps[:, IN_BANK[k % 2], (j % 2) * SPAN:(j % 2 + 1) * SPAN],
                                   ACT.Identity, bias=b_delta[:, j:j + 1]).then_inc(delta_copied, 1)

            def soft_log(g, par, k):
                st = Steps(act, soft_steps, g * 8 + k * 2)
                act.wait_ge(delta_copied, g * JT + 2 * k + 2)
                if k == 0:
                    act.wait_ge(bc_stored, (g + 1) * DMA)
                reused(act, delta_ready, g * 4 + k - 1)
                part = soft_part[k % 2]
                st(act.activation(part, dl[par][:, 2 * k:2 * k + 2, :], ACT.Abs))
                st.wait()
                st(act.activation(part, part, ACT.Exp, scale=-1.0))
                st.wait()
                act.activation(part, part, ACT.Ln, bias=1.0).then_inc(soft_ready, 1)

            def decays(g, par, u):
                j, c = u % JT, u // JT
                if u == 0:
                    act.wait_ge(delta_ready, g * 4 + 4)
                reused(act, scanned, g * UNITS + u - 1)
                for n in range(CH):
                    last = act.activation(
                        decay[u % 2][:, n, :].rearrange("p (s t) -> p s t", s=G)[:, :, 1:],
                        dl[par][:, j, :].rearrange("p (s t) -> p s t", s=G)[:, :, 1:], ACT.Exp,
                        scale=A[:, j, c * CH + n:c * CH + n + 1])
                last.then_inc(decays_ready, 1)

            act.wait_ge(params_loaded, 6 * DMA)
            act.activation(A, A, ACT.Exp).then_inc(params_set, 1)
            copy_xnT(0)
            for k in range(4):
                copy_in(0, 2 * k)
                copy_in(0, 2 * k + 1)
                if k:
                    tanh_x(0, 0, 2 * k - 2)
                    tanh_x(0, 0, 2 * k - 1)
            tanh_x(0, 0, 6)
            tanh_x(0, 0, 7)
            for j in range(JT):
                tanh_skip(0, 0, j)
            copy_low(0)
            for k in range(4):
                copy_delta(0, 0, k)
            for k in range(4):
                soft_log(0, 0, k)
            copy_xnT(1)
            act.wait_ge(params_set, 7)
            decays(0, 0, 0)

            def body(g, par, next, next2, prev):
                for u in range(UNITS):
                    if u < UNITS - 1:
                        decays(g, par, u + 1)
                    elif next:
                        decays(g + 1, 1 - par, 0)
                    if next:
                        if u < 4:
                            copy_in(g + 1, 2 * u)
                            copy_in(g + 1, 2 * u + 1)
                        if 1 <= u < 5:
                            tanh_x(g + 1, 1 - par, 2 * u - 2)
                            tanh_x(g + 1, 1 - par, 2 * u - 1)
                        if u == 7:
                            copy_low(g + 1)
                        if 8 <= u < 12:
                            copy_delta(g + 1, 1 - par, u - 8)
                        if 9 <= u < 13:
                            soft_log(g + 1, 1 - par, u - 9)
                        if 10 <= u < 14:
                            tanh_skip(g + 1, 1 - par, 2 * u - 20)
                            tanh_skip(g + 1, 1 - par, 2 * u - 19)
                    if next2 and u == 14:
                        copy_xnT(g + 2)

            over_groups(act, body)

        @block.vector
        def _(dve):
            def x_moments(g):
                for s in range(G):
                    b = g * G + s
                    st = Steps(dve, xstat_steps, b * 3)
                    dve.wait_ge(x_loaded[s], (g + 1) * DMA)
                    st(dve.bn_stats(xstats[:, s, :], xa[s]))
                    st.wait()
                    dve.memset(xmoments[:, s, 2:3], 0.0)
                    st(dve.bn_aggr(xmoments[:, s, 0:2], xstats[:, s, :]))
                    st.wait()
                    st(dve.scalar_tensor_tensor(xmoments[:, s, 0:1], xmoments[:, s, 0:1], xmoments[:, s, 0:1],
                                                xmoments[:, s, 1:2], ALU.mult, ALU.add))
                    st.wait()
                    dve.tensor_scalar(xmoments[:, s, 0:1], xmoments[:, s, 0:1], EPS, None, ALU.add)\
                        .then_inc(square_ready, 1)

            def scale_x(g):
                for s in range(G):
                    b = g * G + s
                    dve.wait_ge(xrms_ready, b + 1)
                    dve.tensor_scalar(xa[s], xa[s], xrms[:, s, :], None, ALU.mult).then_inc(x_scaled, 1)

            def convolve(g, par, k):
                for i in range(TAPS):
                    for j in (2 * k, 2 * k + 1):
                        tile = xs[par][:, j, :].rearrange("p (s t) -> p s t", s=G)
                        taps = xp[j % 2][:, :, i:i + TOK]
                        if i == 0:
                            dve.wait_ge(in_copied, g * JT + j + 1)
                            reused(dve, dx_ready, (g - 1) * JT)
                            reused(dve, y_added, (g - 1) * UNITS)
                            ins = dve.tensor_scalar(tile, taps, conv_w[:, j, 0:1], conv_b[:, j:j + 1],
                                                    ALU.mult, ALU.add)
                        else:
                            dve.wait_ge(conv_steps, g * 24 + k * 6 + (i - 1) * 2 + j % 2 + 1)
                            ins = dve.scalar_tensor_tensor(tile, taps, conv_w[:, j, i:i + 1], tile,
                                                           ALU.mult, ALU.add)
                        ins.then_inc(convolved if i == TAPS - 1 else conv_steps, 1)

            def gate_x(g, par, k):
                for j in (2 * k, 2 * k + 1):
                    dve.wait_ge(x_tanh, g * JT + j + 1)
                    dve.scalar_tensor_tensor(xs[par][:, j, :], th[j % 2], 1.0, xs[par][:, j, :], ALU.add, ALU.mult)\
                        .then_inc(x_gated, 1)

            def gate_skip(g, par, j):
                dve.wait_ge(skip_tanh, g * JT + j + 1)
                dve.scalar_tensor_tensor(sk[par][:, j, :], sk[par][:, j, :], 1.0,
                                         ps[:, SKIP_BANK[j % 2], 0:SPAN], ALU.add, ALU.mult).then_inc(skip_gated, 1)

            def softplus(g, par, k):
                dve.wait_ge(soft_ready, g * 4 + k + 1)
                part = dl[par][:, 2 * k:2 * k + 2, :]
                dve.scalar_tensor_tensor(part, part, 0.0, soft_part[k % 2], ALU.max, ALU.add).then_inc(delta_ready, 1)

            def scan(g, u):
                c = u // JT
                dve.wait_ge(decays_ready, g * UNITS + u + 1)
                dve.wait_ge(inputs_ready, g * UNITS + u + 1)
                flat = state[u % 2].rearrange("p n t -> p (n t)")
                dve.tensor_tensor_scan(flat, decay[u % 2].rearrange("p n t -> p (n t)"), flat, 0.0,
                                       ALU.mult, ALU.add).then_inc(scanned, 1)
                dve.wait_ge(scanned, g * UNITS + u + 1)
                if u % JT == 0:
                    dve.wait_ge(c_spread[c], (g + 1) * DMA)
                dve.tensor_tensor(state[u % 2], state[u % 2], Cb[c], ALU.mult).then_inc(weighed, 1)

            def add_y(g, par, u):
                j = u % JT
                dve.wait_ge(y_summed, g * UNITS + u + 1)
                if u < JT:
                    reused(dve, gated, g * JT - JT + j + 1)
                    ins = dve.scalar_tensor_tensor(yacc[:, j, :], xs[par][:, j, :], W_D[:, j:j + 1],
                                                   ps[:, Y_BANK[u % 2], 0:SPAN], ALU.mult, ALU.add)
                else:
                    dve.wait_ge(y_added, g * UNITS + u - JT + 1)
                    ins = dve.tensor_tensor(yacc[:, j, :], yacc[:, j, :], ps[:, Y_BANK[u % 2], 0:SPAN], ALU.add)
                ins.then_inc(y_added, 1)

            def normalise(b, s):
                st = Steps(dve, norm_steps, b * 2)
                dve.wait_ge(out_projected, b + 1)
                dve.wait_ge(resid_doubled, b + 1)
                dve.scalar_tensor_tensor(xr, ps[:, O_BANK[s], :], 0.5, xr, ALU.mult, ALU.add)\
                    .then_inc(resid_added, 1)
                dve.wait_ge(resid_added, b + 1)
                norm_moments(dve, norm, st, xr, stats, moments)

            def finish_norm(b):
                norm_apply(dve, b, norm, xr, moments, rstd, out, stored)

            for k in range(2):
                dve.memset(xp[k][:, :, 0:TAPS - 1], 0.0).then_inc(params_set, 1)
                dve.memset(decay[k].rearrange("p n (s t) -> p (n s) t", s=G)[:, :, 0:1], 0.0).then_inc(params_set, 1)
            x_moments(0)
            dve.wait_ge(params_loaded, 6 * DMA)
            pair = arena[:, conv_at:conv_at + JT * TAPS + JT]
            dve.tensor_scalar(pair, pair, 0.5, None, ALU.mult).then_inc(params_set, 1)
            dve.wait_ge(params_set, 6)
            dve.tensor_scalar(A, A, -1.0, None, ALU.mult).then_inc(params_set, 1)
            dve.wait_ge(params_set, 7)
            scale_x(0)
            for k in range(4):
                convolve(0, 0, k)
                if k:
                    gate_x(0, 0, k - 1)
            gate_x(0, 0, 3)
            x_moments(1)
            for j in range(JT):
                gate_skip(0, 0, j)
            scale_x(1)
            for k in range(4):
                softplus(0, 0, k)

            def body(g, par, next, next2, prev):
                for u in range(UNITS):
                    scan(g, u)
                    if u:
                        add_y(g, par, u - 1)
                    if next:
                        if u < 4:
                            convolve(g + 1, 1 - par, u)
                        if 1 <= u < 5:
                            gate_x(g + 1, 1 - par, u - 1)
                        if 10 <= u < 14:
                            softplus(g + 1, 1 - par, u - 10)
                            gate_skip(g + 1, 1 - par, 2 * u - 20)
                            gate_skip(g + 1, 1 - par, 2 * u - 19)
                    if prev and u in (5, 9):
                        normalise((g - 1) * G + (u - 5) // 4, (u - 5) // 4)
                    if prev and u in (6, 10):
                        finish_norm((g - 1) * G + (u - 6) // 4)
                    if next2 and u == 7:
                        x_moments(g + 2)
                    if next2 and u == 8:
                        scale_x(g + 2)
                add_y(g, par, UNITS - 1)

            over_groups(dve, body)
            for s in range(G):
                normalise(SEQS - G + s, s)
                finish_norm(SEQS - G + s)

        @block.gpsimd
        def _(pool):
            def x_power(g):
                for s in range(G):
                    pool.wait_ge(square_ready, g * G + s + 1)
                    pool.tensor_tensor(xrms[:, s, :], xmoments[:, s, 0:1], minus_half, ALU.pow)\
                        .then_inc(xrms_ready, 1)

            def make_inputs(g, par, u):
                j, c = u % JT, u // JT
                if u == 0:
                    pool.wait_ge(delta_ready, g * 4 + 4)
                if u < JT:
                    reused(pool, inputs_ready, g * UNITS - JT + j + 1)
                    pool.tensor_tensor(dx[:, j, :], dl[par][:, j, :], xs[par][:, j, :], ALU.mult)\
                        .then_inc(dx_ready, 1)
                    pool.wait_ge(dx_ready, g * JT + j + 1)
                if u % JT == 0:
                    pool.wait_ge(b_spread[c], (g + 1) * DMA)
                reused(pool, y_summed, g * UNITS + u - 1)
                pool.tensor_tensor(state[u % 2], spread(dx[:, j, :], 1, CH), Bb[c], ALU.mult)\
                    .then_inc(inputs_ready, 1)

            def gate_y(g, par, j):
                pool.wait_ge(y_added, g * UNITS + JT + j + 1)
                pool.tensor_tensor(sk[par][:, j, :], sk[par][:, j, :], yacc[:, j, :], ALU.mult).then_inc(gated, 1)

            def double_resid(b):
                pool.wait_ge(resid_loaded, (b + 1) * DMA)
                pool.tensor_tensor(xr, xr, xr, ALU.add).then_inc(resid_doubled, 1)

            x_power(0)
            x_power(1)
            make_inputs(0, 0, 0)

            def body(g, par, next, next2, prev):
                for u in range(UNITS):
                    if u < UNITS - 1:
                        make_inputs(g, par, u + 1)
                    elif next:
                        make_inputs(g + 1, 1 - par, 0)
                    if next2 and u == 7:
                        x_power(g + 2)
                    if u >= JT + 2:
                        gate_y(g, par, u - JT - 2)
                    if prev and u in (3, 8):
                        double_resid((g - 1) * G + (u - 3) // 5)
                    if prev and u in (5, 9):
                        norm_gpsimd(pool, (g - 1) * G + (u - 5) // 4, norm, moments, rstd, minus_half)
                gate_y(g, par, JT - 2)
                gate_y(g, par, JT - 1)

            over_groups(pool, body)
            for s in range(G):
                double_resid(SEQS - G + s)
                norm_gpsimd(pool, SEQS - G + s, norm, moments, rstd, minus_half)


def stage_normed_attention(nc, sem, ps, arena, const, weights, prefetch, src, ctx, dst):
    H, HD, CC = 16, 128, 2
    NB = H // 4
    WIDE = H * HD
    SCALE = HD ** -0.5
    ident, minus_half = const["ident"], const["minus_half"]
    Wq, Wk, Wv, Wo, first_loaded, rest_loaded, given, regions = weights

    r0, r1, r = (Region(arena, *span) for span in regions)
    q, k = r0.take(NB, D), r0.take(NB, D)
    V, qT, kT, prob = r1.take(WIDE), r1.take(H, P), r1.take(H, P), r1.take(H, P)
    probT, yT = r.take(2, D), r.take(H, P)
    squares = r.take(2, D)
    xa, ca, xr, out = r.take(D), r.take(CC * P), r.take(D), r.take(D)
    xT, cT, fT = r.take(KC, P), r.take(CC, P), r.take(KC, P)
    W, fbias, fz, fout = r.take(KC, D), r.take(D), r.take(D), r.take(D)
    gq, gk, ones = r.take(1), r.take(1), r.take(P)
    ssq = r.take(2, H)
    scale_q, scale_k = ssq[:, 0, :], ssq[:, 1, :]
    power = r.take(H)
    top, shift, total, rtotal = r.take(H), r.take(H), r.take(H), r.take(H)
    rms_raw = r.take(2, H)
    stats, moments, rstd = r.take(6), r.take(3), r.take(1)
    fstats, fmoments, frstd = r.take(6), r.take(3), r.take(1)
    wsum, wscale, wden = r.take(1), r.take(1), r.take(1)
    ternary = prob.rearrange("p a b -> p (a b)")

    x_loaded = sem("e_x_loaded")
    given_loaded = sem("e_given_loaded")
    consts_set = sem("e_consts_set")
    resid_loaded = sem("e_resid_loaded")
    stored = sem("e_stored")
    w_steps = sem("e_w_steps")
    w_summed = sem("e_w_summed")
    w_total = sem("e_w_total")
    w_ready = sem("e_w_ready")
    x_turned = sem("e_x_turned")
    xT_copied = sem("e_xT_copied")
    projected = sem("e_projected")
    proj_copied = sem("e_proj_copied")
    squared = sem("e_squared")
    squares_summed = sem("e_squares_summed")
    rms_steps = sem("e_rms_steps")
    rms_ready = sem("e_rms_ready")
    rms_powered = sem("e_rms_powered")
    scale_ready = sem("e_scale_ready")
    k_normed = sem("e_k_normed")
    q_turned = sem("e_q_turned")
    k_turned = sem("e_k_turned")
    qT_copied = sem("e_qT_copied")
    kT_copied = sem("e_kT_copied")
    scored = sem("e_scored")
    top_found = sem("e_top_found")
    shift_ready = sem("e_shift_ready")
    exp_done = sem("e_exp_done")
    total_inverted = sem("e_total_inverted")
    prob_normed = sem("e_prob_normed")
    prob_turned = sem("e_prob_turned")
    probT_copied = sem("e_probT_copied")
    mixed = sem("e_mixed")
    yT_copied = sem("e_yT_copied")
    out_projected = sem("e_out_projected")
    resid_added = sem("e_resid_added")
    dve_steps = sem("e_dve_steps")
    norm = NormSems(sem, "e")
    f_turned = sem("f_turned")
    fT_copied = sem("f_T_copied")
    f_biased = sem("f_biased")
    f_projected = sem("f_projected")
    f_added = sem("f_added")
    f_steps = sem("f_steps")
    fnorm = NormSems(sem, "f")
    LAST = SEQS - 1
    X_BANK, C_BANK, O_BANK, FT_BANK, F_BANK = 7, 6, 7, 7, 6
    Q_BANK, K_BANK = (0, 2), (1, 3)

    with nc.Block() as block:
        @block.sync
        def _(sp):
            def load_x(b):
                sp.dma_start(xa, row(src, b)).then_inc(x_loaded, DMA)
                sp.dma_start(ca, row(ctx, b)).then_inc(x_loaded, DMA)

            load_x(0)
            for tile, dram in ((W, given["weight"].rearrange("(k p) n -> p k n", p=P)),
                               (fbias, given["bias"].partition_broadcast(P)), (gq, given["gq"]), (gk, given["gk"])):
                sp.dma_start(tile, dram).then_inc(given_loaded, DMA)
            sp.wait_ge(x_turned, 2)
            load_x(1)

            def body(b, ahead, behind=True):
                reused(sp, norm.out, b)
                sp.dma_start(xr, row(src, b)).then_inc(resid_loaded, DMA)
                if behind:
                    sp.wait_ge(fnorm.out, b)
                    sp.dma_start(row(dst, b - 1), fout).then_inc(stored, DMA)
                if ahead:
                    sp.wait_ge(x_turned, 2 * b + 4)
                    load_x(b + 2)

            body(0, True, False)
            with sp.Fori(1, SEQS - 2) as b:
                body(b, True)
            body(SEQS - 2, False)
            body(LAST, False)
            sp.wait_ge(fnorm.out, SEQS)
            sp.dma_start(row(dst, LAST), fout).then_inc(stored, DMA)
            sp.wait_ge(stored, SEQS * DMA)

        @block.tensor
        def _(pe):
            def turn_x(b, first=False):
                pe.wait_ge(x_loaded, 2 * (b + 1) * DMA)
                if not first:
                    reused(pe, fT_copied, b - 1)
                turn(pe, ps[:, X_BANK, :], halves(xa), ident).then_inc(x_turned, 1)
                if not first:
                    reused(pe, f_added, b - 1)
                turn(pe, ps[:, C_BANK, :], halves(ca, CC), ident).then_inc(x_turned, 1)

            def proj(b, c):
                pe.wait_ge(xT_copied, 2 * b + (1 if c < NB else 2))
                reused(pe, proj_copied, 12 * b + c - 1)
                lhs, w, n = ((xT, Wq, KC), (cT, Wk, CC), (cT, Wv, CC))[c // NB]
                cols = slice(c % NB * D, (c % NB + 1) * D)
                project(pe, ps[:, 4 + c % 2, :], lambda i: lhs[:, i, :], lambda i: w[:, i, cols], n)\
                    .then_inc(projected, 1)

            def turn_qk(b):
                for c in range(NB):
                    if c == 0:
                        reused(pe, probT_copied, b * NB)
                        pe.wait_ge(proj_copied, 12 * b + NB)
                    elif c == 1:
                        reused(pe, yT_copied, b * NB)
                    else:
                        pe.wait_ge(qT_copied, b * NB + c - 1)
                    turn(pe, ps[:, Q_BANK[c % 2], :], halves(q[:, c, :]), ident).then_inc(q_turned, 1)
                    pe.wait_ge(k_normed, b * NB + c + 1)
                    if c >= 2:
                        pe.wait_ge(kT_copied, b * NB + c - 1)
                    turn(pe, ps[:, K_BANK[c % 2], :], halves(k[:, c, :]), ident).then_inc(k_turned, 1)

            def scores(b):
                pe.wait_ge(qT_copied, b * NB + NB)
                pe.wait_ge(kT_copied, b * NB + NB)
                for c in range(NB):
                    for h in range(4 * c, 4 * c + 4):
                        last = pe.matmul(ps[:, c, (h % 4) * P:(h % 4 + 1) * P], qT[:, h, :], kT[:, h, :],
                                         start=True, stop=True)
                    last.then_inc(scored, 1)

            def turn_prob(b, c):
                pe.wait_ge(prob_normed, b * NB + c + 1)
                if c >= 2:
                    pe.wait_ge(probT_copied, b * NB + c - 1)
                turn(pe, ps[:, c % 2, :], [prob[:, h, :] for h in range(4 * c, 4 * c + 4)], ident)\
                    .then_inc(prob_turned, 1)

            def mix(b, c):
                pe.wait_ge(probT_copied, b * NB + c + 1)
                if c < 2:
                    pe.wait_ge(proj_copied, 12 * b + 12)
                    pe.wait_ge(exp_done, b * NB + 3 + c)
                else:
                    pe.wait_ge(yT_copied, b * NB + c - 1)
                for h in range(4 * c, 4 * c + 4):
                    last = pe.matmul(ps[:, 2 + c % 2, (h % 4) * P:(h % 4 + 1) * P], V[:, h * P:(h + 1) * P],
                                     probT[:, c % 2, (h % 4) * P:(h % 4 + 1) * P], start=True, stop=True)
                last.then_inc(mixed, 1)

            def attend(b):
                turn_prob(b, 0)
                for c in range(NB):
                    if c + 1 < NB:
                        turn_prob(b, c + 1)
                    mix(b, c)

            def out_proj(b, last=False):
                pe.wait_ge(yT_copied, b * NB + NB)
                pe.wait_ge(xT_copied, 2 * b + (1 if last else 3))
                reused(pe, fT_copied, b)
                project(pe, ps[:, O_BANK, :], lambda i: yT[:, i, :], lambda i: Wo[:, i, :], H)\
                    .then_inc(out_projected, 1)

            def turn_f(b):
                pe.wait_ge(norm.out, b + 1)
                turn(pe, ps[:, FT_BANK, :], halves(out), ident).then_inc(f_turned, 1)

            def proj_f(b, last=False):
                pe.wait_ge(fT_copied, b + 1)
                pe.wait_ge(xT_copied, 2 * b + (2 if last else 4))
                project(pe, ps[:, F_BANK, :], lambda i: fT[:, i, :], lambda i: W[:, i, :], KC)\
                    .then_inc(f_projected, 1)

            pe.wait_ge(consts_set, 1)
            pe.wait_ge(w_summed, 1)
            pe.matmul(ps[:, 0, 0:1], ones, wsum, start=True, stop=True).then_inc(w_total, 1)
            turn_x(0, first=True)
            pe.wait_ge(first_loaded, 2 * DMA)
            pe.wait_ge(rest_loaded, 2 * DMA)
            for c in range(12):
                proj(0, c)
            pe.wait_ge(w_ready, 1)

            def body(b, first=False):
                turn_qk(b)
                if not first:
                    turn_f(b - 1)
                scores(b)
                if not first:
                    proj_f(b - 1)
                turn_x(b + 1)
                for c in range(2 * NB):
                    proj(b + 1, c)
                attend(b)
                for c in range(2 * NB, 3 * NB):
                    proj(b + 1, c)
                out_proj(b)

            body(0, True)
            with pe.Fori(1, LAST) as b:
                body(b)
            turn_qk(LAST)
            turn_f(LAST - 1)
            scores(LAST)
            proj_f(LAST - 1)
            attend(LAST)
            out_proj(LAST, last=True)
            turn_f(LAST)
            proj_f(LAST, last=True)

        @block.scalar
        def _(act):
            def copy_xT(b):
                act.wait_ge(x_turned, 2 * b + 1)
                reused(act, projected, 12 * b)
                act.activation(xT, ps[:, X_BANK, :].rearrange("p (a b) -> p a b", a=KC), ACT.Copy)\
                    .then_inc(xT_copied, 1)
                act.wait_ge(x_turned, 2 * b + 2)
                act.activation(cT, ps[:, C_BANK, 0:CC * P].rearrange("p (a b) -> p a b", a=CC), ACT.Copy)\
                    .then_inc(xT_copied, 1)

            def copy_proj(b, c):
                act.wait_ge(projected, 12 * b + c + 1)
                if c < NB:
                    reused(act, q_turned, b * NB)
                    reused(act, squared, 8 * b)
                    dest = q[:, c, :]
                elif c < 2 * NB:
                    reused(act, k_turned, b * NB)
                    dest = k[:, c - NB, :]
                else:
                    reused(act, mixed, b * NB)
                    dest = V[:, (c - 2 * NB) * D:(c - 2 * NB + 1) * D]
                act.activation(dest, ps[:, 4 + c % 2, :], ACT.Copy).then_inc(proj_copied, 1)

            def copy_qT(b, c):
                act.wait_ge(q_turned, b * NB + c + 1)
                reused(act, scored, b * NB)
                act.activation(qT[:, 4 * c:4 * c + 4, :], ps[:, Q_BANK[c % 2], :].rearrange("p (a b) -> p a b", a=4), ACT.Copy,
                               scale=gq).then_inc(qT_copied, 1)

            def exps(b, c):
                act.wait_ge(shift_ready, b * NB + c + 1)
                reused(act, prob_turned, (b - 1) * NB + c + 1)
                reused(act, total_inverted, (b - 1) * NB + c + 1)
                for h in range(4 * c, 4 * c + 4):
                    last = act.activation(prob[:, h, :], ps[:, c, (h % 4) * P:(h % 4 + 1) * P], ACT.Exp,
                                          bias=shift[:, h:h + 1], scale=scale_q[:, h:h + 1],
                                          accum_out=total[:, h:h + 1])
                last.then_inc(exp_done, 1)

            def copy_fT(b):
                act.wait_ge(f_turned, b + 1)
                reused(act, f_projected, b)
                act.activation(fT, ps[:, FT_BANK, :].rearrange("p (a b) -> p a b", a=KC), ACT.Copy)\
                    .then_inc(fT_copied, 1)

            act.wait_ge(given_loaded, 4 * DMA)
            act.activation(ternary, W.rearrange("p a b -> p (a b)"), ACT.Abs, accum_out=wsum).then_inc(w_summed, 1)
            copy_xT(0)
            for c in range(12):
                copy_proj(0, c)

            def body(b, first=False):
                for c in range(NB):
                    copy_qT(b, c)
                if not first:
                    copy_fT(b - 1)
                copy_xT(b + 1)
                for c in range(NB):
                    exps(b, c)
                    copy_proj(b + 1, c)
                for c in range(NB, 3 * NB):
                    copy_proj(b + 1, c)

            body(0, True)
            with act.Fori(1, LAST) as b:
                body(b)
            for c in range(NB):
                copy_qT(LAST, c)
            copy_fT(LAST - 1)
            for c in range(NB):
                exps(LAST, c)
            copy_fT(LAST)

        @block.vector
        def _(dve):
            def make_ternary():
                MAGIC = 12582912.0
                w = W.rearrange("p a b -> p (a b)")
                st = Steps(dve, w_steps, 0)
                dve.wait_ge(w_total, 1)
                st(dve.tensor_scalar(wscale, ps[:, 0, 0:1], 1.0 / (D * D), None, ALU.mult))
                st.wait()
                st(dve.tensor_scalar(wden, wscale, 1e-10, None, ALU.add))
                st.wait()
                st(dve.reciprocal(wden, wden))
                st.wait()
                st(dve.tensor_scalar(ternary, w, wden, 1.0, ALU.mult, ALU.min))
                st.wait()
                st(dve.tensor_scalar(ternary, ternary, -1.0, MAGIC, ALU.max, ALU.add))
                st.wait()
                st(dve.tensor_scalar(ternary, ternary, -MAGIC, None, ALU.add))
                st.wait()
                st(dve.scalar_tensor_tensor(ternary, ternary, wscale, w, ALU.mult, ALU.subtract))
                st.wait()
                dve.tensor_tensor(w, w, ternary, ALU.add).then_inc(w_ready, 1)

            def copy_kT(b, c):
                dve.wait_ge(k_turned, b * NB + c + 1)
                if c == 0:
                    reused(dve, scored, b * NB)
                dve.tensor_scalar(kT[:, 4 * c:4 * c + 4, :], ps[:, K_BANK[c % 2], :].rearrange("p (a b) -> p a b", a=4),
                                  gk, None, ALU.mult).then_inc(kT_copied, 1)

            def find_shift(b, c):
                heads = slice(4 * c, 4 * c + 4)
                dve.wait_ge(scored, b * NB + c + 1)
                if c == 0:
                    dve.wait_ge(scale_ready, b * 2 + 2)
                dve.tensor_reduce(top[:, heads], ps[:, c, :].rearrange("p (h k) -> p h k", h=4), AX.X, ALU.max)\
                    .then_inc(top_found, 1)
                dve.wait_ge(top_found, b * NB + c + 1)
                reused(dve, exp_done, (b - 1) * NB + c + 1)
                dve.scalar_tensor_tensor(shift[:, heads], top[:, heads], -1.0, scale_q[:, heads], ALU.mult, ALU.mult)\
                    .then_inc(shift_ready, 1)

            def invert_total(b, c):
                heads = slice(4 * c, 4 * c + 4)
                dve.wait_ge(exp_done, b * NB + c + 1)
                reused(dve, prob_normed, (b - 1) * NB + c + 1)
                dve.reciprocal(rtotal[:, heads], total[:, heads]).then_inc(total_inverted, 1)

            def sum_squares(b, which, c):
                n = NB * which + c
                dve.wait_ge(squared, 8 * b + n + 1)
                if c == 0:
                    reused(dve, rms_powered, 2 * b)
                dve.tensor_reduce(rms_raw[:, which, 4 * c:4 * c + 4],
                                  squares[:, n % 2, :].rearrange("p (h d) -> p h d", h=4), AX.X, ALU.add)\
                    .then_inc(squares_summed, 1)

            def mean_square(b, which):
                dve.wait_ge(squares_summed, 8 * b + NB * (which + 1))
                dve.tensor_scalar(rms_raw[:, which, :], rms_raw[:, which, :], 1.0 / HD, EPS, ALU.mult, ALU.add)\
                    .then_inc(rms_ready, 1)

            def take_scale(b, which):
                dve.wait_ge(rms_powered, 2 * b + which + 1)
                if which == 0:
                    reused(dve, exp_done, b * NB)
                else:
                    reused(dve, k_normed, b * NB)
                dve.tensor_scalar(ssq[:, which, :], rms_raw[:, which, :], (SCALE, 1.0)[which], None, ALU.mult)\
                    .then_inc(scale_ready, 1)

            def copy_probT(b, c):
                dve.wait_ge(prob_turned, b * NB + c + 1)
                reused(dve, mixed, b * NB + c - 1)
                dve.tensor_copy(probT[:, c % 2, :], ps[:, c % 2, :]).then_inc(probT_copied, 1)

            def copy_yT(b, c):
                dve.wait_ge(mixed, b * NB + c + 1)
                if c == 0:
                    reused(dve, out_projected, b)
                dve.tensor_copy(yT[:, 4 * c:4 * c + 4, :], ps[:, 2 + c % 2, :].rearrange("p (a b) -> p a b", a=4))\
                    .then_inc(yT_copied, 1)

            def normalise(b):
                st = Steps(dve, dve_steps, b * 2)
                dve.wait_ge(out_projected, b + 1)
                dve.wait_ge(resid_loaded, (b + 1) * DMA)
                dve.tensor_tensor(xr, ps[:, O_BANK, :], xr, ALU.add).then_inc(resid_added, 1)
                dve.wait_ge(resid_added, b + 1)
                reused(dve, f_turned, b)
                reused(dve, f_biased, b)
                norm_vector(dve, b, norm, st, xr, stats, moments, rstd, out, None)

            def normalise_f(b):
                st = Steps(dve, f_steps, b * 2)
                dve.wait_ge(f_projected, b + 1)
                dve.wait_ge(f_biased, b + 1)
                dve.tensor_tensor(fz, ps[:, F_BANK, :], fz, ALU.add).then_inc(f_added, 1)
                dve.wait_ge(f_added, b + 1)
                norm_vector(dve, b, fnorm, st, fz, fstats, fmoments, frstd, fout, stored)

            dve.memset(ones, 1.0).then_inc(consts_set, 1)
            make_ternary()
            for which in range(2):
                for c in range(NB):
                    sum_squares(0, which, c)
                mean_square(0, which)
                take_scale(0, which)

            def body(b, first=False):
                for c in range(NB):
                    copy_kT(b, c)
                for c in range(NB):
                    find_shift(b, c)
                if not first:
                    normalise_f(b - 1)
                for c in range(NB):
                    invert_total(b, c)
                    sum_squares(b + 1, 0, c)
                mean_square(b + 1, 0)
                take_scale(b + 1, 0)
                copy_probT(b, 0)
                for c in range(NB):
                    if c + 1 < NB:
                        copy_probT(b, c + 1)
                    copy_yT(b, c)
                    sum_squares(b + 1, 1, c)
                mean_square(b + 1, 1)
                take_scale(b + 1, 1)
                normalise(b)

            body(0, True)
            body(1)
            with dve.Fori(2, LAST) as b:
                body(b)
            for c in range(NB):
                copy_kT(LAST, c)
            for c in range(NB):
                find_shift(LAST, c)
            normalise_f(LAST - 1)
            for c in range(NB):
                invert_total(LAST, c)
            copy_probT(LAST, 0)
            for c in range(NB):
                if c + 1 < NB:
                    copy_probT(LAST, c + 1)
                copy_yT(LAST, c)
            normalise(LAST)
            normalise_f(LAST)

        @block.gpsimd
        def _(pool):
            def square(b, which, c):
                n = NB * which + c
                tile = (q, k)[which][:, c, :]
                pool.wait_ge(proj_copied, 12 * b + n + 1)
                reused(pool, squares_summed, 8 * b + n - 1)
                pool.tensor_tensor(squares[:, n % 2, :], tile, tile, ALU.mult).then_inc(squared, 1)

            def root(b, which):
                pool.wait_ge(rms_ready, 2 * b + which + 1)
                pool.tensor_tensor(rms_raw[:, which, :], rms_raw[:, which, :],
                                   minus_half.broadcast_to([P, H]), ALU.pow).then_inc(rms_powered, 1)

            def norm_k(b, c):
                pool.wait_ge(scale_ready, 2 * b + 2)
                tile = k[:, c, :].rearrange("p (h d) -> p h d", h=4)
                pool.tensor_tensor(tile, tile, spread(scale_k[:, 4 * c:4 * c + 4], 2, HD), ALU.mult)\
                    .then_inc(k_normed, 1)

            def norm_prob(b, c):
                pool.wait_ge(total_inverted, b * NB + c + 1)
                tile = prob[:, 4 * c:4 * c + 4, :]
                pool.tensor_tensor(tile, tile, spread(rtotal[:, 4 * c:4 * c + 4], 2, P), ALU.mult)\
                    .then_inc(prob_normed, 1)

            def bias_f(b):
                pool.wait_ge(norm.out, b + 1)
                reused(pool, fnorm.out, b)
                pool.tensor_tensor(fz, out, fbias, ALU.add).then_inc(f_biased, 1)

            def make_keys(b):
                for c in range(NB):
                    square(b, 0, c)
                root(b, 0)
                for c in range(NB):
                    square(b, 1, c)
                root(b, 1)
                for c in range(NB):
                    norm_k(b, c)

            pool.wait_ge(given_loaded, 4 * DMA)
            make_keys(0)

            def body(b, first=False):
                if not first:
                    bias_f(b - 1)
                    norm_gpsimd(pool, b - 1, fnorm, fmoments, frstd, minus_half)
                for c in range(NB):
                    norm_prob(b, c)
                    square(b + 1, 0, c)
                root(b + 1, 0)
                for c in range(NB):
                    square(b + 1, 1, c)
                root(b + 1, 1)
                for c in range(NB):
                    norm_k(b + 1, c)
                norm_gpsimd(pool, b, norm, moments, rstd, minus_half)

            body(0, True)
            body(1)
            with pool.Fori(2, LAST) as b:
                body(b)
            bias_f(LAST - 1)
            norm_gpsimd(pool, LAST - 1, fnorm, fmoments, frstd, minus_half)
            for c in range(NB):
                norm_prob(LAST, c)
            norm_gpsimd(pool, LAST, norm, moments, rstd, minus_half)
            bias_f(LAST)
            norm_gpsimd(pool, LAST, fnorm, fmoments, frstd, minus_half)


def program(nc, x, ctx, pos, t, outs):
    with ExitStack() as stack:
        def sem(name):
            return stack.enter_context(nc.semaphore(name))

        arena = stack.enter_context(nc.sbuf_tensor("arena", [P, ARENA], F32))
        ps = stack.enter_context(nc.psum_tensor("banks", [P, 8, 512], F32))
        x_after = [nc.dram_tensor(f"x_after_{n}", (SEQS, TOK, D), F32).ap() for n in range(4)]

        KB = 256
        WORK = 144 * KB
        c = Region(arena, WORK)
        const = {"ident": c.take(P), "minus_half": c.take(1)}
        const["work_c"] = c.at
        const.update(freq=c.take(4), bout=c.take(D))
        const["work_b"] = c.at
        const.update(rope_cos=c.take(64), rope_sgnsin=c.take(64), causal=c.take(P))
        const["work"] = c.at
        const["loaded"] = sem("consts_loaded")
        const["loads"] = 5
        const["halved"] = sem("minus_half_set")
        a_weights, b_weights = sem("a_weights_loaded"), sem("b_weights_loaded")
        w = Region(arena, 0)
        Wqkv, Wo = w.take(KC, 4 * D), w.take(8, D)
        We = [arena[:, k * 16 * KB:(k + 1) * 16 * KB] for k in range(KC)]
        Wr = Region(arena, 80 * KB).take(KC, 8 * D)
        router_loaded, experts_loaded = sem("router_loaded"), sem("experts_loaded")
        d_weights = sem("d_weights_loaded")
        w = Region(arena, 80 * KB, WORK)
        W_skip, W_in, Wd1, Wd2 = w.take(KC, 2 * D), w.take(KC, 2 * D), w.take(8, P), w.take(8 * P)
        Wbc, W_out = w.take(8, 32), w.take(8, D)
        d_params = {name: t[name] for name in ("conv_w", "conv_b", "b_delta", "A_log", "W_D", "norm_w")}
        d_regions = ((0, 80 * KB), (w.at, WORK), (const["work_c"], ARENA))
        e_first, e_rest = sem("e_first_loaded"), sem("e_rest_loaded")
        eWo, eWq = Region(arena, 0).take(16, D), Region(arena, 48 * KB).take(KC, 4 * D)
        w = Region(arena, 80 * KB)
        eWk, eWv = w.take(2, 4 * D), w.take(2, 4 * D)
        e_given = {"weight": t["L1_ffn_weight"], "bias": t["L1_ffn_bias"], "gq": t["gq"], "gk": t["gk"]}
        e_regions = ((32 * KB, 48 * KB), (w.at, WORK), (const["work_c"], ARENA))
        bc_dram = nc.dram_tensor("b_and_c", (8, 32, 256), F32).ap()
        w = Region(arena, 48 * KB, 72 * KB)
        xWq, xWkv, xWout = w.take(KC, D), w.take(2, 2 * D), w.take(KC, D)

        with nc.Block() as block:
            @block.sync
            def _(sp):
                for name in ("ident", "rope_cos", "rope_sgnsin", "causal"):
                    sp.dma_start(const[name], t[name]).then_inc(const["loaded"], DMA)
                sp.dma_start(const["freq"], t["freq"].partition_broadcast(P)).then_inc(const["loaded"], DMA)
                for c0, c1, name in ((0, 1024, "L0_attn_Wq"), (1024, 1536, "L0_attn_Wk"), (1536, 2048, "L0_attn_Wv")):
                    sp.dma_start(Wqkv[:, :, c0:c1], t[name].rearrange("(k p) n -> p k n", p=P)).then_inc(a_weights, DMA)
                sp.dma_start(Wo, t["L0_attn_Wo"].rearrange("(k p) n -> p k n", p=P)).then_inc(a_weights, DMA)

            @block.gpsimd
            def _(pool):
                pool.memset(const["minus_half"], -0.5).then_inc(const["halved"], 1)
                pool.wait_ge(const["halved"], 1)

        def load_b(sp):
            for dst, name in ((xWq, "L0_xattn_Wq"), (xWkv, "L0_xattn_Wkv"), (xWout, "L0_xattn_Wout")):
                sp.dma_start(dst, t[name].rearrange("(k p) n -> p k n", p=P)).then_inc(b_weights, DMA)
            sp.dma_start(const["bout"], t["L0_xattn_bout"].partition_broadcast(P)).then_inc(b_weights, DMA)

            sp.dma_start(Wr, t["L0_ffn_router_w"].rearrange("(k p) n -> p k n", p=P)).then_inc(router_loaded, DMA)

        def load_experts(chunks):
            def load(sp):
                for k in chunks:
                    sp.dma_start(We[k], t["L0_ffn_expert_w"][k * P:(k + 1) * P, :]).then_inc(experts_loaded, DMA)
            return load

        def load_d(sp):
            for dst, name in ((W_in, "L1_attn_W_in"), (W_skip, "L1_attn_W_skip"), (Wd1, "L1_attn_W_delta_1"),
                              (Wbc[:, :, 0:16], "L1_attn_W_B"), (Wbc[:, :, 16:32], "L1_attn_W_C"),
                              (W_out, "L1_attn_W_out")):
                sp.dma_start(dst, t[name].rearrange("(k p) n -> p k n", p=P)).then_inc(d_weights, DMA)
            sp.dma_start(Wd2, t["L1_attn_W_delta_2"]).then_inc(d_weights, DMA)

        def load_e_first(sp):
            for dst, name in ((eWk, "L1_xattn_Wk"), (eWv, "L1_xattn_Wv")):
                sp.dma_start(dst, t[name].rearrange("(k p) n -> p k n", p=P)).then_inc(e_first, DMA)

        def load_e_rest(sp):
            for dst, name in ((eWq, "L1_xattn_Wq"), (eWo, "L1_xattn_Wo")):
                sp.dma_start(dst, t[name].rearrange("(k p) n -> p k n", p=P)).then_inc(e_rest, DMA)

        def stage(build, weights, prefetch, *places, **more):
            own = []

            def own_sem(name):
                own.append(nc.alloc_semaphore(name))
                return own[-1]

            build(nc, own_sem, ps, arena, const, weights, prefetch, *places, **more)
            nc.clear_and_free_semaphores(own)
            nc.all_engine_barrier()

        stage(stage_self_attention, (Wqkv, Wo, a_weights), load_b, x, x_after[0])
        stage(stage_cross_attention, (xWq, xWkv, xWout, const["bout"], b_weights), load_experts(range(KC - 1)),
              x_after[0], ctx, pos, x_after[1], extra=(72 * KB, 80 * KB))
        stage(stage_experts, (Wr, lambda k: We[k], (t["L0_ffn_router_b"], t["L0_ffn_expert_b"]), router_loaded,
                              experts_loaded), (load_experts([KC - 1]), load_d), x_after[1], x_after[2],
              extra=(64 * KB, 80 * KB))
        stage(stage_selective_scan, (W_skip, W_in, Wd1, Wd2, Wbc, W_out, d_params, d_weights, d_regions),
              (load_e_first, load_e_rest), x_after[2], x_after[3], bc_dram)
        stage(stage_normed_attention, (eWq, eWk, eWv, eWo, e_first, e_rest, e_given, e_regions), None,
              x_after[3], ctx, outs)


_WEIGHTS = ["L0_attn_Wq", "L0_attn_Wk", "L0_attn_Wv", "L0_attn_Wo",
            "L0_xattn_Wq", "L0_xattn_Wkv", "L0_xattn_Wout", "L0_xattn_bout",
            "L0_ffn_router_w", "L0_ffn_router_b", "L0_ffn_expert_w", "L0_ffn_expert_b",
            "L1_attn_W_skip", "L1_attn_W_in", "L1_attn_W_delta_1", "L1_attn_W_delta_2", "L1_attn_W_B", "L1_attn_W_C",
            "L1_attn_W_out", "L1_xattn_Wq", "L1_xattn_Wk", "L1_xattn_Wv", "L1_xattn_Wo", "L1_ffn_bias"]


def tables():
    import numpy as np
    inv = 1.0 / np.float32(10000.0) ** (np.arange(0, 64, 2, dtype=np.float32) / np.float32(64))
    f = np.arange(TOK, dtype=np.float32)[:, None] * inv[None, :].astype(np.float32)
    cos, sin = np.cos(f), np.sin(f)
    k, q = np.arange(TOK)[:, None], np.arange(TOK)[None, :]
    return {
        "freq": (np.float32(10000.0) ** (-np.arange(4, dtype=np.float32) / np.float32(4))).astype(np.float32),
        "ident": np.eye(P, dtype=np.float32),
        "rope_cos": np.concatenate([cos, cos], -1).astype(np.float32),
        "rope_sgnsin": np.concatenate([-sin, sin], -1).astype(np.float32),
        "causal": (k <= q).astype(np.float32),
    }


def kernel(**inputs):
    import numpy as _np
    import concourse.bacc as _bacc
    from concourse.bass_utils import run_bass_kernel_spmd as _run

    nc = _bacc.Bacc("TRN2", target_bir_lowering=False, num_devices=1)
    given = {"x": inputs["x"], "ctx": inputs["ctx_1024"], "pos": inputs["fside_BxSx2_0"]}
    given.update({name: inputs[name] for name in _WEIGHTS})
    wq = _np.asarray(given["L0_attn_Wq"])
    given["L0_attn_Wq"] = wq.reshape(D, 4, 2, 2, 64).transpose(0, 1, 3, 2, 4).reshape(D, 1024)
    given["L0_ffn_router_w"] = _np.asarray(given["L0_ffn_router_w"]).reshape(D, 8, D).transpose(2, 1, 0)\
        .reshape(D, 8 * D)
    given["L0_ffn_router_b"] = _np.asarray(given["L0_ffn_router_b"]).reshape(D, 8).T.reshape(8 * D)
    given["L0_ffn_expert_w"] = _np.asarray(given["L0_ffn_expert_w"]).transpose(2, 0, 1).reshape(D, 8 * D)
    def by_tile(name, *rest):
        return _np.asarray(inputs[name]).reshape(8, P, *rest).swapaxes(0, 1)
    given["conv_w"] = _np.asarray(inputs["L1_attn_conv_w"]).reshape(4, 8, P).transpose(2, 1, 0)
    given["conv_b"], given["b_delta"] = by_tile("L1_attn_conv_b"), by_tile("L1_attn_b_delta_2")
    given["A_log"], given["W_D"] = by_tile("L1_attn_A_log", 16), by_tile("L1_attn_W_D")
    given["norm_w"] = _np.asarray(inputs["L1_attn_norm_w"]).reshape(KC, P).T
    given["gq"], given["gk"] = (_np.asarray(inputs[f"L1_xattn_{n}"]).reshape(P, 1) for n in ("gq", "gk"))
    given["L1_ffn_weight"] = _np.asarray(inputs["L1_ffn_weight"]).T
    given.update(tables())
    arrays, args = {}, {}
    for name, a in given.items():
        a = _np.ascontiguousarray(a)
        arrays[f"in_{name}"] = a
        args[name] = nc.dram_tensor(f"in_{name}", a.shape, F32, kind="ExternalInput").ap()
    out = nc.dram_tensor("out_0", (SEQS, TOK, D), F32, kind="ExternalOutput").ap()
    program(nc, args["x"], args["ctx"], args["pos"], args, out)
    r = _run(nc, [arrays], core_ids=[0])
    return r.results[0]["out_0"]
```

```python
from contextlib import ExitStack

import concourse.bass as bass
from concourse import mybir

F32 = mybir.dt.float32
ALU = mybir.AluOpType
ACT = mybir.ActivationFunctionType
AX = mybir.AxisListType

P = 128
SEQS, TOK, D = 16, 128, 512
KC = D // P
EPS = 1e-5
DMA = 16
TWO_PI = 6.283185307179586
ARENA = 53200


class Region:

    def __init__(self, arena, start, end=ARENA):
        self.arena, self.at, self.end = arena, start, end

    def take(self, *dims):
        n = 1
        for d in dims:
            n *= d
        assert self.at + n <= self.end, (self.at, n, self.end)
        view = self.arena[:, self.at:self.at + n]
        self.at += n
        if len(dims) == 2:
            return view.rearrange("p (a b) -> p a b", a=dims[0])
        if len(dims) == 3:
            return view.rearrange("p (a b c) -> p a b c", a=dims[0], b=dims[1])
        return view


def reused(eng, sem, value):
    if not isinstance(value, int) or value > 0:
        eng.wait_ge(sem, value)


class Steps:

    def __init__(self, eng, sem, before):
        self.eng, self.sem, self.before, self.n = eng, sem, before, 0

    def __call__(self, ins):
        ins.then_inc(self.sem, 1)
        self.n += 1

    def wait(self):
        reused(self.eng, self.sem, self.before + self.n)


def over_sequences(eng, body):
    body(0)
    with eng.Fori(1, SEQS - 1) as b:
        body(b)


def row(dram, b):
    return dram[bass.ds(b, 1), :, :].rearrange("a p d -> (a p) d")


def spread(ap, axis, n):
    v = ap.unsqueeze(axis)
    shape = list(v.shape)
    shape[axis] = n
    return v.broadcast_to(shape)


def project(pe, bank, stationary, moving, chunks):
    for c in range(chunks):
        last = pe.matmul(bank, stationary(c), moving(c), start=(c == 0), stop=(c == chunks - 1))
    return last


def turn(pe, bank, tiles, ident):
    for i, tile in enumerate(tiles):
        last = pe.transpose(bank[:, i * P:(i + 1) * P], tile, ident)
    return last


def halves(tile, n=KC):
    return [tile[:, i * P:(i + 1) * P] for i in range(n)]


class NormSems:

    def __init__(self, sem, stage):
        self.var = sem(f"{stage}_variance_ready")
        self.rstd = sem(f"{stage}_rstd_ready")
        self.out = sem(f"{stage}_normed")


def norm_moments(dve, sems, steps, z, stats, moments):
    steps.wait()
    steps(dve.bn_stats(stats, z))
    steps.wait()
    dve.memset(moments[:, 2:3], 0.0)
    steps(dve.bn_aggr(moments[:, 0:2], stats))
    steps.wait()
    dve.tensor_scalar(moments[:, 1:2], moments[:, 1:2], EPS, None, ALU.add).then_inc(sems.var, 1)


def norm_apply(dve, b, sems, z, moments, rstd, out, stored):
    dve.wait_ge(sems.rstd, b + 1)
    if stored is not None:
        reused(dve, stored, b * DMA)
    dve.tensor_scalar(out, z, moments[:, 0:1], rstd, ALU.subtract, ALU.mult).then_inc(sems.out, 1)


def norm_vector(dve, b, sems, steps, z, stats, moments, rstd, out, stored):
    norm_moments(dve, sems, steps, z, stats, moments)
    norm_apply(dve, b, sems, z, moments, rstd, out, stored)


def norm_gpsimd(pool, b, sems, moments, rstd, minus_half):
    pool.wait_ge(sems.var, b + 1)
    pool.tensor_tensor(rstd, moments[:, 1:2], minus_half, ALU.pow).then_inc(sems.rstd, 1)


def stage_self_attention(nc, sem, ps, arena, const, weights, prefetch, src, dst):
    HEADS, KV, HD = 16, 8, 64
    CAP, SCALE = 50.0, 256.0 ** -0.5
    ident, minus_half = const["ident"], const["minus_half"]
    cos, sgnsin, causal = const["rope_cos"], const["rope_sgnsin"], const["causal"]
    Wqkv, Wo, q_loaded, given = weights

    r = Region(arena, const["work"])
    xa, xr = r.take(D), r.take(D)
    xT = r.take(KC, P)
    tcos, tsin = r.take(3, D), r.take(3, D)
    qk = r.take(3 * D)
    qkT = r.take(12, P)
    V = r.take(KV, HD + 1)
    prob = r.take(4, D)
    y, yT = r.take(HEADS * HD), r.take(8, P)
    rden = r.take(4, 4)
    z, out = r.take(D), r.take(D)
    stats, moments, rstd = r.take(6), r.take(3), r.take(1)
    qT, kT = qkT[:, 0:8, :], qkT[:, 8:12, :]

    x_loaded = sem("a_x_loaded")
    kv_loaded = sem("a_kv_loaded")
    out_loaded = sem("a_out_weight_loaded")
    resid_loaded = sem("a_resid_loaded")
    stored = sem("a_stored")
    consts_set = sem("a_consts_set")
    x_turned = sem("a_x_turned")
    xT_copied = sem("a_xT_copied")
    projected = sem("a_projected")
    v_copied = sem("a_v_copied")
    rope_parts = sem("a_rope_parts")
    roped = sem("a_roped")
    qk_turned = sem("a_qk_turned")
    qkT_copied = sem("a_qkT_copied")
    scored = sem("a_scored")
    capped_done = sem("a_capped")
    exp_done = sem("a_exp_done")
    masked = sem("a_masked")
    mixed = sem("a_mixed")
    y_normed = sem("a_y_normed")
    y_turned = sem("a_y_turned")
    yT_copied = sem("a_yT_copied")
    out_projected = sem("a_out_projected")
    resid_added = sem("a_resid_added")
    dve_steps = sem("a_dve_steps")
    norm = NormSems(sem, "a")
    DVE_STEPS = 6
    LAST = SEQS - 1

    X_BANK = 4
    P_BANK = [5, 6, 5, 6]
    Y_BANK = [7, 4, 7, 4]
    YT_BANK = [5, 6]
    O_BANK = 7

    with nc.Block() as block:
        @block.sync
        def _(sp):
            sp.dma_start(xa, row(src, 0)).then_inc(x_loaded, DMA)
            for c, w in ((2, given[0]), (3, given[1])):
                sp.dma_start(Wqkv[:, :, c * D:(c + 1) * D], w.rearrange("(k p) n -> p k n", p=P))\
                    .then_inc(kv_loaded, DMA)
            sp.dma_start(Wo, given[2].rearrange("(k p) n -> p k n", p=P)).then_inc(out_loaded, DMA)
            sp.wait_ge(x_turned, 1)
            sp.dma_start(xa, row(src, 1)).then_inc(x_loaded, DMA)

            def body(b, more):
                reused(sp, resid_added, b)
                sp.dma_start(xr, row(src, b)).then_inc(resid_loaded, DMA)
                if more:
                    sp.wait_ge(x_turned, b + 2)
                    sp.dma_start(xa, row(src, b + 2)).then_inc(x_loaded, DMA)
                sp.wait_ge(norm.out, b + 1)
                sp.dma_start(row(dst, b), out).then_inc(stored, DMA)

            for b, load in enumerate(prefetch):
                body(b, True)
                load(sp)
            with sp.Fori(len(prefetch), SEQS - 2) as b:
                body(b, True)
            body(SEQS - 2, False)
            body(LAST, False)
            sp.wait_ge(stored, SEQS * DMA)

        @block.tensor
        def _(pe):
            def turn_x(b, first=False):
                pe.wait_ge(x_loaded, (b + 1) * DMA)
                if not first:
                    pe.wait_ge(y_normed, (b - 1) * 4)
                turn(pe, ps[:, X_BANK, :], halves(xa), ident).then_inc(x_turned, 1)

            def proj(b, c, first=False):
                if c == 0:
                    pe.wait_ge(xT_copied, b + 1)
                    if not first:
                        pe.wait_ge(yT_copied, (b - 1) * 2)
                if c == 2:
                    pe.wait_ge(rope_parts, b * 3 + 1)
                if c == 3:
                    pe.wait_ge(rope_parts, b * 3 + 2)
                project(pe, ps[:, P_BANK[c], :], lambda k: xT[:, k, :],
                        lambda k: Wqkv[:, k, c * D:(c + 1) * D], KC).then_inc(projected, 1)

            def turn_qk(b):
                pe.wait_ge(roped, b * 3 + 3)
                reused(pe, capped_done, b * 4)
                for t in range(2):
                    turn(pe, ps[:, t, :], halves(qk[:, t * D:(t + 1) * D]), ident).then_inc(qk_turned, 1)
                turn(pe, ps[:, 2, :], halves(qk[:, 2 * D:3 * D]), ident).then_inc(qk_turned, 1)

            def scores(b):
                pe.wait_ge(qkT_copied, b * 3 + 3)
                for g in range(4):
                    ihalf, p = g // 2, g % 2
                    rows = slice(64 * p, 64 * p + 64)
                    for i in range(2):
                        t = 2 * ihalf + i
                        last = pe.matmul(ps[:, g, i * 256:(i + 1) * 256], kT[rows, t, :],
                                         qT[rows, 2 * t:2 * t + 2, :], start=True, stop=True)
                    last.then_inc(scored, 1)

            def mix(b, g, last):
                ihalf, p = g // 2, g % 2
                pe.wait_ge(masked, b * 4 + g + 1)
                if g == 0:
                    pe.wait_ge(v_copied, b + 1)
                    reused(pe, resid_added, b)
                elif g == 1:
                    pe.wait_ge(xT_copied, b + (1 if last else 2))
                else:
                    pe.wait_ge(y_normed, b * 4 + g - 1)
                for s in range(4):
                    kv = 2 * (2 * ihalf + s // 2) + p
                    done = pe.matmul(ps[:, Y_BANK[g], s * 65:(s + 1) * 65], prob[:, g, s * P:(s + 1) * P],
                                     V[:, kv, :], start=True, stop=True)
                done.then_inc(mixed, 1)

            def turn_y(b, t, last):
                pe.wait_ge(y_normed, b * 4 + 2 * t + 2)
                if not last:
                    if t == 0:
                        pe.wait_ge(rope_parts, b * 3 + 6)
                    else:
                        pe.wait_ge(v_copied, b + 2)
                turn(pe, ps[:, YT_BANK[t], :], halves(y[:, t * D:(t + 1) * D]), ident).then_inc(y_turned, 1)

            def out_proj(b, chunks):
                pe.wait_ge(yT_copied, b * 2 + chunks[0] // 4 + 1)
                if chunks[0] == 0:
                    pe.wait_ge(y_normed, b * 4 + 3)
                for k in chunks:
                    last = pe.matmul(ps[:, O_BANK, :], yT[:, k, :], Wo[:, k, :], start=(k == 0), stop=(k == 7))
                return last

            def mix_and_project(b, last=False):
                for g in range(3):
                    mix(b, g, last)
                turn_y(b, 0, last)
                mix(b, 3, last)
                out_proj(b, (0, 1))
                turn_y(b, 1, last)
                out_proj(b, (2, 3))
                out_proj(b, (4, 5, 6, 7)).then_inc(out_projected, 1)

            pe.wait_ge(q_loaded, DMA)
            pe.wait_ge(const["loaded"], const["loads"] * DMA)
            turn_x(0, first=True)
            proj(0, 0, first=True)
            proj(0, 1, first=True)
            pe.wait_ge(kv_loaded, 2 * DMA)
            proj(0, 2, first=True)
            proj(0, 3, first=True)
            pe.wait_ge(out_loaded, DMA)

            def body(b):
                turn_x(b + 1)
                turn_qk(b)
                proj(b + 1, 0)
                proj(b + 1, 1)
                scores(b)
                proj(b + 1, 2)
                proj(b + 1, 3)
                mix_and_project(b)

            over_sequences(pe, body)
            turn_qk(LAST)
            scores(LAST)
            mix_and_project(LAST, last=True)

        @block.scalar
        def _(act):
            def copy_xT(b):
                act.wait_ge(x_turned, b + 1)
                reused(act, projected, b * 4)
                act.activation(xT, ps[:, X_BANK, :].rearrange("p (a b) -> p a b", a=KC), ACT.Copy)\
                    .then_inc(xT_copied, 1)

            def copy_v(b):
                act.wait_ge(projected, b * 4 + 4)
                reused(act, mixed, b * 4)
                act.activation(V[:, :, 0:HD], ps[:, P_BANK[3], :].rearrange("p (h d) -> p h d", h=KV), ACT.Copy)\
                    .then_inc(v_copied, 1)

            def copy_qk(b):
                for t in range(3):
                    act.wait_ge(qk_turned, b * 3 + t + 1)
                    if t == 0:
                        reused(act, scored, b * 4)
                    act.activation(qkT[:, 4 * t:4 * t + 4, :], ps[:, t, :].rearrange("p (a b) -> p a b", a=4),
                                   ACT.Copy).then_inc(qkT_copied, 1)

            def softmax(b):
                for g in range(4):
                    act.wait_ge(scored, b * 4 + g + 1)
                    reused(act, mixed, b * 4)
                    act.activation(prob[:, g, :], ps[:, g, :], ACT.Tanh, scale=SCALE / CAP)\
                        .then_inc(capped_done, 1)
                for g in range(4):
                    act.wait_ge(capped_done, b * 4 + g + 1)
                    act.activation(prob[:, g, :], prob[:, g, :], ACT.Exp, scale=CAP).then_inc(exp_done, 1)

            def copy_yT(b, t):
                act.wait_ge(y_turned, b * 2 + t + 1)
                reused(act, out_projected, b)
                act.activation(yT[:, 4 * t:4 * t + 4, :],
                               ps[:, YT_BANK[t], :].rearrange("p (a b) -> p a b", a=4), ACT.Copy)\
                    .then_inc(yT_copied, 1)

            act.wait_ge(consts_set, 1)
            copy_xT(0)
            copy_v(0)

            def body(b):
                copy_xT(b + 1)
                copy_qk(b)
                softmax(b)
                copy_yT(b, 0)
                copy_v(b + 1)
                copy_yT(b, 1)

            over_sequences(act, body)
            copy_qk(LAST)
            softmax(LAST)
            copy_yT(LAST, 0)
            copy_yT(LAST, 1)

        @block.vector
        def _(dve):
            def rope_products(b, c):
                src_bank = ps[:, P_BANK[c], :].rearrange("p (h a d) -> p h a d", h=8, a=2)
                dve.wait_ge(projected, b * 4 + c + 1)
                reused(dve, roped, b * 3)
                dve.tensor_tensor(tcos[:, c, :].rearrange("p (h a) -> p h a", h=8),
                                  ps[:, P_BANK[c], :].rearrange("p (h a) -> p h a", h=8),
                                  spread(cos, 1, 8), ALU.mult)
                dve.tensor_tensor(tsin[:, c, :].rearrange("p (h a d) -> p h a d", h=8, a=2),
                                  src_bank[:, :, ::-1, :],
                                  spread(sgnsin.rearrange("p (a d) -> p a d", a=2), 1, 8), ALU.mult)\
                    .then_inc(rope_parts, 1)

            def norm_mix(b):
                st = Steps(dve, dve_steps, b * DVE_STEPS)
                for g in range(4):
                    ihalf, p = g // 2, g % 2
                    bank = ps[:, Y_BANK[g], 0:260].rearrange("q (s d) -> q s d", s=4)
                    dve.wait_ge(mixed, b * 4 + g + 1)
                    st(dve.reciprocal(rden[:, g, :], bank[:, :, HD]))
                    st.wait()
                    if g == 0:
                        reused(dve, y_turned, b * 2)
                    heads = y[:, ihalf * D:(ihalf + 1) * D].rearrange(
                        "q (i p j d) -> q i p j d", i=2, p=2, j=2)[:, :, p]
                    for i in range(2):
                        last = dve.tensor_tensor(heads[:, i], bank[:, 2 * i:2 * i + 2, 0:HD],
                                                 spread(rden[:, g, 2 * i:2 * i + 2], 2, HD), ALU.mult)
                    last.then_inc(y_normed, 1)
                dve.wait_ge(out_projected, b + 1)
                dve.wait_ge(resid_loaded, (b + 1) * DMA)
                dve.tensor_tensor(z, ps[:, O_BANK, :], xr, ALU.add).then_inc(resid_added, 1)
                dve.wait_ge(resid_added, b + 1)
                st.wait()
                norm_vector(dve, b, norm, st, z, stats, moments, rstd, out, stored)
                assert st.n == DVE_STEPS, st.n

            dve.memset(V[:, :, HD:HD + 1], 1.0).then_inc(consts_set, 1)
            dve.wait_ge(const["loaded"], const["loads"] * DMA)
            for c in range(3):
                rope_products(0, c)

            def body(b):
                rope_products(b + 1, 0)
                rope_products(b + 1, 1)
                rope_products(b + 1, 2)
                norm_mix(b)

            over_sequences(dve, body)
            norm_mix(LAST)

        @block.gpsimd
        def _(pool):
            def rope_sum(b, c):
                pool.wait_ge(rope_parts, b * 3 + c + 1)
                if c == 0:
                    reused(pool, qk_turned, b * 3)
                pool.tensor_tensor(qk[:, c * D:(c + 1) * D], tcos[:, c, :], tsin[:, c, :], ALU.add)\
                    .then_inc(roped, 1)

            def mask(b, g):
                pool.wait_ge(exp_done, b * 4 + g + 1)
                v = prob[:, g, :].rearrange("k (s q) -> k s q", s=4)
                pool.tensor_tensor(v, v, spread(causal, 1, 4), ALU.mult).then_inc(masked, 1)

            pool.wait_ge(const["loaded"], const["loads"] * DMA)
            for c in range(3):
                rope_sum(0, c)

            def body(b):
                rope_sum(b + 1, 0)
                rope_sum(b + 1, 1)
                for g in range(4):
                    mask(b, g)
                rope_sum(b + 1, 2)
                norm_gpsimd(pool, b, norm, moments, rstd, minus_half)

            over_sequences(pool, body)
            for g in range(4):
                mask(LAST, g)
            norm_gpsimd(pool, LAST, norm, moments, rstd, minus_half)


def stage_cross_attention(nc, sem, ps, arena, const, weights, prefetch, src, ctx, pos, dst, extra):
    HEADS, HD, PAD, CC = 32, 16, 32, 2
    SCALE = HD ** -0.5
    TILES = 8
    ident, minus_half = const["ident"], const["minus_half"]
    Wq, Wkv, Wout, bout, weights_loaded = weights

    r = Region(arena, const["work_b"])
    xa, ca, xr = r.take(D), r.take(CC * P), r.take(D)
    xT, cT = r.take(KC, P), r.take(CC, P)
    tcos, tsin = r.take(2, D), r.take(2, D)
    qkp = r.take(2, HEADS * PAD)
    qkT = r.take(2 * TILES, P)
    V = r.take(HEADS, HD + 1)
    prob = r.take(TILES // 2, D)
    probT = r.take(4, D)
    more = Region(arena, *extra)
    prob2 = more.take(TILES // 2, D)
    y, yT = r.take(D), r.take(KC, P)
    top, rden = r.take(TILES, 4), r.take(2, 16)
    z, out = r.take(D), r.take(D)
    stats, moments, rstd = r.take(6), r.take(3), r.take(1)
    cosr, sinr = r.take(SEQS, 16), r.take(SEQS, 16)
    pos_sb, freq = r.take(2 * SEQS), const["freq"]
    ang, turns = tcos[:, 0, 0:128], tcos[:, 0, 128:256]

    def prob_tile(n):
        return prob[:, n, :] if n < 4 else prob2[:, n - 4, :]

    x_loaded = sem("b_x_loaded")
    resid_loaded = sem("b_resid_loaded")
    pos_loaded = sem("b_pos_loaded")
    stored = sem("b_stored")
    consts_set = sem("b_consts_set")
    angles_ready = sem("b_angles_ready")
    sines_ready = sem("b_sines_ready")
    tables_ready = sem("b_tables_ready")
    x_turned = sem("b_x_turned")
    xT_copied = sem("b_xT_copied")
    projected = sem("b_projected")
    v_copied = sem("b_v_copied")
    rope_parts = sem("b_rope_parts")
    roped = sem("b_roped")
    qk_turned = sem("b_qk_turned")
    qkT_copied = sem("b_qkT_copied")
    scored = sem("b_scored")
    top_found = sem("b_top_found")
    shifted = sem("b_shifted")
    exp_done = sem("b_exp_done")
    prob_turned = sem("b_prob_turned")
    probT_copied = sem("b_probT_copied")
    mixed = sem("b_mixed")
    y_normed = sem("b_y_normed")
    y_turned = sem("b_y_turned")
    yT_copied = sem("b_yT_copied")
    out_projected = sem("b_out_projected")
    resid_biased = sem("b_resid_biased")
    resid_added = sem("b_resid_added")
    dve_steps = sem("b_dve_steps")
    norm = NormSems(sem, "b")
    SET_STEPS, DVE_STEPS = 12, 4
    LAST = SEQS - 1
    X_BANK, C_BANK, Q_BANK, K_BANK, V_BANK, YT_BANK, O_BANK = 4, 5, 6, 7, 5, 4, 6
    Y_BANK = [6, 7]

    with nc.Block() as block:
        @block.sync
        def _(sp):
            def load_x(b):
                sp.dma_start(xa, row(src, b)).then_inc(x_loaded, DMA)
                sp.dma_start(ca, row(ctx, b)).then_inc(x_loaded, DMA)

            sp.dma_start(pos_sb.rearrange("t (b p) -> t b p", p=2), pos.rearrange("b t p -> t b p"))\
                .then_inc(pos_loaded, DMA)
            load_x(0)
            prefetch(sp)
            sp.wait_ge(x_turned, 2)
            load_x(1)

            def body(b, more):
                reused(sp, resid_added, b)
                sp.dma_start(xr, row(src, b)).then_inc(resid_loaded, DMA)
                if more:
                    sp.wait_ge(x_turned, 2 * b + 4)
                    load_x(b + 2)
                sp.wait_ge(norm.out, b + 1)
                sp.dma_start(row(dst, b), out).then_inc(stored, DMA)

            body(0, True)
            with sp.Fori(1, SEQS - 2) as b:
                body(b, True)
            body(SEQS - 2, False)
            body(LAST, False)
            sp.wait_ge(stored, SEQS * DMA)

        @block.tensor
        def _(pe):
            def turn_x(b, first=False):
                pe.wait_ge(x_loaded, 2 * (b + 1) * DMA)
                if not first:
                    reused(pe, yT_copied, (b - 1) * 2)
                turn(pe, ps[:, X_BANK, :], halves(xa), ident).then_inc(x_turned, 1)
                if not first:
                    pe.wait_ge(v_copied, b)
                turn(pe, ps[:, C_BANK, :], halves(ca, CC), ident).then_inc(x_turned, 1)

            def proj_q(b, first=False):
                pe.wait_ge(xT_copied, 2 * b + 1)
                if not first:
                    reused(pe, resid_added, b - 1)
                project(pe, ps[:, Q_BANK, :], lambda k: xT[:, k, :], lambda k: Wq[:, k, :], KC)\
                    .then_inc(projected, 1)

            def proj_k(b, first=False):
                pe.wait_ge(xT_copied, 2 * b + 2)
                if not first:
                    reused(pe, y_normed, (b - 1) * 2)
                project(pe, ps[:, K_BANK, :], lambda k: cT[:, k, :], lambda k: Wkv[:, k, 0:D], CC)\
                    .then_inc(projected, 1)

            def proj_v(b):
                reused(pe, probT_copied, b * 8)
                project(pe, ps[:, V_BANK, :], lambda k: cT[:, k, :], lambda k: Wkv[:, k, D:2 * D], CC)\
                    .then_inc(projected, 1)

            def turn_qk(b):
                reused(pe, shifted, b * 8)
                for n in range(4):
                    if n % 2 == 0:
                        pe.wait_ge(roped, b * 2 + n // 2 + 1)
                    turn(pe, ps[:, n, :], halves(qkp[:, n // 2, (n % 2) * D:(n % 2 + 1) * D]), ident)\
                        .then_inc(qk_turned, 1)

            def scores(b, half):
                if half == 0:
                    pe.wait_ge(qkT_copied, b * 4 + 4)
                for rg in range(4):
                    rows = slice(32 * rg, 32 * rg + 32)
                    if half == 1:
                        pe.wait_ge(shifted, b * 8 + rg + 1)
                    for g in range(4):
                        t = 4 * half + g
                        last = pe.matmul(ps[:, rg, g * P:(g + 1) * P], qkT[rows, t, :], qkT[rows, TILES + t, :],
                                         start=True, stop=True)
                    last.then_inc(scored, 1)

            def turn_prob(b, n, last):
                bank = 4 + n % 2
                pe.wait_ge(exp_done, b * 8 + n + 1)
                if n >= 2:
                    pe.wait_ge(probT_copied, b * 8 + n - 1)
                elif not last:
                    pe.wait_ge(xT_copied, 2 * b + 3 + n)
                turn(pe, ps[:, bank, :], halves(prob_tile(n)), ident).then_inc(prob_turned, 1)

            def mix(b, n, last):
                half, rg = n // 4, n % 4
                pe.wait_ge(probT_copied, b * 8 + n + 1)
                if rg == 0 and not last:
                    pe.wait_ge(rope_parts, (b + 1) * 2 + half + 1)
                for g in range(4):
                    h = 4 * g + rg
                    done = pe.matmul(ps[:, Y_BANK[half], h * 17:(h + 1) * 17], probT[:, n % 4, g * P:(g + 1) * P],
                                     V[:, 16 * half + h, :], start=True, stop=True)
                done.then_inc(mixed, 1)

            def attend(b, last=False):
                pe.wait_ge(v_copied, b + 1)
                turn_prob(b, 0, last)
                for n in range(8):
                    if n < 7:
                        turn_prob(b, n + 1, last)
                    mix(b, n, last)

            def turn_y(b, half):
                pe.wait_ge(y_normed, b * 2 + half + 1)
                if half == 0:
                    pe.wait_ge(probT_copied, b * 8 + 7)
                else:
                    pe.wait_ge(yT_copied, b * 2 + 1)
                turn(pe, ps[:, YT_BANK, half * 256:(half + 1) * 256], halves(y[:, half * 256:(half + 1) * 256], 2),
                     ident).then_inc(y_turned, 1)

            def out_proj(b):
                for k in range(KC):
                    if k % 2 == 0:
                        pe.wait_ge(yT_copied, b * 2 + k // 2 + 1)
                    last = pe.matmul(ps[:, O_BANK, :], yT[:, k, :], Wout[:, k, :], start=(k == 0), stop=(k == KC - 1))
                last.then_inc(out_projected, 1)

            pe.wait_ge(weights_loaded, 4 * DMA)
            turn_x(0, first=True)
            proj_q(0, first=True)
            proj_k(0, first=True)
            proj_v(0)

            def body(b):
                turn_qk(b)
                turn_x(b + 1)
                scores(b, 0)
                proj_q(b + 1)
                scores(b, 1)
                proj_k(b + 1)
                attend(b)
                turn_y(b, 0)
                proj_v(b + 1)
                turn_y(b, 1)
                out_proj(b)

            over_sequences(pe, body)
            turn_qk(LAST)
            scores(LAST, 0)
            scores(LAST, 1)
            attend(LAST, last=True)
            turn_y(LAST, 0)
            turn_y(LAST, 1)
            out_proj(LAST)

        @block.scalar
        def _(act):
            def copy_xT(b):
                act.wait_ge(x_turned, 2 * b + 1)
                reused(act, projected, b * 3)
                act.activation(xT, ps[:, X_BANK, :].rearrange("p (a b) -> p a b", a=KC), ACT.Copy)\
                    .then_inc(xT_copied, 1)
                act.wait_ge(x_turned, 2 * b + 2)
                act.activation(cT, ps[:, C_BANK, 0:CC * P].rearrange("p (a b) -> p a b", a=CC), ACT.Copy)\
                    .then_inc(xT_copied, 1)

            def copy_v(b):
                act.wait_ge(projected, b * 3 + 3)
                reused(act, mixed, b * 8)
                act.activation(V[:, :, 0:HD], ps[:, V_BANK, :].rearrange("p (h d) -> p h d", h=HEADS), ACT.Copy)\
                    .then_inc(v_copied, 1)

            def copy_qk(b):
                for n in range(4):
                    act.wait_ge(qk_turned, b * 4 + n + 1)
                    if n == 0:
                        reused(act, scored, b * 8)
                    act.activation(qkT[:, 4 * n:4 * n + 4, :], ps[:, n, :].rearrange("p (a b) -> p a b", a=4),
                                   ACT.Copy).then_inc(qkT_copied, 1)

            def exps(b, n):
                act.wait_ge(shifted, b * 8 + n + 1)
                act.activation(prob_tile(n), prob_tile(n), ACT.Exp, scale=SCALE).then_inc(exp_done, 1)

            def copy_probT(b, n):
                act.wait_ge(prob_turned, b * 8 + n + 1)
                reused(act, mixed, b * 8 + n - 3)
                act.activation(probT[:, n % 4, :], ps[:, 4 + n % 2, :], ACT.Copy).then_inc(probT_copied, 1)

            def softmaxes(b):
                for n in range(6):
                    exps(b, n)
                for n in range(8):
                    copy_probT(b, n)
                    if n < 2:
                        exps(b, n + 6)

            def copy_yT(b, half):
                act.wait_ge(y_turned, b * 2 + half + 1)
                reused(act, out_projected, b)
                act.activation(yT[:, 2 * half:2 * half + 2, :], ps[:, YT_BANK, half * 256:(half + 1) * 256]
                               .rearrange("p (a b) -> p a b", a=2), ACT.Copy).then_inc(yT_copied, 1)

            for n, table in ((0, sinr), (1, cosr)):
                act.wait_ge(angles_ready, n + 1)
                reused(act, tables_ready, n)
                act.activation(turns, ang, ACT.Sin).then_inc(sines_ready, 1)
            copy_xT(0)
            act.wait_ge(consts_set, 2)
            copy_v(0)

            def body(b):
                copy_qk(b)
                copy_xT(b + 1)
                softmaxes(b)
                copy_yT(b, 0)
                copy_v(b + 1)
                copy_yT(b, 1)

            over_sequences(act, body)
            copy_qk(LAST)
            softmaxes(LAST)
            copy_yT(LAST, 0)
            copy_yT(LAST, 1)

        @block.vector
        def _(dve):
            def make_tables():
                st = Steps(dve, dve_steps, 0)
                dve.wait_ge(pos_loaded, DMA)
                HALF_TURN, MAGIC = TWO_PI / 2, 12582912.0
                HI = 6.28125
                for n, (table, shift) in enumerate(((sinr, 0.0), (cosr, HALF_TURN / 2))):
                    if n == 1:
                        dve.wait_ge(tables_ready, 1)
                    dve.tensor_tensor(ang.rearrange("t (b j) -> t b j", j=4), spread(pos_sb, 2, 4),
                                      spread(freq, 1, 2 * SEQS), ALU.mult).then_inc(dve_steps, 1)
                    st.n += 1
                    st.wait()
                    st(dve.tensor_scalar(ang, ang, shift, None, ALU.add))
                    st.wait()
                    st(dve.tensor_scalar(turns, ang, 1.0 / TWO_PI, MAGIC, ALU.mult, ALU.add))
                    st.wait()
                    st(dve.tensor_scalar(turns, turns, -MAGIC, None, ALU.add))
                    st.wait()
                    st(dve.scalar_tensor_tensor(ang, turns, -HI, ang, ALU.mult, ALU.add))
                    st.wait()
                    st(dve.scalar_tensor_tensor(ang, turns, HI - TWO_PI, ang, ALU.mult, ALU.add))
                    st.wait()
                    dve.tensor_scalar(ang, ang, 3.1415925, -3.1415925, ALU.min, ALU.max).then_inc(angles_ready, 1)
                    dve.wait_ge(sines_ready, n + 1)
                    pair = table.rearrange("t b (j s) -> t (b j) s", s=2)
                    if n == 0:
                        dve.tensor_scalar(pair[:, :, 0], turns, -1.0, None, ALU.mult)
                    else:
                        dve.tensor_copy(pair[:, :, 0], turns)
                    dve.tensor_copy(pair[:, :, 1], turns).then_inc(tables_ready, 1)
                dve.wait_ge(tables_ready, 2)
                assert st.n == SET_STEPS, st.n

            def rope_products(b, c):
                bank = ps[:, (Q_BANK, K_BANK)[c], :]
                dve.wait_ge(projected, b * 3 + c + 1)
                reused(dve, roped, b * 2)
                if isinstance(b, int):
                    cosb, sinb = cosr[:, b, :], sinr[:, b, :]
                else:
                    cosb = cosr[:, bass.ds(b, 1), :].rearrange("t b j -> t (b j)")
                    sinb = sinr[:, bass.ds(b, 1), :].rearrange("t b j -> t (b j)")
                dve.tensor_tensor(tcos[:, c, :].rearrange("p (h a) -> p h a", h=HEADS),
                                  bank.rearrange("p (h a) -> p h a", h=HEADS), spread(cosb, 1, HEADS), ALU.mult)
                dve.tensor_tensor(tsin[:, c, :].rearrange("p (h a s) -> p h a s", h=HEADS, s=2),
                                  bank.rearrange("p (h a s) -> p h a s", h=HEADS, s=2)[:, :, :, ::-1],
                                  spread(sinb.rearrange("p (a s) -> p a s", s=2), 1, HEADS), ALU.mult)\
                    .then_inc(rope_parts, 1)

            def shift(b, half):
                for n in range(4 * half, 4 * half + 4):
                    bank = ps[:, n % 4, :].rearrange("q (g k) -> q g k", g=4)
                    dve.wait_ge(scored, b * 8 + n + 1)
                    dve.tensor_reduce(top[:, n, :], bank, AX.X, ALU.max).then_inc(top_found, 1)
                    dve.wait_ge(top_found, b * 8 + n + 1)
                    reused(dve, prob_turned, (b - 1) * 8 + n + 1)
                    dve.tensor_tensor(prob_tile(n).rearrange("q (g k) -> q g k", g=4), bank,
                                      spread(top[:, n, :], 2, P), ALU.subtract).then_inc(shifted, 1)

            def norm_mix(b):
                st = Steps(dve, dve_steps, SET_STEPS + b * DVE_STEPS)
                for half in range(2):
                    bank = ps[:, Y_BANK[half], 0:272].rearrange("q (h d) -> q h d", h=16)
                    dve.wait_ge(mixed, b * 8 + 4 * half + 4)
                    st(dve.reciprocal(rden[:, half, :], bank[:, :, HD]))
                    st.wait()
                    if half == 0:
                        reused(dve, y_turned, b * 2)
                    dve.tensor_tensor(y[:, half * 256:(half + 1) * 256].rearrange("q (h d) -> q h d", h=16),
                                      bank[:, :, 0:HD], spread(rden[:, half, :], 2, HD), ALU.mult)\
                        .then_inc(y_normed, 1)
                dve.wait_ge(out_projected, b + 1)
                dve.wait_ge(resid_biased, b + 1)
                dve.tensor_tensor(z, ps[:, O_BANK, :], xr, ALU.add).then_inc(resid_added, 1)
                dve.wait_ge(resid_added, b + 1)
                norm_vector(dve, b, norm, st, z, stats, moments, rstd, out, stored)
                assert st.n == DVE_STEPS, st.n

            dve.memset(V[:, :, HD:HD + 1], 1.0).then_inc(consts_set, 1)
            make_tables()
            rope_products(0, 0)
            rope_products(0, 1)

            def body(b):
                shift(b, 0)
                rope_products(b + 1, 0)
                shift(b, 1)
                rope_products(b + 1, 1)
                norm_mix(b)

            over_sequences(dve, body)
            shift(LAST, 0)
            shift(LAST, 1)
            norm_mix(LAST)

        @block.gpsimd
        def _(pool):
            def rope_sum(b, c):
                pool.wait_ge(rope_parts, b * 2 + c + 1)
                reused(pool, qk_turned, b * 4)
                pool.tensor_tensor(qkp[:, c, :].rearrange("p (h a) -> p h a", h=HEADS)[:, :, 0:HD],
                                   tcos[:, c, :].rearrange("p (h a) -> p h a", h=HEADS),
                                   tsin[:, c, :].rearrange("p (h a) -> p h a", h=HEADS), ALU.add)\
                    .then_inc(roped, 1)

            def bias(b):
                pool.wait_ge(resid_loaded, (b + 1) * DMA)
                pool.tensor_tensor(xr, xr, bout, ALU.add).then_inc(resid_biased, 1)

            pool.memset(qkp, 0.0).then_inc(consts_set, 1)
            pool.wait_ge(consts_set, 2)
            pool.wait_ge(weights_loaded, 4 * DMA)
            rope_sum(0, 0)
            rope_sum(0, 1)

            def body(b):
                bias(b)
                rope_sum(b + 1, 0)
                rope_sum(b + 1, 1)
                norm_gpsimd(pool, b, norm, moments, rstd, minus_half)

            over_sequences(pool, body)
            bias(LAST)
            norm_gpsimd(pool, LAST, norm, moments, rstd, minus_half)


def over_pairs(eng, body):
    body(0, 0)
    with eng.Fori(0, (SEQS - 2) // 2) as i:
        body(i * 2 + 1, 1)
        body(i * 2 + 2, 0)


def stage_experts(nc, sem, ps, arena, const, weights, prefetch, src, dst, extra):
    E = 8
    QW = D // 4
    ident, minus_half = const["ident"], const["minus_half"]
    Wr, We_chunk, rbias, router_loaded, experts_loaded = weights

    r = Region(arena, const["work_c"])
    logits = [r.take(E, D) for _ in range(2)]
    rb = Region(arena, *extra).take(E, D)
    eb, cT = r.take(D), r.take(P)
    scaled_sb = r.take(D)
    ladder = r.at
    wide, narrow = r.take(E, QW), r.take(E, QW)
    r2 = Region(arena, ladder, r.at)
    mask, count = r2.take(2, D), r2.take(2, D)
    m1, m2, ex = r.take(D), r.take(D), r.take(D)
    w1 = r.take(D)
    w2, left = ex, m1
    xa, acc, out = r.take(D), r.take(D), r.take(D)
    xT = [r.take(KC, P) for _ in range(2)]
    c = [r.take(E) for _ in range(2)]
    part = r.take(2, E)
    stats, moments, rstd = r.take(6), r.take(3), r.take(1)

    x_loaded = sem("c_x_loaded")
    acc_loaded = sem("c_acc_loaded")
    bias_loaded = sem("c_bias_loaded")
    stored = sem("c_stored")
    x_turned = sem("c_x_turned")
    xT_copied = sem("c_xT_copied")
    routed = sem("c_routed")
    logits_copied = sem("c_logits_copied")
    logits_biased = sem("c_logits_biased")
    gap_ready = sem("c_gap_ready")
    gap_exp = sem("c_gap_exp")
    ties_found = sem("c_ties_found")
    ties_counted = sem("c_ties_counted")
    ties_kept = sem("c_ties_kept")
    first_weighed = sem("c_first_weighed")
    second_weighed = sem("c_second_weighed")
    first_totalled = sem("c_first_totalled")
    second_totalled = sem("c_second_totalled")
    c_ready = sem("c_c_ready")
    expert_ready = sem("c_expert_ready")
    expert_scaled = sem("c_expert_scaled")
    expert_summed = sem("c_expert_summed")
    c_turned = sem("c_c_turned")
    cT_copied = sem("c_cT_copied")
    bias_ready = sem("c_bias_ready")
    summed = sem("c_summed")
    dve_steps = sem("c_dve_steps")
    norm = NormSems(sem, "c")
    LAST = SEQS - 1
    R_BANK, E_BANK, X_BANK, C_BANK = 0, 4, 6, 7
    NORM_STEPS = 2

    def expert_bank(b, e):
        if isinstance(b, int) and b in (0, LAST):
            return (4, 5, 0, 1, 2, 3, 4, 5)[e]
        return E_BANK + e % 2

    with nc.Block() as block:
        @block.sync
        def _(sp):
            sp.dma_start(xa, row(src, 0)).then_inc(x_loaded, DMA)
            sp.dma_start(rb.rearrange("p e o -> p (e o)"), rbias[0].partition_broadcast(P)).then_inc(bias_loaded, DMA)
            sp.dma_start(eb[0:E, :], rbias[1]).then_inc(bias_loaded, DMA)
            prefetch[0](sp)
            sp.wait_ge(x_turned, 1)
            sp.dma_start(xa, row(src, 1)).then_inc(x_loaded, DMA)
            sp.dma_start(acc, row(src, 0)).then_inc(acc_loaded, DMA)

            def body(b, left):
                if left > 1:
                    sp.wait_ge(x_turned, b + 2)
                    sp.dma_start(xa, row(src, b + 2)).then_inc(x_loaded, DMA)
                sp.wait_ge(norm.out, b + 1)
                if left > 0:
                    sp.dma_start(acc, row(src, b + 1)).then_inc(acc_loaded, DMA)
                sp.dma_start(row(dst, b), out).then_inc(stored, DMA)

            with sp.Fori(0, SEQS - 2) as b:
                body(b, 2)
            body(SEQS - 2, 1)
            sp.wait_ge(routed, SEQS * E)
            prefetch[1](sp)
            body(LAST, 0)
            sp.wait_ge(stored, SEQS * DMA)

        @block.tensor
        def _(pe):
            def turn_x(b):
                pe.wait_ge(x_loaded, (b + 1) * DMA)
                reused(pe, xT_copied, b)
                turn(pe, ps[:, X_BANK, :], halves(xa), ident).then_inc(x_turned, 1)

            def route(b, par):
                pe.wait_ge(xT_copied, b + 1)
                for e in range(E):
                    reused(pe, logits_copied, b * E + e - 3)
                    if isinstance(b, int) and b == 2 and e < 4:
                        pe.wait_ge(expert_scaled, e + 3)
                    project(pe, ps[:, R_BANK + e % 4, :], lambda k: xT[par][:, k, :],
                            lambda k: Wr[:, k, e * D:(e + 1) * D], KC).then_inc(routed, 1)

            def experts(b, par, chosen):
                for e in chosen:
                    if expert_bank(b, e) < E_BANK:
                        pe.wait_ge(logits_copied, min(b + 2, SEQS) * E)
                    elif isinstance(b, int) and b in (0, LAST) and e >= 6:
                        pe.wait_ge(expert_scaled, b * E + e - 5)
                    else:
                        reused(pe, expert_scaled, b * E + e - 1)
                    project(pe, ps[:, expert_bank(b, e), :], lambda k: xT[par][:, k, :],
                            lambda k: We_chunk(k)[:, e * D:(e + 1) * D], KC).then_inc(expert_ready, 1)

            def turn_c(b, par):
                reused(pe, summed, b)
                pe.wait_ge(c_ready, b + 1)
                pe.transpose(ps[0:E, C_BANK, 0:P], c[par], ident).then_inc(c_turned, 1)

            def expert_bias(b):
                pe.wait_ge(cT_copied, b + 1)
                pe.matmul(ps[:, C_BANK, :], cT[0:E, :], eb[0:E, :], start=True, stop=True).then_inc(bias_ready, 1)

            pe.wait_ge(router_loaded, KC * DMA)
            turn_x(0)
            route(0, 0)
            turn_x(1)
            pe.wait_ge(experts_loaded, KC * DMA)
            pe.wait_ge(bias_loaded, 2 * DMA)

            def body(b, par, turns=True):
                route(b + 1, 1 - par)
                experts(b, par, range(6))
                if turns:
                    turn_x(b + 2)
                turn_c(b, par)
                experts(b, par, range(6, E))
                expert_bias(b)

            body(0, 0)
            body(1, 1)
            body(2, 0)
            with pe.Fori(1, (SEQS - 4) // 2) as i:
                body(i * 2 + 1, 1)
                body(i * 2 + 2, 0)
            body(SEQS - 3, 1)
            body(SEQS - 2, 0, turns=False)
            experts(LAST, 1, range(E))
            turn_c(LAST, 1)
            expert_bias(LAST)

        @block.scalar
        def _(act):
            def copy_xT(b, par):
                act.wait_ge(x_turned, b + 1)
                reused(act, expert_ready, (b - 1) * E)
                act.activation(xT[par], ps[:, X_BANK, :].rearrange("p (a b) -> p a b", a=KC), ACT.Copy)\
                    .then_inc(xT_copied, 1)

            def copy_logits(b, par, e):
                act.wait_ge(routed, b * E + e + 1)
                if e == 0:
                    reused(act, c_ready, b - 1)
                act.activation(logits[par][:, e, :], ps[:, R_BANK + e % 4, :], ACT.Copy)\
                    .then_inc(logits_copied, 1)

            def total(b, par, e):
                if e < E:
                    act.wait_ge(first_weighed, b * E + e + 1)
                    if e == 0:
                        reused(act, c_ready, b)
                    act.activation(mask[:, e % 2, :], mask[:, e % 2, :], ACT.Copy, accum_out=part[:, 0, e:e + 1])\
                        .then_inc(first_totalled, 1)
                if e:
                    act.wait_ge(second_weighed, b * E + e)
                    tile = logits[par][:, e - 1, :]
                    act.activation(tile, tile, ACT.Copy, accum_out=part[:, 1, e - 1:e]).then_inc(second_totalled, 1)

            def scale(b, par, e):
                act.wait_ge(expert_ready, b * E + e + 1)
                if e == 0:
                    act.wait_ge(c_ready, b + 1)
                reused(act, expert_summed, b * E + e)
                act.activation(scaled_sb, ps[:, expert_bank(b, e), :], ACT.Copy, scale=c[par][:, e:e + 1])\
                    .then_inc(expert_scaled, 1)

            def exp_gap(b):
                act.wait_ge(gap_ready, b + 1)
                act.activation(ex, ex, ACT.Exp).then_inc(gap_exp, 1)

            def copy_cT(b):
                act.wait_ge(c_turned, b + 1)
                reused(act, bias_ready, b)
                act.activation(cT[0:E, :], ps[0:E, C_BANK, 0:P], ACT.Copy).then_inc(cT_copied, 1)

            copy_xT(0, 0)
            for e in range(E):
                copy_logits(0, 0, e)
            copy_xT(1, 1)

            def body(b, par, turns=True):
                if isinstance(b, int) and b == 0:
                    for e in range(E):
                        if e == 4:
                            exp_gap(0)
                        if e >= 6:
                            total(0, 0, e - 6)
                        copy_logits(1, 1, e)
                    for n in range(2, E + 1):
                        total(0, 0, n)
                else:
                    for e, sums in enumerate(((2,), (3,), (), (4,), (5,), (6,), (7,), (8,))):
                        for n in sums:
                            total(b, par, n)
                        copy_logits(b + 1, 1 - par, e)
                for e in range(5):
                    scale(b, par, e)
                exp_gap(b + 1)
                scale(b, par, 5)
                if turns:
                    copy_xT(b + 2, par)
                copy_cT(b)
                total(b + 1, 1 - par, 0)
                scale(b, par, 6)
                total(b + 1, 1 - par, 1)
                scale(b, par, 7)

            body(0, 0)
            with act.Fori(0, (SEQS - 4) // 2) as i:
                body(i * 2 + 1, 1)
                body(i * 2 + 2, 0)
            body(SEQS - 3, 1)
            body(SEQS - 2, 0, turns=False)
            for n in range(2, E + 1):
                total(LAST, 1, n)
            for e in range(E):
                scale(LAST, 1, e)
            copy_cT(LAST)

        @block.vector
        def _(dve):
            def find_top(b, par, st):
                dve.wait_ge(logits_biased, b * E + E)
                for q in range(4):
                    cols = slice(q * QW, (q + 1) * QW)
                    lg = logits[par][:, :, cols].rearrange("p (a s) o -> p a s o", s=2)
                    st.wait()
                    st(dve.tensor_tensor(wide[:, 0:4, :], lg[:, :, 0, :], lg[:, :, 1, :], ALU.max))
                    st(dve.tensor_tensor(wide[:, 4:8, :], lg[:, :, 0, :], lg[:, :, 1, :], ALU.min))
                    st.wait()
                    hi = wide[:, 0:4, :].rearrange("p (a s) o -> p a s o", s=2)
                    lo = wide[:, 4:8, :].rearrange("p (a s) o -> p a s o", s=2)
                    st(dve.tensor_tensor(narrow[:, 2:4, :], hi[:, :, 0, :], hi[:, :, 1, :], ALU.min))
                    st(dve.tensor_tensor(narrow[:, 4:6, :], lo[:, :, 0, :], lo[:, :, 1, :], ALU.max))
                    st(dve.tensor_tensor(narrow[:, 0:2, :], hi[:, :, 0, :], hi[:, :, 1, :], ALU.max))
                    st.wait()
                    dve.tensor_tensor(narrow[:, 6:8, :], narrow[:, 2:4, :], narrow[:, 4:6, :], ALU.max)\
                        .then_inc(st.sem, 1)
                    st.n += 1
                    dve.tensor_tensor(m1[:, cols], narrow[:, 0, :], narrow[:, 1, :], ALU.max)
                    st.wait()
                    dve.tensor_tensor(narrow[:, 2, :], narrow[:, 0, :], narrow[:, 1, :], ALU.min)
                    st(dve.tensor_tensor(narrow[:, 4, :], narrow[:, 6, :], narrow[:, 7, :], ALU.max))
                    st.wait()
                    st(dve.tensor_tensor(m2[:, cols], narrow[:, 2, :], narrow[:, 4, :], ALU.max))
                st.wait()
                dve.tensor_tensor(ex, m2, m1, ALU.subtract).then_inc(gap_ready, 1)

            def weights(b, st):
                st.wait()
                st(dve.tensor_tensor(left, m1, m2, ALU.is_gt))
                st.wait()
                dve.tensor_scalar(left, left, -1.0, 2.0, ALU.mult, ALU.add).then_inc(st.sem, 1)
                st.n += 1
                dve.wait_ge(gap_exp, b + 1)
                st(dve.tensor_scalar(w1, ex, 1.0, None, ALU.add))
                st.wait()
                st(dve.reciprocal(w1, w1))
                st.wait()
                st(dve.tensor_tensor(w2, ex, w1, ALU.mult))

            def compare(b, par, e, st):
                lg = logits[par][:, e, :]
                if e >= 2:
                    dve.wait_ge(first_totalled, b * E + e - 1)
                st(dve.tensor_tensor(mask[:, e % 2, :], lg, m2, ALU.is_gt))
                st.wait()
                dve.tensor_tensor(lg, lg, m2, ALU.is_equal).then_inc(ties_found, 1)
                dve.tensor_tensor(mask[:, e % 2, :], mask[:, e % 2, :], w1, ALU.mult).then_inc(first_weighed, 1)

            def keep(b, par, e):
                lg = logits[par][:, e, :]
                dve.wait_ge(ties_counted, b * E + e + 1)
                dve.scalar_tensor_tensor(lg, count[:, e % 2, :], 0.0, lg, ALU.is_ge, ALU.mult).then_inc(ties_kept, 1)
                dve.wait_ge(ties_kept, b * E + e + 1)
                dve.tensor_tensor(lg, lg, w2, ALU.mult).then_inc(second_weighed, 1)

            def choose(b, par, first, last, st):
                for e in range(first, last):
                    if e < E:
                        compare(b, par, e, st)
                    if e:
                        keep(b, par, e - 1)

            def finish_c(b, par):
                reused(dve, expert_scaled, (b - 1) * E)
                reused(dve, c_turned, b - 1)
                dve.wait_ge(first_totalled, b * E + E)
                dve.wait_ge(second_totalled, b * E + E)
                dve.tensor_tensor(c[par], part[:, 0, :], part[:, 1, :], ALU.add).then_inc(c_ready, 1)

            def normalise(b, steps):
                dve.wait_ge(bias_ready, b + 1)
                dve.wait_ge(expert_summed, b * E + E)
                dve.tensor_tensor(acc, acc, ps[:, C_BANK, :], ALU.add).then_inc(summed, 1)
                dve.wait_ge(summed, b + 1)
                norm_vector(dve, b, norm, steps, acc, stats, moments, rstd, out, stored)

            st = Steps(dve, dve_steps, 0)
            find_top(0, 0, st)
            weights(0, st)
            choose(0, 0, 0, E + 1, st)
            finish_c(0, 0)
            per_top = st.n

            def body(b, par):
                st = Steps(dve, dve_steps, per_top + b * (per_top + NORM_STEPS))
                dve.wait_ge(first_totalled, b * E + E)
                dve.wait_ge(ties_kept, b * E + E)
                find_top(b + 1, 1 - par, st)
                weights(b + 1, st)
                choose(b + 1, 1 - par, 0, 4, st)
                normalise(b, st)
                choose(b + 1, 1 - par, 4, E + 1, st)
                finish_c(b + 1, 1 - par)
                assert st.n == per_top + NORM_STEPS, st.n

            over_pairs(dve, body)
            normalise(LAST, Steps(dve, dve_steps, per_top + LAST * (per_top + NORM_STEPS)))

        @block.gpsimd
        def _(pool):
            def add_bias(b, par, e):
                pool.wait_ge(logits_copied, b * E + e + 1)
                pool.tensor_tensor(logits[par][:, e, :], logits[par][:, e, :], rb[:, e, :], ALU.add)\
                    .then_inc(logits_biased, 1)

            def add_expert(b, e):
                pool.wait_ge(expert_scaled, b * E + e + 1)
                if e == 0:
                    pool.wait_ge(acc_loaded, (b + 1) * DMA)
                else:
                    pool.wait_ge(expert_summed, b * E + e)
                pool.tensor_tensor(acc, acc, scaled_sb, ALU.add).then_inc(expert_summed, 1)

            def count_ties(b, par, e):
                pool.wait_ge(ties_found, b * E + e + 1)
                if e >= 2:
                    pool.wait_ge(ties_kept, b * E + e - 1)
                if e:
                    pool.wait_ge(ties_counted, b * E + e)
                pool.tensor_tensor(count[:, e % 2, :], count[:, (e - 1) % 2, :] if e else left, logits[par][:, e, :],
                                   ALU.subtract).then_inc(ties_counted, 1)

            pool.wait_ge(bias_loaded, 2 * DMA)
            for e in range(E):
                add_bias(0, 0, e)
            for e in range(E):
                count_ties(0, 0, e)

            def body(b, par):
                for e in range(E):
                    add_bias(b + 1, 1 - par, e)
                for e in range(6):
                    add_expert(b, e)
                count_ties(b + 1, 1 - par, 0)
                add_expert(b, 6)
                count_ties(b + 1, 1 - par, 1)
                add_expert(b, 7)
                count_ties(b + 1, 1 - par, 2)
                count_ties(b + 1, 1 - par, 3)
                norm_gpsimd(pool, b, norm, moments, rstd, minus_half)
                for e in range(4, E):
                    count_ties(b + 1, 1 - par, e)

            over_pairs(pool, body)
            for e in range(E):
                add_expert(LAST, e)
            norm_gpsimd(pool, LAST, norm, moments, rstd, minus_half)


def stage_selective_scan(nc, sem, ps, arena, const, weights, prefetch, src, dst, bc_dram):
    GROUPS, G, SPAN = 8, 2, 256
    JT, N, CH = 8, 16, 8
    UNITS = JT * N // CH
    TAPS = 4
    ident, minus_half = const["ident"], const["minus_half"]
    W_skip, W_in, Wd1, Wd2, Wbc, W_out, params, weights_loaded, region = weights

    r = Region(arena, *region[0])
    xs = [r.take(JT, SPAN) for _ in range(2)]
    dl = [r.take(JT, SPAN) for _ in range(2)]
    sk = [r.take(JT, SPAN) for _ in range(2)]
    Bb, Cb = [r.take(CH, SPAN) for _ in range(2)], [r.take(CH, SPAN) for _ in range(2)]
    r1 = Region(arena, *region[1])
    xa = [r1.take(D) for _ in range(G)]
    th = [r1.take(SPAN) for _ in range(2)]
    d1 = r1.take(SPAN)
    r2 = Region(arena, *region[2])
    decay = [r2.take(CH, SPAN) for _ in range(2)]
    state = [r2.take(CH, SPAN) for _ in range(2)]
    dx, yacc = r2.take(JT, SPAN), r2.take(JT, SPAN)
    xnT = r2.take(KC, SPAN)
    soft = r2.take(KC, SPAN)
    xp = [r2.take(G, TOK + TAPS - 1) for _ in range(2)]
    xr, out = r2.take(D), r2.take(D)
    conv_at = r2.at
    conv_w, conv_b, b_delta = r2.take(JT, TAPS), r2.take(JT), r2.take(JT)
    A, W_D, norm_w = r2.take(JT, N), r2.take(JT), r2.take(KC)
    stats, moments, rstd = r2.take(6), r2.take(3), r2.take(1)
    xstats, xmoments, xrms = r2.take(G, 6), r2.take(G, 3), r2.take(G, 1)
    bc = soft[0:2 * N, 0, :]
    soft_part = [soft[:, 2:4, :], soft[:, 0:2, :]]
    OUTS = {2: (0, 0), 4: (0, 1), 6: (1, 0), 7: (1, 1)}
    SKIPS = {10: (0,), 11: (1, 2), 12: (3, 4), 13: (5, 6), 14: (7,)}

    x_loaded = [sem(f"d_x{s}_loaded") for s in range(G)]
    params_loaded = sem("d_params_loaded")
    params_set = sem("d_params_set")
    resid_loaded = sem("d_resid_loaded")
    stored = sem("d_stored")
    bc_stored = sem("d_bc_stored")
    bc_written = sem("d_bc_written")
    b_spread = [sem(f"d_b{c}_spread") for c in range(2)]
    c_spread = [sem(f"d_c{c}_spread") for c in range(2)]
    xstat_steps = sem("d_xstat_steps")
    square_ready = sem("d_square_ready")
    xrms_ready = sem("d_xrms_ready")
    x_scaled = sem("d_x_scaled")
    x_turned = sem("d_x_turned")
    xnT_copied = sem("d_xnT_copied")
    in_projected = sem("d_in_projected")
    in_copied = sem("d_in_copied")
    conv_steps = sem("d_conv_steps")
    convolved = sem("d_convolved")
    x_tanh = sem("d_x_tanh")
    x_gated = sem("d_x_gated")
    skip_projected = sem("d_skip_projected")
    skip_tanh = sem("d_skip_tanh")
    skip_gated = sem("d_skip_gated")
    low_projected = sem("d_low_projected")
    low_copied = sem("d_low_copied")
    delta_projected = sem("d_delta_projected")
    delta_copied = sem("d_delta_copied")
    soft_steps = sem("d_soft_steps")
    soft_ready = sem("d_soft_ready")
    delta_ready = sem("d_delta_ready")
    dx_ready = sem("d_dx_ready")
    decays_ready = sem("d_decays_ready")
    inputs_ready = sem("d_inputs_ready")
    scanned = sem("d_scanned")
    weighed = sem("d_weighed")
    y_summed = sem("d_y_summed")
    y_added = sem("d_y_added")
    gated = sem("d_gated")
    out_projected = sem("d_out_projected")
    resid_doubled = sem("d_resid_doubled")
    resid_added = sem("d_resid_added")
    norm_steps = sem("d_norm_steps")
    norm = NormSems(sem, "d")

    Y_BANK, IN_BANK, SKIP_BANK, LOW_BANK, X_BANK, O_BANK = [0, 1], [2, 3], [4, 5], 6, [6, 7], [4, 5]

    def over_groups(eng, body):
        body(0, 0, True, True, False)
        body(1, 1, True, True, True)
        with eng.Fori(0, (GROUPS - 4) // 2) as i:
            body(i * 2 + 2, 0, True, True, True)
            body(i * 2 + 3, 1, True, True, True)
        body(6, 0, True, False, True)
        body(7, 1, False, False, True)

    with nc.Block() as block:
        @block.sync
        def _(sp):
            def load_x(g, s):
                reused(sp, x_turned, g * G - G + s + 1)
                sp.dma_start(xa[s], row(src, g * G + s)).then_inc(x_loaded[s], DMA)

            def load_resid(b):
                reused(sp, norm.out, b)
                sp.dma_start(xr, row(src, b)).then_inc(resid_loaded, DMA)

            def store(b):
                sp.wait_ge(norm.out, b + 1)
                sp.dma_start(row(dst, b), out).then_inc(stored, DMA)

            def spread_bc(g, c):
                if c == 0:
                    sp.wait_ge(low_copied, g * 2 + 2)
                    sp.dma_start(bc_dram[bass.ds(g, 1), :, :].rearrange("a n t -> (a n) t"), bc)\
                        .then_inc(bc_stored, DMA)
                    sp.wait_ge(bc_stored, (g + 1) * DMA)
                    sp.sem_inc(bc_written, 1)
                for tile, first, done, users in ((Bb[c], 0, b_spread[c], inputs_ready), (Cb[c], N, c_spread[c], weighed)):
                    reused(sp, users, g * UNITS - UNITS + (c + 1) * JT)
                    rows = bc_dram[bass.ds(g, 1), first + c * CH:first + (c + 1) * CH, :]
                    sp.dma_start(tile.rearrange("p n t -> p (n t)"),
                                 rows.rearrange("a n t -> (a n t)").partition_broadcast(P)).then_inc(done, DMA)

            sp.dma_start(xa[0], row(src, 0)).then_inc(x_loaded[0], DMA)
            sp.dma_start(xa[1], row(src, 1)).then_inc(x_loaded[1], DMA)
            for tile, name in ((conv_w, "conv_w"), (conv_b, "conv_b"), (b_delta, "b_delta"), (A, "A_log"),
                               (W_D, "W_D"), (norm_w, "norm_w")):
                sp.dma_start(tile, params[name]).then_inc(params_loaded, DMA)
            load_x(1, 0)
            load_x(1, 1)
            spread_bc(0, 0)
            spread_bc(0, 1)

            def body(g, par, next, next2, prev):
                if prev:
                    load_resid(g * G - G)
                if next2:
                    load_x(g + 2, 0)
                    load_x(g + 2, 1)
                if prev:
                    load_resid(g * G - G + 1)
                    store(g * G - G)
                if next:
                    spread_bc(g + 1, 0)
                if prev:
                    store(g * G - G + 1)
                if next:
                    spread_bc(g + 1, 1)

            body(0, 0, True, True, False)
            body(1, 1, True, True, True)
            with sp.Fori(0, (GROUPS - 4) // 2) as i:
                body(i * 2 + 2, 0, True, True, True)
                body(i * 2 + 3, 1, True, True, True)
            body(6, 0, True, False, True)
            sp.wait_ge(skip_projected, GROUPS * JT)
            prefetch[0](sp)
            body(7, 1, False, False, True)
            sp.wait_ge(weighed, GROUPS * UNITS)
            sp.wait_ge(y_added, GROUPS * UNITS - JT)
            load_resid(SEQS - 2)
            sp.wait_ge(x_turned, SEQS)
            sp.wait_ge(resid_loaded, (SEQS - 1) * DMA)
            sp.dma_start(xa[1], row(src, SEQS - 1)).then_inc(resid_loaded, DMA)
            prefetch[1](sp)
            store(SEQS - 2)
            store(SEQS - 1)
            sp.wait_ge(stored, SEQS * DMA)

        @block.tensor
        def _(pe):
            def turn_x(g):
                for s in range(G):
                    pe.wait_ge(x_scaled, g * G + s + 1)
                    reused(pe, xnT_copied, g * G)
                    reused(pe, low_copied, g * 2)
                    turn(pe, ps[:, X_BANK[s], :], halves(xa[s]), ident).then_inc(x_turned, 1)

            def project_in(g, j):
                pe.wait_ge(xnT_copied, g * G + G)
                if j < 2:
                    reused(pe, delta_copied, g * JT)
                else:
                    pe.wait_ge(in_copied, g * JT + j - 1)
                project(pe, ps[:, IN_BANK[j % 2], 0:SPAN], lambda k: W_in[:, k, j * P:(j + 1) * P],
                        lambda k: xnT[:, k, :], KC).then_inc(in_projected, 1)

            def project_skip(g, j):
                reused(pe, skip_gated, g * JT + j - 1)
                if j < 2:
                    reused(pe, resid_added, (g - 2) * G + j + 1)
                project(pe, ps[:, SKIP_BANK[j % 2], 0:SPAN], lambda k: W_skip[:, k, j * P:(j + 1) * P],
                        lambda k: xnT[:, k, :], KC).then_inc(skip_projected, 1)

            def project_low(g, par):
                pe.wait_ge(x_gated, g * JT + JT)
                pe.wait_ge(xnT_copied, g * G + G)
                project(pe, ps[:, LOW_BANK, 0:SPAN], lambda k: Wd1[:, k, :], lambda k: xs[par][:, k, :], JT)\
                    .then_inc(low_projected, 1)

            def project_bc(g, par):
                pe.wait_ge(low_copied, g * 2 + 1)
                project(pe, ps[0:2 * N, LOW_BANK, SPAN:2 * SPAN], lambda k: Wbc[:, k, :],
                        lambda k: xs[par][:, k, :], JT).then_inc(low_projected, 1)

            def project_delta(g, k):
                pe.wait_ge(low_copied, g * 2 + 1)
                pe.wait_ge(in_copied, g * JT + JT)
                if k >= 2:
                    pe.wait_ge(delta_copied, g * JT + 2 * k - 2)
                for i in range(2):
                    j = 2 * k + i
                    pe.matmul(ps[:, IN_BANK[k % 2], i * SPAN:(i + 1) * SPAN], Wd2[:, j * P:(j + 1) * P], d1,
                              start=True, stop=True).then_inc(delta_projected, 1)

            def sum_states(g, u):
                pe.wait_ge(weighed, g * UNITS + u + 1)
                reused(pe, y_added, g * UNITS + u - 1)
                project(pe, ps[:, Y_BANK[u % 2], 0:SPAN], lambda n: ident, lambda n: state[u % 2][:, n, :], CH)\
                    .then_inc(y_summed, 1)

            def project_out(g, s, par, groups_ahead, half):
                if half == 0:
                    pe.wait_ge(gated, g * JT + JT)
                    pe.wait_ge(skip_gated, (g + groups_ahead + 1) * JT)
                for k in range(half * JT // 2, (half + 1) * JT // 2):
                    last = pe.matmul(ps[:, O_BANK[s], :], sk[par][:, k, s * TOK:(s + 1) * TOK], W_out[:, k, :],
                                     start=(k == 0), stop=(k == JT - 1))
                if half:
                    last.then_inc(out_projected, 1)

            pe.wait_ge(weights_loaded, 7 * DMA)
            turn_x(0)
            for j in range(JT):
                project_in(0, j)
            for j in range(2):
                project_skip(0, j)
            project_low(0, 0)
            project_bc(0, 0)
            for k in range(4):
                project_delta(0, k)
            for j in range(2, JT):
                project_skip(0, j)
            turn_x(1)
            project_in(1, 0)
            project_in(1, 1)

            def body(g, par, next, next2, prev):
                for u in range(UNITS):
                    if next and u in (1, 3, 5):
                        project_in(g + 1, u + 1)
                        project_in(g + 1, u + 2)
                    if next2 and u == UNITS - 1:
                        project_in(g + 2, 0)
                        project_in(g + 2, 1)
                    if prev and u in OUTS:
                        s, half = OUTS[u]
                        project_out(g - 1, s, 1 - par, 1, half)
                    if next:
                        if u == 8:
                            project_low(g + 1, 1 - par)
                        if u == 9:
                            project_bc(g + 1, 1 - par)
                        if u in (9, 10):
                            project_delta(g + 1, 2 * u - 18)
                            project_delta(g + 1, 2 * u - 17)
                        for j in SKIPS.get(u, ()):
                            project_skip(g + 1, j)
                    if next2 and u == 14:
                        turn_x(g + 2)
                    sum_states(g, u)

            over_groups(pe, body)
            pe.wait_ge(resid_added, (GROUPS - 1) * G)
            for s in range(G):
                project_out(GROUPS - 1, s, 1, 0, 0)
                project_out(GROUPS - 1, s, 1, 0, 1)

        @block.scalar
        def _(act):
            def copy_xnT(g):
                for s in range(G):
                    act.wait_ge(x_turned, g * G + s + 1)
                    reused(act, skip_projected, g * JT)
                    for k in range(KC):
                        last = act.activation(xnT[:, k, s * TOK:(s + 1) * TOK], ps[:, X_BANK[s], k * P:(k + 1) * P],
                                              ACT.Copy, scale=norm_w[:, k:k + 1])
                    last.then_inc(xnT_copied, 1)

            def copy_in(g, j):
                act.wait_ge(in_projected, g * JT + j + 1)
                reused(act, convolved, g * JT + j - 1)
                act.activation(xp[j % 2][:, :, TAPS - 1:], ps[:, IN_BANK[j % 2], 0:SPAN]
                               .rearrange("p (s t) -> p s t", s=G), ACT.Copy).then_inc(in_copied, 1)

            def tanh_x(g, par, j):
                act.wait_ge(convolved, g * JT + j + 1)
                reused(act, x_gated, g * JT + j - 1)
                act.activation(th[j % 2], xs[par][:, j, :], ACT.Tanh).then_inc(x_tanh, 1)

            def tanh_skip(g, par, j):
                act.wait_ge(skip_projected, g * JT + j + 1)
                reused(act, out_projected, (g - 1) * G)
                act.activation(sk[par][:, j, :], ps[:, SKIP_BANK[j % 2], 0:SPAN], ACT.Tanh, scale=0.5)\
                    .then_inc(skip_tanh, 1)

            def copy_low(g):
                act.wait_ge(low_projected, g * 2 + 1)
                reused(act, delta_projected, g * JT)
                act.activation(d1, ps[:, LOW_BANK, 0:SPAN], ACT.Copy).then_inc(low_copied, 1)

            def copy_bc(g):
                act.wait_ge(low_projected, g * 2 + 2)
                reused(act, delta_ready, g * 4)
                reused(act, bc_stored, g * DMA)
                act.activation(bc, ps[0:2 * N, LOW_BANK, SPAN:2 * SPAN], ACT.Copy).then_inc(low_copied, 1)

            def copy_delta(g, par, k):
                for j in (2 * k, 2 * k + 1):
                    act.wait_ge(delta_projected, g * JT + 2 * k + 2)
                    reused(act, dx_ready, (g - 1) * JT)
                    reused(act, decays_ready, (g - 1) * UNITS)
                    act.activation(dl[par][:, j, :], ps[:, IN_BANK[k % 2], (j % 2) * SPAN:(j % 2 + 1) * SPAN],
                                   ACT.Identity, bias=b_delta[:, j:j + 1]).then_inc(delta_copied, 1)

            def soft_log(g, par, h):
                st = Steps(act, soft_steps, g * 8 + h * 4)
                act.wait_ge(delta_copied, g * JT + 4 * h + 4)
                act.wait_ge(bc_stored, (g + 1) * DMA)
                reused(act, delta_ready, g * 4 + 2 * h)
                for i in range(2):
                    k = 2 * h + i
                    st(act.activation(soft_part[i], dl[par][:, 2 * k:2 * k + 2, :], ACT.Abs))
                st.wait()
                for i in range(2):
                    st(act.activation(soft_part[i], soft_part[i], ACT.Exp, scale=-1.0))
                st.wait()
                for i in range(2):
                    act.activation(soft_part[i], soft_part[i], ACT.Ln, bias=1.0).then_inc(soft_ready, 1)

            def decays(g, par, u):
                j, c = u % JT, u // JT
                if u == 0:
                    act.wait_ge(delta_ready, g * 4 + 4)
                reused(act, scanned, g * UNITS + u - 1)
                for n in range(CH):
                    last = act.activation(
                        decay[u % 2][:, n, :].rearrange("p (s t) -> p s t", s=G)[:, :, 1:],
                        dl[par][:, j, :].rearrange("p (s t) -> p s t", s=G)[:, :, 1:], ACT.Exp,
                        scale=A[:, j, c * CH + n:c * CH + n + 1])
                last.then_inc(decays_ready, 1)

            act.wait_ge(params_loaded, 6 * DMA)
            act.activation(A, A, ACT.Exp).then_inc(params_set, 1)
            copy_xnT(0)
            for k in range(4):
                copy_in(0, 2 * k)
                copy_in(0, 2 * k + 1)
                if k:
                    tanh_x(0, 0, 2 * k - 2)
                    tanh_x(0, 0, 2 * k - 1)
            tanh_x(0, 0, 6)
            tanh_x(0, 0, 7)
            for j in range(2):
                tanh_skip(0, 0, j)
            copy_low(0)
            copy_bc(0)
            for k in range(4):
                copy_delta(0, 0, k)
            soft_log(0, 0, 0)
            soft_log(0, 0, 1)
            act.wait_ge(params_set, 7)
            decays(0, 0, 0)
            for j in range(2, JT):
                tanh_skip(0, 0, j)
            copy_xnT(1)
            copy_in(1, 0)
            copy_in(1, 1)

            def body(g, par, next, next2, prev):
                for u in range(UNITS):
                    if u < UNITS - 1:
                        decays(g, par, u + 1)
                    elif next:
                        decays(g + 1, 1 - par, 0)
                    if next:
                        if u in (1, 3, 5, 7):
                            tanh_x(g + 1, 1 - par, u - 1)
                            tanh_x(g + 1, 1 - par, u)
                        if u in (1, 3, 5):
                            copy_in(g + 1, u + 1)
                            copy_in(g + 1, u + 2)
                        if u == 8:
                            copy_low(g + 1)
                        if u == 9:
                            copy_bc(g + 1)
                        if u in (9, 10):
                            copy_delta(g + 1, 1 - par, 2 * u - 18)
                            copy_delta(g + 1, 1 - par, 2 * u - 17)
                        for j in SKIPS.get(u, ()):
                            tanh_skip(g + 1, 1 - par, j)
                        if u in (11, 13):
                            soft_log(g + 1, 1 - par, u // 2 - 5)
                    if next2 and u == 14:
                        copy_xnT(g + 2)
                    if next2 and u == UNITS - 1:
                        copy_in(g + 2, 0)
                        copy_in(g + 2, 1)

            over_groups(act, body)

        @block.vector
        def _(dve):
            def x_moments(g):
                for s in range(G):
                    b = g * G + s
                    st = Steps(dve, xstat_steps, b * 3)
                    dve.wait_ge(x_loaded[s], (g + 1) * DMA)
                    st(dve.bn_stats(xstats[:, s, :], xa[s]))
                    st.wait()
                    dve.memset(xmoments[:, s, 2:3], 0.0)
                    st(dve.bn_aggr(xmoments[:, s, 0:2], xstats[:, s, :]))
                    st.wait()
                    st(dve.scalar_tensor_tensor(xmoments[:, s, 0:1], xmoments[:, s, 0:1], xmoments[:, s, 0:1],
                                                xmoments[:, s, 1:2], ALU.mult, ALU.add))
                    st.wait()
                    dve.tensor_scalar(xmoments[:, s, 0:1], xmoments[:, s, 0:1], EPS, None, ALU.add)\
                        .then_inc(square_ready, 1)

            def scale_x(g):
                for s in range(G):
                    b = g * G + s
                    dve.wait_ge(xrms_ready, b + 1)
                    dve.tensor_scalar(xa[s], xa[s], xrms[:, s, :], None, ALU.mult).then_inc(x_scaled, 1)

            def convolve(g, par, k):
                for i in range(TAPS):
                    for j in (2 * k, 2 * k + 1):
                        tile = xs[par][:, j, :].rearrange("p (s t) -> p s t", s=G)
                        taps = xp[j % 2][:, :, i:i + TOK]
                        if i == 0:
                            dve.wait_ge(in_copied, g * JT + j + 1)
                            reused(dve, dx_ready, (g - 1) * JT)
                            reused(dve, y_added, (g - 1) * UNITS)
                            ins = dve.tensor_scalar(tile, taps, conv_w[:, j, 0:1], conv_b[:, j:j + 1],
                                                    ALU.mult, ALU.add)
                        else:
                            dve.wait_ge(conv_steps, g * 24 + k * 6 + (i - 1) * 2 + j % 2 + 1)
                            ins = dve.scalar_tensor_tensor(tile, taps, conv_w[:, j, i:i + 1], tile,
                                                           ALU.mult, ALU.add)
                        ins.then_inc(convolved if i == TAPS - 1 else conv_steps, 1)

            def gate_x(g, par, k):
                for j in (2 * k, 2 * k + 1):
                    dve.wait_ge(x_tanh, g * JT + j + 1)
                    dve.scalar_tensor_tensor(xs[par][:, j, :], th[j % 2], 1.0, xs[par][:, j, :], ALU.add, ALU.mult)\
                        .then_inc(x_gated, 1)

            def gate_skip(g, par, j):
                dve.wait_ge(skip_tanh, g * JT + j + 1)
                dve.scalar_tensor_tensor(sk[par][:, j, :], sk[par][:, j, :], 1.0,
                                         ps[:, SKIP_BANK[j % 2], 0:SPAN], ALU.add, ALU.mult).then_inc(skip_gated, 1)

            def softplus(g, par, k):
                dve.wait_ge(soft_ready, g * 4 + k + 1)
                part = dl[par][:, 2 * k:2 * k + 2, :]
                dve.scalar_tensor_tensor(part, part, 0.0, soft_part[k % 2], ALU.max, ALU.add).then_inc(delta_ready, 1)

            def scan(g, u):
                c = u // JT
                dve.wait_ge(decays_ready, g * UNITS + u + 1)
                dve.wait_ge(inputs_ready, g * UNITS + u + 1)
                flat = state[u % 2].rearrange("p n t -> p (n t)")
                dve.tensor_tensor_scan(flat, decay[u % 2].rearrange("p n t -> p (n t)"), flat, 0.0,
                                       ALU.mult, ALU.add).then_inc(scanned, 1)
                dve.wait_ge(scanned, g * UNITS + u + 1)
                if u % JT == 0:
                    dve.wait_ge(c_spread[c], (g + 1) * DMA)
                dve.tensor_tensor(state[u % 2], state[u % 2], Cb[c], ALU.mult).then_inc(weighed, 1)

            def add_y(g, par, u):
                j = u % JT
                dve.wait_ge(y_summed, g * UNITS + u + 1)
                if u < JT:
                    reused(dve, gated, g * JT - JT + j + 1)
                    ins = dve.scalar_tensor_tensor(yacc[:, j, :], xs[par][:, j, :], W_D[:, j:j + 1],
                                                   ps[:, Y_BANK[u % 2], 0:SPAN], ALU.mult, ALU.add)
                else:
                    dve.wait_ge(y_added, g * UNITS + u - JT + 1)
                    ins = dve.tensor_tensor(yacc[:, j, :], yacc[:, j, :], ps[:, Y_BANK[u % 2], 0:SPAN], ALU.add)
                ins.then_inc(y_added, 1)

            def normalise(b, s, xr=xr):
                st = Steps(dve, norm_steps, b * 2)
                dve.wait_ge(out_projected, b + 1)
                dve.wait_ge(resid_doubled, b + 1)
                dve.scalar_tensor_tensor(xr, ps[:, O_BANK[s], :], 0.5, xr, ALU.mult, ALU.add)\
                    .then_inc(resid_added, 1)
                dve.wait_ge(resid_added, b + 1)
                norm_moments(dve, norm, st, xr, stats, moments)

            def finish_norm(b, xr=xr):
                norm_apply(dve, b, norm, xr, moments, rstd, out, stored)

            for k in range(2):
                dve.memset(xp[k][:, :, 0:TAPS - 1], 0.0).then_inc(params_set, 1)
                dve.memset(decay[k].rearrange("p n (s t) -> p (n s) t", s=G)[:, :, 0:1], 0.0).then_inc(params_set, 1)
            x_moments(0)
            dve.wait_ge(params_loaded, 6 * DMA)
            pair = arena[:, conv_at:conv_at + JT * TAPS + JT]
            dve.tensor_scalar(pair, pair, 0.5, None, ALU.mult).then_inc(params_set, 1)
            dve.wait_ge(params_set, 6)
            dve.tensor_scalar(A, A, -1.0, None, ALU.mult).then_inc(params_set, 1)
            dve.wait_ge(params_set, 7)
            scale_x(0)
            for k in range(4):
                convolve(0, 0, k)
                if k:
                    gate_x(0, 0, k - 1)
            gate_x(0, 0, 3)
            for j in range(2):
                gate_skip(0, 0, j)
            x_moments(1)
            scale_x(1)
            for k in range(4):
                softplus(0, 0, k)
            for j in range(2, JT):
                gate_skip(0, 0, j)

            def body(g, par, next, next2, prev):
                for u in range(UNITS):
                    scan(g, u)
                    if u:
                        add_y(g, par, u - 1)
                    elif prev:
                        add_y(g - 1, 1 - par, UNITS - 1)
                    if next:
                        if u in (0, 2, 4, 6):
                            convolve(g + 1, 1 - par, u // 2)
                        if u in (1, 3, 5, 7):
                            gate_x(g + 1, 1 - par, u // 2)
                        if u in (12, 14):
                            softplus(g + 1, 1 - par, u - 12)
                            softplus(g + 1, 1 - par, u - 11)
                        for j in SKIPS.get(u, ()):
                            gate_skip(g + 1, 1 - par, j)
                    if prev and u in (5, 8):
                        normalise((g - 1) * G + u // 8, u // 8)
                    if prev and u in (6, 9):
                        finish_norm((g - 1) * G + u // 8)
                    if next2 and u == 9:
                        x_moments(g + 2)
                    if next2 and u == 10:
                        scale_x(g + 2)

            over_groups(dve, body)
            add_y(GROUPS - 1, 1, UNITS - 1)
            for s in range(G):
                normalise(SEQS - G + s, s, (xr, xa[1])[s])
                finish_norm(SEQS - G + s, (xr, xa[1])[s])

        @block.gpsimd
        def _(pool):
            def x_power(g):
                for s in range(G):
                    pool.wait_ge(square_ready, g * G + s + 1)
                    pool.tensor_tensor(xrms[:, s, :], xmoments[:, s, 0:1], minus_half, ALU.pow)\
                        .then_inc(xrms_ready, 1)

            def make_inputs(g, par, u):
                j, c = u % JT, u // JT
                if u == 0:
                    pool.wait_ge(delta_ready, g * 4 + 4)
                if u < JT:
                    reused(pool, inputs_ready, g * UNITS - JT + j + 1)
                    pool.tensor_tensor(dx[:, j, :], dl[par][:, j, :], xs[par][:, j, :], ALU.mult)\
                        .then_inc(dx_ready, 1)
                    pool.wait_ge(dx_ready, g * JT + j + 1)
                if u % JT == 0:
                    pool.wait_ge(b_spread[c], (g + 1) * DMA)
                reused(pool, y_summed, g * UNITS + u - 1)
                pool.tensor_tensor(state[u % 2], spread(dx[:, j, :], 1, CH), Bb[c], ALU.mult)\
                    .then_inc(inputs_ready, 1)

            def gate_y(g, par, j):
                pool.wait_ge(y_added, g * UNITS + JT + j + 1)
                pool.tensor_tensor(sk[par][:, j, :], sk[par][:, j, :], yacc[:, j, :], ALU.mult).then_inc(gated, 1)

            def double_resid(b, xr=xr):
                pool.wait_ge(resid_loaded, (b + 1) * DMA)
                pool.tensor_tensor(xr, xr, xr, ALU.add).then_inc(resid_doubled, 1)

            x_power(0)
            x_power(1)
            make_inputs(0, 0, 0)

            def body(g, par, next, next2, prev):
                for u in range(UNITS):
                    if u < UNITS - 1:
                        make_inputs(g, par, u + 1)
                    elif next:
                        make_inputs(g + 1, 1 - par, 0)
                    if prev and u == 0:
                        gate_y(g - 1, 1 - par, JT - 1)
                    if next2 and u == 9:
                        x_power(g + 2)
                    if u >= JT + 2:
                        gate_y(g, par, u - JT - 2)
                    if prev and u in (1, 7):
                        double_resid((g - 1) * G + u // 4)
                    if prev and u in (5, 8):
                        norm_gpsimd(pool, (g - 1) * G + u // 8, norm, moments, rstd, minus_half)
                gate_y(g, par, JT - 2)

            over_groups(pool, body)
            gate_y(GROUPS - 1, 1, JT - 1)
            for s in range(G):
                double_resid(SEQS - G + s, (xr, xa[1])[s])
                norm_gpsimd(pool, SEQS - G + s, norm, moments, rstd, minus_half)


def stage_normed_attention(nc, sem, ps, arena, const, weights, prefetch, src, ctx, dst):
    H, HD, CC = 16, 128, 2
    NB = H // 4
    WIDE = H * HD
    SCALE = HD ** -0.5
    ident, minus_half = const["ident"], const["minus_half"]
    Wq, Wk, Wv, Wo, kv_loaded, q_loaded, given, regions = weights

    r0, r1, r = (Region(arena, *span) for span in regions)
    q, k = r0.take(NB, D), r0.take(NB, D)
    V, qT, kT, prob = r1.take(WIDE), r1.take(H, P), r1.take(H, P), r1.take(H, P)
    probT, yT = r.take(2, D), r.take(H, P)
    squares = r.take(2, D)
    xa, ca, xr, out = r.take(D), r.take(CC * P), r.take(D), r.take(D)
    xT, cT, fT = r.take(KC, P), r.take(CC, P), r.take(KC, P)
    W, fbias, fz, fout = r.take(KC, D), r.take(D), r.take(D), r.take(D)
    gq, gk, ones = r.take(1), r.take(1), r.take(P)
    ssq = r.take(2, H)
    scale_q, scale_k = ssq[:, 0, :], ssq[:, 1, :]
    power = r.take(H)
    top, shift, total, rtotal = r.take(H), r.take(H), r.take(H), r.take(H)
    rms_raw = r.take(2, H)
    stats, moments, rstd = r.take(6), r.take(3), r.take(1)
    fstats, fmoments, frstd = r.take(6), r.take(3), r.take(1)
    wsum, wscale, wden = r.take(1), r.take(1), r.take(1)
    ternary = prob.rearrange("p a b -> p (a b)")

    x_loaded = sem("e_x_loaded")
    given_loaded = sem("e_given_loaded")
    out_loaded = sem("e_out_weight_loaded")
    consts_set = sem("e_consts_set")
    resid_loaded = sem("e_resid_loaded")
    stored = sem("e_stored")
    w_steps = sem("e_w_steps")
    w_summed = sem("e_w_summed")
    w_total = sem("e_w_total")
    w_ready = sem("e_w_ready")
    x_turned = sem("e_x_turned")
    xT_copied = sem("e_xT_copied")
    projected = sem("e_projected")
    proj_copied = sem("e_proj_copied")
    squared = sem("e_squared")
    squares_summed = sem("e_squares_summed")
    rms_steps = sem("e_rms_steps")
    rms_ready = sem("e_rms_ready")
    rms_powered = sem("e_rms_powered")
    scale_ready = sem("e_scale_ready")
    k_normed = sem("e_k_normed")
    q_turned = sem("e_q_turned")
    k_turned = sem("e_k_turned")
    qT_copied = sem("e_qT_copied")
    kT_copied = sem("e_kT_copied")
    scored = sem("e_scored")
    top_found = sem("e_top_found")
    shift_ready = sem("e_shift_ready")
    exp_done = sem("e_exp_done")
    total_inverted = sem("e_total_inverted")
    prob_normed = sem("e_prob_normed")
    prob_turned = sem("e_prob_turned")
    probT_copied = sem("e_probT_copied")
    mixed = sem("e_mixed")
    yT_copied = sem("e_yT_copied")
    out_projected = sem("e_out_projected")
    resid_added = sem("e_resid_added")
    dve_steps = sem("e_dve_steps")
    norm = NormSems(sem, "e")
    f_turned = sem("f_turned")
    fT_copied = sem("f_T_copied")
    f_biased = sem("f_biased")
    f_projected = sem("f_projected")
    f_added = sem("f_added")
    f_steps = sem("f_steps")
    fnorm = NormSems(sem, "f")
    LAST = SEQS - 1
    X_BANK, C_BANK, O_BANK, FT_BANK, F_BANK = 7, 6, 7, 7, 6
    Q_BANK, K_BANK = (0, 2), (1, 3)

    with nc.Block() as block:
        @block.sync
        def _(sp):
            def load_x(b):
                sp.dma_start(xa, row(src, b)).then_inc(x_loaded, DMA)
                sp.dma_start(ca, row(ctx, b)).then_inc(x_loaded, DMA)

            load_x(0)
            for tile, dram in ((W, given["weight"].rearrange("(k p) n -> p k n", p=P)),
                               (fbias, given["bias"].partition_broadcast(P)), (gq, given["gq"]), (gk, given["gk"])):
                sp.dma_start(tile, dram).then_inc(given_loaded, DMA)
            sp.dma_start(Wo, given["Wo"].rearrange("(k p) n -> p k n", p=P)).then_inc(out_loaded, DMA)
            sp.wait_ge(x_turned, 2)
            load_x(1)

            def body(b, ahead, behind=True):
                reused(sp, norm.out, b)
                sp.dma_start(xr, row(src, b)).then_inc(resid_loaded, DMA)
                if behind:
                    sp.wait_ge(fnorm.out, b)
                    sp.dma_start(row(dst, b - 1), fout).then_inc(stored, DMA)
                if ahead:
                    sp.wait_ge(x_turned, 2 * b + 4)
                    load_x(b + 2)

            body(0, True, False)
            with sp.Fori(1, SEQS - 2) as b:
                body(b, True)
            body(SEQS - 2, False)
            body(LAST, False)
            sp.wait_ge(fnorm.out, SEQS)
            sp.dma_start(row(dst, LAST), fout).then_inc(stored, DMA)
            sp.wait_ge(stored, SEQS * DMA)

        @block.tensor
        def _(pe):
            def turn_x(b, first=False):
                pe.wait_ge(x_loaded, 2 * (b + 1) * DMA)
                if not first:
                    reused(pe, fT_copied, b - 1)
                turn(pe, ps[:, X_BANK, :], halves(xa), ident).then_inc(x_turned, 1)

            def turn_ctx(b, first=False):
                if not first:
                    reused(pe, f_added, b - 1)
                turn(pe, ps[:, C_BANK, :], halves(ca, CC), ident).then_inc(x_turned, 1)

            def proj(b, c):
                pe.wait_ge(xT_copied, 2 * b + (1 if c < NB else 2))
                reused(pe, proj_copied, 12 * b + c - 1)
                lhs, w, n = ((xT, Wq, KC), (cT, Wk, CC), (cT, Wv, CC))[c // NB]
                cols = slice(c % NB * D, (c % NB + 1) * D)
                project(pe, ps[:, 4 + c % 2, :], lambda i: lhs[:, i, :], lambda i: w[:, i, cols], n)\
                    .then_inc(projected, 1)

            def turn_qk(b):
                for c in range(NB):
                    if c == 0:
                        reused(pe, probT_copied, b * NB)
                        pe.wait_ge(proj_copied, 12 * b + NB)
                    elif c == 1:
                        reused(pe, yT_copied, b * NB)
                    else:
                        pe.wait_ge(qT_copied, b * NB + c - 1)
                    turn(pe, ps[:, Q_BANK[c % 2], :], halves(q[:, c, :]), ident).then_inc(q_turned, 1)
                    pe.wait_ge(k_normed, b * NB + c + 1)
                    if c >= 2:
                        pe.wait_ge(kT_copied, b * NB + c - 1)
                    turn(pe, ps[:, K_BANK[c % 2], :], halves(k[:, c, :]), ident).then_inc(k_turned, 1)

            def scores(b):
                pe.wait_ge(qT_copied, b * NB + NB)
                pe.wait_ge(kT_copied, b * NB + NB)
                for c in range(NB):
                    for h in range(4 * c, 4 * c + 4):
                        last = pe.matmul(ps[:, c, (h % 4) * P:(h % 4 + 1) * P], qT[:, h, :], kT[:, h, :],
                                         start=True, stop=True)
                    last.then_inc(scored, 1)

            def turn_prob(b, c):
                pe.wait_ge(prob_normed, b * NB + c + 1)
                if c >= 2:
                    pe.wait_ge(probT_copied, b * NB + c - 1)
                turn(pe, ps[:, c % 2, :], [prob[:, h, :] for h in range(4 * c, 4 * c + 4)], ident)\
                    .then_inc(prob_turned, 1)

            def mix(b, c):
                pe.wait_ge(probT_copied, b * NB + c + 1)
                if c < 2:
                    pe.wait_ge(proj_copied, 12 * b + 12)
                    pe.wait_ge(exp_done, b * NB + 3 + c)
                else:
                    pe.wait_ge(yT_copied, b * NB + c - 1)
                for h in range(4 * c, 4 * c + 4):
                    last = pe.matmul(ps[:, 2 + c % 2, (h % 4) * P:(h % 4 + 1) * P], V[:, h * P:(h + 1) * P],
                                     probT[:, c % 2, (h % 4) * P:(h % 4 + 1) * P], start=True, stop=True)
                last.then_inc(mixed, 1)

            def attend(b, last=False):
                turn_prob(b, 0)
                for c in range(NB):
                    if c + 1 < NB:
                        turn_prob(b, c + 1)
                    if not last and c % 2 == 0:
                        proj(b + 1, 2 * NB + c // 2)
                    mix(b, c)

            def out_proj(b, last=False):
                pe.wait_ge(yT_copied, b * NB + NB)
                pe.wait_ge(xT_copied, 2 * b + (1 if last else 3))
                reused(pe, fT_copied, b)
                project(pe, ps[:, O_BANK, :], lambda i: yT[:, i, :], lambda i: Wo[:, i, :], H)\
                    .then_inc(out_projected, 1)

            def turn_f(b):
                pe.wait_ge(norm.out, b + 1)
                turn(pe, ps[:, FT_BANK, :], halves(out), ident).then_inc(f_turned, 1)

            def proj_f(b, last=False):
                pe.wait_ge(fT_copied, b + 1)
                pe.wait_ge(xT_copied, 2 * b + (2 if last else 4))
                project(pe, ps[:, F_BANK, :], lambda i: fT[:, i, :], lambda i: W[:, i, :], KC)\
                    .then_inc(f_projected, 1)

            turn_x(0, first=True)
            turn_ctx(0, first=True)
            pe.wait_ge(kv_loaded, 2 * DMA)
            pe.wait_ge(q_loaded, DMA)
            for c in range(12):
                proj(0, c)
                if c == 1:
                    pe.wait_ge(consts_set, 1)
                    pe.wait_ge(w_summed, 1)
                    pe.matmul(ps[:, 0, 0:1], ones, wsum, start=True, stop=True).then_inc(w_total, 1)
            pe.wait_ge(w_ready, 1)
            pe.wait_ge(out_loaded, DMA)

            def body(b, first=False):
                turn_qk(b)
                if not first:
                    turn_f(b - 1)
                scores(b)
                turn_x(b + 1)
                if not first:
                    proj_f(b - 1)
                for c in range(2 * NB):
                    proj(b + 1, c)
                    if c == 1:
                        turn_ctx(b + 1)
                attend(b)
                for c in range(2 * NB + 2, 3 * NB):
                    proj(b + 1, c)
                out_proj(b)

            body(0, True)
            with pe.Fori(1, LAST) as b:
                body(b)
            turn_qk(LAST)
            turn_f(LAST - 1)
            scores(LAST)
            proj_f(LAST - 1)
            attend(LAST, last=True)
            out_proj(LAST, last=True)
            turn_f(LAST)
            proj_f(LAST, last=True)

        @block.scalar
        def _(act):
            def copy_xT(b):
                act.wait_ge(x_turned, 2 * b + 1)
                reused(act, projected, 12 * b)
                act.activation(xT, ps[:, X_BANK, :].rearrange("p (a b) -> p a b", a=KC), ACT.Copy)\
                    .then_inc(xT_copied, 1)

            def copy_cT(b):
                act.wait_ge(x_turned, 2 * b + 2)
                act.activation(cT, ps[:, C_BANK, 0:CC * P].rearrange("p (a b) -> p a b", a=CC), ACT.Copy)\
                    .then_inc(xT_copied, 1)

            def copy_proj(b, c):
                act.wait_ge(projected, 12 * b + c + 1)
                if c < NB:
                    reused(act, q_turned, b * NB)
                    reused(act, squared, 8 * b)
                    dest = q[:, c, :]
                elif c < 2 * NB:
                    reused(act, k_turned, b * NB)
                    dest = k[:, c - NB, :]
                else:
                    reused(act, mixed, b * NB)
                    dest = V[:, (c - 2 * NB) * D:(c - 2 * NB + 1) * D]
                act.activation(dest, ps[:, 4 + c % 2, :], ACT.Copy).then_inc(proj_copied, 1)

            def copy_qT(b, c):
                act.wait_ge(q_turned, b * NB + c + 1)
                reused(act, scored, b * NB)
                act.activation(qT[:, 4 * c:4 * c + 4, :], ps[:, Q_BANK[c % 2], :].rearrange("p (a b) -> p a b", a=4), ACT.Copy,
                               scale=gq).then_inc(qT_copied, 1)

            def exps(b, c):
                act.wait_ge(shift_ready, b * NB + c + 1)
                reused(act, prob_turned, (b - 1) * NB + c + 1)
                reused(act, total_inverted, (b - 1) * NB + c + 1)
                for h in range(4 * c, 4 * c + 4):
                    last = act.activation(prob[:, h, :], ps[:, c, (h % 4) * P:(h % 4 + 1) * P], ACT.Exp,
                                          bias=shift[:, h:h + 1], scale=scale_q[:, h:h + 1],
                                          accum_out=total[:, h:h + 1])
                last.then_inc(exp_done, 1)

            def copy_fT(b):
                act.wait_ge(f_turned, b + 1)
                reused(act, f_projected, b)
                act.activation(fT, ps[:, FT_BANK, :].rearrange("p (a b) -> p a b", a=KC), ACT.Copy)\
                    .then_inc(fT_copied, 1)

            copy_xT(0)
            copy_cT(0)
            act.wait_ge(given_loaded, 4 * DMA)
            act.activation(ternary, W.rearrange("p a b -> p (a b)"), ACT.Abs, accum_out=wsum).then_inc(w_summed, 1)
            for c in range(12):
                copy_proj(0, c)

            def body(b, first=False):
                for c in range(NB):
                    copy_qT(b, c)
                if not first:
                    copy_fT(b - 1)
                copy_xT(b + 1)
                for c in range(NB):
                    exps(b, c)
                    copy_proj(b + 1, c)
                    if c == 1:
                        copy_cT(b + 1)
                for c in range(NB, 3 * NB):
                    copy_proj(b + 1, c)

            body(0, True)
            with act.Fori(1, LAST) as b:
                body(b)
            for c in range(NB):
                copy_qT(LAST, c)
            copy_fT(LAST - 1)
            for c in range(NB):
                exps(LAST, c)
            copy_fT(LAST)

        @block.vector
        def _(dve):
            def make_ternary():
                MAGIC = 12582912.0
                w = W.rearrange("p a b -> p (a b)")
                st = Steps(dve, w_steps, 0)
                dve.wait_ge(w_total, 1)
                st(dve.tensor_scalar(wscale, ps[:, 0, 0:1], 1.0 / (D * D), None, ALU.mult))
                st.wait()
                st(dve.tensor_scalar(wden, wscale, 1e-10, None, ALU.add))
                st.wait()
                st(dve.reciprocal(wden, wden))
                st.wait()
                st(dve.tensor_scalar(ternary, w, wden, 1.0, ALU.mult, ALU.min))
                st.wait()
                st(dve.tensor_scalar(ternary, ternary, -1.0, MAGIC, ALU.max, ALU.add))
                st.wait()
                st(dve.tensor_scalar(ternary, ternary, -MAGIC, None, ALU.add))
                st.wait()
                st(dve.scalar_tensor_tensor(ternary, ternary, wscale, w, ALU.mult, ALU.subtract))
                st.wait()
                dve.tensor_tensor(w, w, ternary, ALU.add).then_inc(w_ready, 1)

            def copy_kT(b, c):
                dve.wait_ge(k_turned, b * NB + c + 1)
                if c == 0:
                    reused(dve, scored, b * NB)
                dve.tensor_scalar(kT[:, 4 * c:4 * c + 4, :], ps[:, K_BANK[c % 2], :].rearrange("p (a b) -> p a b", a=4),
                                  gk, None, ALU.mult).then_inc(kT_copied, 1)

            def find_shift(b, c):
                heads = slice(4 * c, 4 * c + 4)
                dve.wait_ge(scored, b * NB + c + 1)
                if c == 0:
                    dve.wait_ge(scale_ready, b * 2 + 2)
                dve.tensor_reduce(top[:, heads], ps[:, c, :].rearrange("p (h k) -> p h k", h=4), AX.X, ALU.max)\
                    .then_inc(top_found, 1)
                dve.wait_ge(top_found, b * NB + c + 1)
                reused(dve, exp_done, (b - 1) * NB + c + 1)
                dve.scalar_tensor_tensor(shift[:, heads], top[:, heads], -1.0, scale_q[:, heads], ALU.mult, ALU.mult)\
                    .then_inc(shift_ready, 1)

            def invert_total(b, c):
                heads = slice(4 * c, 4 * c + 4)
                dve.wait_ge(exp_done, b * NB + c + 1)
                reused(dve, prob_normed, (b - 1) * NB + c + 1)
                dve.reciprocal(rtotal[:, heads], total[:, heads]).then_inc(total_inverted, 1)

            def sum_squares(b, which, c):
                n = NB * which + c
                dve.wait_ge(squared, 8 * b + n + 1)
                if c == 0:
                    reused(dve, rms_powered, 2 * b)
                dve.tensor_reduce(rms_raw[:, which, 4 * c:4 * c + 4],
                                  squares[:, n % 2, :].rearrange("p (h d) -> p h d", h=4), AX.X, ALU.add)\
                    .then_inc(squares_summed, 1)

            def mean_square(b, which):
                dve.wait_ge(squares_summed, 8 * b + NB * (which + 1))
                dve.tensor_scalar(rms_raw[:, which, :], rms_raw[:, which, :], 1.0 / HD, EPS, ALU.mult, ALU.add)\
                    .then_inc(rms_ready, 1)

            def take_scale(b, which):
                dve.wait_ge(rms_powered, 2 * b + which + 1)
                if which == 0:
                    reused(dve, exp_done, b * NB)
                else:
                    reused(dve, k_normed, b * NB)
                dve.tensor_scalar(ssq[:, which, :], rms_raw[:, which, :], (SCALE, 1.0)[which], None, ALU.mult)\
                    .then_inc(scale_ready, 1)

            def copy_probT(b, c):
                dve.wait_ge(prob_turned, b * NB + c + 1)
                reused(dve, mixed, b * NB + c - 1)
                dve.tensor_copy(probT[:, c % 2, :], ps[:, c % 2, :]).then_inc(probT_copied, 1)

            def copy_yT(b, c):
                dve.wait_ge(mixed, b * NB + c + 1)
                if c == 0:
                    reused(dve, out_projected, b)
                dve.tensor_copy(yT[:, 4 * c:4 * c + 4, :], ps[:, 2 + c % 2, :].rearrange("p (a b) -> p a b", a=4))\
                    .then_inc(yT_copied, 1)

            def normalise(b):
                st = Steps(dve, dve_steps, b * 2)
                dve.wait_ge(out_projected, b + 1)
                dve.wait_ge(resid_loaded, (b + 1) * DMA)
                dve.tensor_tensor(xr, ps[:, O_BANK, :], xr, ALU.add).then_inc(resid_added, 1)
                dve.wait_ge(resid_added, b + 1)
                norm_moments(dve, norm, st, xr, stats, moments)

            def finish_norm(b):
                reused(dve, f_turned, b)
                reused(dve, f_biased, b)
                norm_apply(dve, b, norm, xr, moments, rstd, out, None)

            def normalise_f(b):
                st = Steps(dve, f_steps, b * 2)
                dve.wait_ge(f_projected, b + 1)
                dve.wait_ge(f_biased, b + 1)
                dve.tensor_tensor(fz, ps[:, F_BANK, :], fz, ALU.add).then_inc(f_added, 1)
                dve.wait_ge(f_added, b + 1)
                norm_vector(dve, b, fnorm, st, fz, fstats, fmoments, frstd, fout, stored)

            dve.memset(ones, 1.0).then_inc(consts_set, 1)
            make_ternary()
            for which in range(2):
                for c in range(NB):
                    sum_squares(0, which, c)
                mean_square(0, which)
                take_scale(0, which)

            def body(b, first=False):
                for c in range(NB):
                    copy_kT(b, c)
                    if c == 1 and not first:
                        finish_norm(b - 1)
                for c in range(NB):
                    find_shift(b, c)
                if not first:
                    normalise_f(b - 1)
                for c in range(NB):
                    invert_total(b, c)
                    sum_squares(b + 1, 0, c)
                mean_square(b + 1, 0)
                take_scale(b + 1, 0)
                copy_probT(b, 0)
                for c in range(NB):
                    if c + 1 < NB:
                        copy_probT(b, c + 1)
                    copy_yT(b, c)
                    sum_squares(b + 1, 1, c)
                mean_square(b + 1, 1)
                take_scale(b + 1, 1)
                normalise(b)

            body(0, True)
            body(1)
            with dve.Fori(2, LAST) as b:
                body(b)
            for c in range(NB):
                copy_kT(LAST, c)
                if c == 1:
                    finish_norm(LAST - 1)
            for c in range(NB):
                find_shift(LAST, c)
            normalise_f(LAST - 1)
            for c in range(NB):
                invert_total(LAST, c)
            copy_probT(LAST, 0)
            for c in range(NB):
                if c + 1 < NB:
                    copy_probT(LAST, c + 1)
                copy_yT(LAST, c)
            normalise(LAST)
            finish_norm(LAST)
            normalise_f(LAST)

        @block.gpsimd
        def _(pool):
            def square(b, which, c):
                n = NB * which + c
                tile = (q, k)[which][:, c, :]
                pool.wait_ge(proj_copied, 12 * b + n + 1)
                reused(pool, squares_summed, 8 * b + n - 1)
                pool.tensor_tensor(squares[:, n % 2, :], tile, tile, ALU.mult).then_inc(squared, 1)

            def root(b, which):
                pool.wait_ge(rms_ready, 2 * b + which + 1)
                pool.tensor_tensor(rms_raw[:, which, :], rms_raw[:, which, :],
                                   minus_half.broadcast_to([P, H]), ALU.pow).then_inc(rms_powered, 1)

            def norm_k(b, c):
                pool.wait_ge(scale_ready, 2 * b + 2)
                tile = k[:, c, :].rearrange("p (h d) -> p h d", h=4)
                pool.tensor_tensor(tile, tile, spread(scale_k[:, 4 * c:4 * c + 4], 2, HD), ALU.mult)\
                    .then_inc(k_normed, 1)

            def norm_prob(b, c):
                pool.wait_ge(total_inverted, b * NB + c + 1)
                tile = prob[:, 4 * c:4 * c + 4, :]
                pool.tensor_tensor(tile, tile, spread(rtotal[:, 4 * c:4 * c + 4], 2, P), ALU.mult)\
                    .then_inc(prob_normed, 1)

            def bias_f(b):
                pool.wait_ge(norm.out, b + 1)
                reused(pool, fnorm.out, b)
                pool.tensor_tensor(fz, out, fbias, ALU.add).then_inc(f_biased, 1)

            def make_keys(b):
                for c in range(NB):
                    square(b, 0, c)
                root(b, 0)
                for c in range(NB):
                    square(b, 1, c)
                root(b, 1)
                for c in range(NB):
                    norm_k(b, c)

            pool.wait_ge(given_loaded, 4 * DMA)
            make_keys(0)

            def body(b, first=False):
                if not first:
                    bias_f(b - 1)
                    norm_gpsimd(pool, b - 1, fnorm, fmoments, frstd, minus_half)
                for c in range(NB):
                    norm_prob(b, c)
                    square(b + 1, 0, c)
                root(b + 1, 0)
                for c in range(NB):
                    square(b + 1, 1, c)
                root(b + 1, 1)
                for c in range(NB):
                    norm_k(b + 1, c)
                norm_gpsimd(pool, b, norm, moments, rstd, minus_half)

            body(0, True)
            body(1)
            with pool.Fori(2, LAST) as b:
                body(b)
            bias_f(LAST - 1)
            norm_gpsimd(pool, LAST - 1, fnorm, fmoments, frstd, minus_half)
            for c in range(NB):
                norm_prob(LAST, c)
            norm_gpsimd(pool, LAST, norm, moments, rstd, minus_half)
            bias_f(LAST)
            norm_gpsimd(pool, LAST, fnorm, fmoments, frstd, minus_half)


def program(nc, x, ctx, pos, t, outs):
    with ExitStack() as stack:
        def sem(name):
            return stack.enter_context(nc.semaphore(name))

        arena = stack.enter_context(nc.sbuf_tensor("arena", [P, ARENA], F32))
        ps = stack.enter_context(nc.psum_tensor("banks", [P, 8, 512], F32))
        x_after = [nc.dram_tensor(f"x_after_{n}", (SEQS, TOK, D), F32).ap() for n in range(4)]

        KB = 256
        WORK = 144 * KB
        c = Region(arena, WORK)
        const = {"ident": c.take(P), "minus_half": c.take(1)}
        const["work_c"] = c.at
        const.update(freq=c.take(4), bout=c.take(D))
        const["work_b"] = c.at
        const.update(rope_cos=c.take(64), rope_sgnsin=c.take(64), causal=c.take(P))
        const["work"] = c.at
        const["loaded"] = sem("consts_loaded")
        const["loads"] = 5
        const["halved"] = sem("minus_half_set")
        a_q, b_weights = sem("a_q_loaded"), sem("b_weights_loaded")
        w = Region(arena, 0)
        Wqkv, Wo = w.take(KC, 4 * D), w.take(8, D)
        We = [arena[:, k * 16 * KB:(k + 1) * 16 * KB] for k in range(KC)]
        Wr = Region(arena, 80 * KB).take(KC, 8 * D)
        router_loaded, experts_loaded = sem("router_loaded"), sem("experts_loaded")
        d_weights = sem("d_weights_loaded")
        w = Region(arena, 80 * KB, WORK)
        W_skip, W_in, Wd1, Wd2 = w.take(KC, 2 * D), w.take(KC, 2 * D), w.take(8, P), w.take(8 * P)
        Wbc, W_out = w.take(8, 32), w.take(8, D)
        d_params = {name: t[name] for name in ("conv_w", "conv_b", "b_delta", "A_log", "W_D", "norm_w")}
        d_regions = ((0, 80 * KB), (w.at, WORK), (const["work_c"], ARENA))
        e_kv, e_q = sem("e_kv_loaded"), sem("e_q_loaded")
        eWo, eWq = Region(arena, 0).take(16, D), Region(arena, 48 * KB).take(KC, 4 * D)
        w = Region(arena, 80 * KB)
        eWk, eWv = w.take(2, 4 * D), w.take(2, 4 * D)
        e_given = {"Wo": t["L1_xattn_Wo"], "weight": t["L1_ffn_weight"], "bias": t["L1_ffn_bias"], "gq": t["gq"], "gk": t["gk"]}
        e_regions = ((32 * KB, 48 * KB), (w.at, WORK), (const["work_c"], ARENA))
        bc_dram = nc.dram_tensor("b_and_c", (8, 32, 256), F32).ap()
        w = Region(arena, 48 * KB, 72 * KB)
        xWq, xWkv, xWout = w.take(KC, D), w.take(2, 2 * D), w.take(KC, D)

        with nc.Block() as block:
            @block.sync
            def _(sp):
                for name in ("ident", "rope_cos", "rope_sgnsin", "causal"):
                    sp.dma_start(const[name], t[name]).then_inc(const["loaded"], DMA)
                sp.dma_start(const["freq"], t["freq"].partition_broadcast(P)).then_inc(const["loaded"], DMA)
                sp.dma_start(Wqkv[:, :, 0:2 * D], t["L0_attn_Wq"].rearrange("(k p) n -> p k n", p=P))\
                    .then_inc(a_q, DMA)

            @block.gpsimd
            def _(pool):
                pool.memset(const["minus_half"], -0.5).then_inc(const["halved"], 1)
                pool.wait_ge(const["halved"], 1)

        def load_b(sp):
            for dst, name in ((xWq, "L0_xattn_Wq"), (xWkv, "L0_xattn_Wkv"), (xWout, "L0_xattn_Wout")):
                sp.dma_start(dst, t[name].rearrange("(k p) n -> p k n", p=P)).then_inc(b_weights, DMA)
            sp.dma_start(const["bout"], t["L0_xattn_bout"].partition_broadcast(P)).then_inc(b_weights, DMA)

        def load_router(k):
            def load(sp):
                sp.dma_start(Wr[:, k, :], t["L0_ffn_router_w"][k * P:(k + 1) * P, :]).then_inc(router_loaded, DMA)
            return load

        def load_experts(chunks):
            def load(sp):
                for k in chunks:
                    sp.dma_start(We[k], t["L0_ffn_expert_w"][k * P:(k + 1) * P, :]).then_inc(experts_loaded, DMA)
            return load

        def load_d(sp):
            for dst, name in ((W_in, "L1_attn_W_in"), (W_skip, "L1_attn_W_skip"), (Wd1, "L1_attn_W_delta_1"),
                              (Wbc[:, :, 0:16], "L1_attn_W_B"), (Wbc[:, :, 16:32], "L1_attn_W_C"),
                              (W_out, "L1_attn_W_out")):
                sp.dma_start(dst, t[name].rearrange("(k p) n -> p k n", p=P)).then_inc(d_weights, DMA)
            sp.dma_start(Wd2, t["L1_attn_W_delta_2"]).then_inc(d_weights, DMA)

        def load_e_kv(sp):
            for dst, name in ((eWk, "L1_xattn_Wk"), (eWv, "L1_xattn_Wv")):
                sp.dma_start(dst, t[name].rearrange("(k p) n -> p k n", p=P)).then_inc(e_kv, DMA)

        def load_e_q(sp):
            sp.dma_start(eWq, t["L1_xattn_Wq"].rearrange("(k p) n -> p k n", p=P)).then_inc(e_q, DMA)

        def stage(build, weights, prefetch, *places, **more):
            own = []

            def own_sem(name):
                own.append(nc.alloc_semaphore(name))
                return own[-1]

            build(nc, own_sem, ps, arena, const, weights, prefetch, *places, **more)
            nc.clear_and_free_semaphores(own)
            nc.all_engine_barrier()

        stage(stage_self_attention, (Wqkv, Wo, a_q, [t[f"L0_attn_W{n}"] for n in "kvo"]),
              [load_b, *(load_router(k) for k in range(KC))], x, x_after[0])
        stage(stage_cross_attention, (xWq, xWkv, xWout, const["bout"], b_weights), load_experts(range(KC - 1)),
              x_after[0], ctx, pos, x_after[1], extra=(72 * KB, 80 * KB))
        stage(stage_experts, (Wr, lambda k: We[k], (t["L0_ffn_router_b"], t["L0_ffn_expert_b"]), router_loaded,
                              experts_loaded), (load_experts([KC - 1]), load_d), x_after[1], x_after[2],
              extra=(64 * KB, 80 * KB))
        stage(stage_selective_scan, (W_skip, W_in, Wd1, Wd2, Wbc, W_out, d_params, d_weights, d_regions),
              (load_e_kv, load_e_q), x_after[2], x_after[3], bc_dram)
        stage(stage_normed_attention, (eWq, eWk, eWv, eWo, e_kv, e_q, e_given, e_regions), None,
              x_after[3], ctx, outs)


_WEIGHTS = ["L0_attn_Wq", "L0_attn_Wk", "L0_attn_Wv", "L0_attn_Wo",
            "L0_xattn_Wq", "L0_xattn_Wkv", "L0_xattn_Wout", "L0_xattn_bout",
            "L0_ffn_router_w", "L0_ffn_router_b", "L0_ffn_expert_w", "L0_ffn_expert_b",
            "L1_attn_W_skip", "L1_attn_W_in", "L1_attn_W_delta_1", "L1_attn_W_delta_2", "L1_attn_W_B", "L1_attn_W_C",
            "L1_attn_W_out", "L1_xattn_Wq", "L1_xattn_Wk", "L1_xattn_Wv", "L1_xattn_Wo", "L1_ffn_bias"]


def tables():
    import numpy as np
    inv = 1.0 / np.float32(10000.0) ** (np.arange(0, 64, 2, dtype=np.float32) / np.float32(64))
    f = np.arange(TOK, dtype=np.float32)[:, None] * inv[None, :].astype(np.float32)
    cos, sin = np.cos(f), np.sin(f)
    k, q = np.arange(TOK)[:, None], np.arange(TOK)[None, :]
    return {
        "freq": (np.float32(10000.0) ** (-np.arange(4, dtype=np.float32) / np.float32(4))).astype(np.float32),
        "ident": np.eye(P, dtype=np.float32),
        "rope_cos": np.concatenate([cos, cos], -1).astype(np.float32),
        "rope_sgnsin": np.concatenate([-sin, sin], -1).astype(np.float32),
        "causal": (k <= q).astype(np.float32),
    }


def kernel(**inputs):
    import numpy as _np
    import concourse.bacc as _bacc
    from concourse.bass_utils import run_bass_kernel_spmd as _run

    nc = _bacc.Bacc("TRN2", target_bir_lowering=False, num_devices=1)
    given = {"x": inputs["x"], "ctx": inputs["ctx_1024"], "pos": inputs["fside_BxSx2_0"]}
    given.update({name: inputs[name] for name in _WEIGHTS})
    wq = _np.asarray(given["L0_attn_Wq"])
    given["L0_attn_Wq"] = wq.reshape(D, 4, 2, 2, 64).transpose(0, 1, 3, 2, 4).reshape(D, 1024)
    given["L0_ffn_router_w"] = _np.asarray(given["L0_ffn_router_w"]).reshape(D, 8, D).transpose(2, 1, 0)\
        .reshape(D, 8 * D)
    given["L0_ffn_router_b"] = _np.asarray(given["L0_ffn_router_b"]).reshape(D, 8).T.reshape(8 * D)
    given["L0_ffn_expert_w"] = _np.asarray(given["L0_ffn_expert_w"]).transpose(2, 0, 1).reshape(D, 8 * D)
    def by_tile(name, *rest):
        return _np.asarray(inputs[name]).reshape(8, P, *rest).swapaxes(0, 1)
    given["conv_w"] = _np.asarray(inputs["L1_attn_conv_w"]).reshape(4, 8, P).transpose(2, 1, 0)
    given["conv_b"], given["b_delta"] = by_tile("L1_attn_conv_b"), by_tile("L1_attn_b_delta_2")
    given["A_log"], given["W_D"] = by_tile("L1_attn_A_log", 16), by_tile("L1_attn_W_D")
    given["norm_w"] = _np.asarray(inputs["L1_attn_norm_w"]).reshape(KC, P).T
    given["gq"], given["gk"] = (_np.asarray(inputs[f"L1_xattn_{n}"]).reshape(P, 1) for n in ("gq", "gk"))
    given["L1_ffn_weight"] = _np.asarray(inputs["L1_ffn_weight"]).T
    given.update(tables())
    arrays, args = {}, {}
    for name, a in given.items():
        a = _np.ascontiguousarray(a)
        arrays[f"in_{name}"] = a
        args[name] = nc.dram_tensor(f"in_{name}", a.shape, F32, kind="ExternalInput").ap()
    out = nc.dram_tensor("out_0", (SEQS, TOK, D), F32, kind="ExternalOutput").ap()
    program(nc, args["x"], args["ctx"], args["pos"], args, out)
    r = _run(nc, [arrays], core_ids=[0])
    return r.results[0]["out_0"]
```
